# Optimizing a Trainium2 kernel written in Bass

```python
import numpy as np
import jax
import jax.numpy as jnp

def _softmax(x, axis=-1):
    return jax.nn.softmax(x, axis=axis)

def _gelu(x):
    return jax.nn.gelu(x, approximate=True)

def _silu(x):
    return jax.nn.silu(x)

def _sigmoid(x):
    return jax.nn.sigmoid(x)

def _layernorm(x, axis=-1, eps=1e-05):
    m = jnp.mean(x, axis=axis, keepdims=True)
    v = jnp.var(x, axis=axis, keepdims=True)
    return (x - m) / jnp.sqrt(v + eps)

def _scatter_add(tgt, idx, src, axis=0):
    return tgt.at[idx].add(src)

def _segment_sum(src, seg, n):
    return jax.ops.segment_sum(src, seg, n)
kernel_name = 'mk_decoder_preln_d1_seqx_r4_3db0e2'

def setup_inputs(seed: int=0):
    np.random.seed(seed)
    _w = jnp.asarray

    def _rec_inputs():
        import jax
        import jax.numpy as jnp
        _rk = jax.random.key(seed)
        x = -0.0003929 + 0.9999 * jax.random.normal(jax.random.fold_in(_rk, 1), (8, 512, 512), jnp.float32)
        _lenS = 512 - jax.random.randint(jax.random.fold_in(_rk, 7), (8,), 0, max(1, 512 // 4) + 1, jnp.int32)
        _lenS2 = 64 - jax.random.randint(jax.random.fold_in(_rk, 8), (8,), 0, max(1, 64 // 4) + 1, jnp.int32)
        _ctx_2048P = jax.random.normal(jax.random.fold_in(_rk, 11), (8, 16, 512), jnp.float32)
        _ctx_2048c = jax.random.dirichlet(jax.random.fold_in(_rk, 511), 0.3 * jnp.ones((16,), jnp.float32), (8, 64))
        _ctx_2048t = jnp.einsum('bsk,bkd->bsd', _ctx_2048c, _ctx_2048P)
        _ctx_2048t = _ctx_2048t * jax.lax.rsqrt(jnp.mean(jnp.square(_ctx_2048t)) + 1e-12) * 0.953939
        ctx_2048 = -1.39393e-06 + 0.999914 * (_ctx_2048t + 0.3 * jax.random.normal(jax.random.fold_in(_rk, 611), (8, 64, 512), jnp.float32))
        itok_BxS_0_1023 = jax.random.randint(jax.random.fold_in(_rk, 12), (8, 512), 0, 256, jnp.int32)
        return (x, ctx_2048, itok_BxS_0_1023)
    x, ctx_2048, itok_BxS_0_1023 = _rec_inputs()

    def _L0_attn_setup():
        import jax, jax.numpy as jnp
        import numpy as np
        import math
        DIM = 512
        N_HEADS = 16
        N_KV_HEADS = 8
        HEAD_DIM = DIM // N_HEADS
        N_REP = N_HEADS // N_KV_HEADS
        BLOCK = 128
        TOPK = 8
        NEG_INF = -10000.0
        SEQ = 1024
        BS = 1

        def _rope_tables(seq_len, head_dim, base=10000.0):
            inv_freq = 1.0 / base ** (jnp.arange(0, head_dim, 2, dtype=jnp.float32) / head_dim)
            ang = jnp.arange(seq_len, dtype=jnp.float32)[:, None] * inv_freq[None, :]
            return (jnp.cos(ang), jnp.sin(ang))

        def _apply_rope(t, cos, sin):
            t1 = t[..., 0::2]
            t2 = t[..., 1::2]
            c = cos[None, :, None, :]
            s = sin[None, :, None, :]
            out_even = t1 * c - t2 * s
            out_odd = t1 * s + t2 * c
            out = jnp.stack([out_even, out_odd], axis=-1)
            return out.reshape(t.shape)
        key = jax.random.key(seed)
        ks = jax.random.split(key, 5)
        scale = 1.0 / math.sqrt(DIM)
        x = jax.random.normal(ks[0], (BS, SEQ, DIM), dtype=jnp.float32)
        wq = jax.random.normal(ks[1], (DIM, N_HEADS * HEAD_DIM), dtype=jnp.float32) * scale
        wk = jax.random.normal(ks[2], (DIM, N_KV_HEADS * HEAD_DIM), dtype=jnp.float32) * scale
        wv = jax.random.normal(ks[3], (DIM, N_KV_HEADS * HEAD_DIM), dtype=jnp.float32) * scale
        wo = jax.random.normal(ks[4], (DIM, DIM), dtype=jnp.float32) * scale
        return {'x': x, 'wq': wq, 'wk': wk, 'wv': wv, 'wo': wo}
    _L0_attn_all = _L0_attn_setup()
    _L0_attn_in = {k: v for k, v in _L0_attn_all.items() if k in ('wq', 'wk', 'wv', 'wo')}
    del _L0_attn_all

    def _L0_xattn_setup():
        import jax, jax.numpy as jnp
        import numpy as np
        B, Lq, Lk = (2, 1024, 256)
        Q_DIM, KV_DIM = (512, 512)
        H, HD = (16, 128)
        KVC, QC, R = (128, 192, 64)
        LOOKBACK = 8
        NEG = -1e+30

        def _rope(x, L):
            half = x.shape[-1] // 2
            inv_freq = 1.0 / 10000.0 ** (jnp.arange(half, dtype=jnp.float32) / half)
            ang = jnp.arange(L, dtype=jnp.float32)[:, None] * inv_freq
            cos, sin = (jnp.cos(ang), jnp.sin(ang))
            x1, x2 = (x[..., :half], x[..., half:])
            return jnp.concatenate([x1 * cos - x2 * sin, x1 * sin + x2 * cos], axis=-1)
        key = jax.random.key(seed)
        ks = jax.random.split(key, 11)

        def w(k, shape, fan_in):
            return jax.random.normal(k, shape, jnp.float32) / np.sqrt(fan_in).astype(np.float32)
        return {'q': jax.random.normal(ks[0], (B, Lq, Q_DIM), jnp.float32), 'kv': jax.random.normal(ks[1], (B, Lk, KV_DIM), jnp.float32), 'seg_id': jnp.sort(jax.random.randint(ks[2], (B, Lq), 0, Lk), axis=-1), 'W_kvc': w(ks[3], (KV_DIM, KVC), KV_DIM), 'W_dq': w(ks[4], (Q_DIM, QC), Q_DIM), 'W_uq': w(ks[5], (QC, H * HD), QC), 'W_qr': w(ks[6], (QC, H * R), QC), 'W_uk': w(ks[7], (KVC, H * HD), KVC), 'W_kr': w(ks[8], (KVC, R), KVC), 'W_uv': w(ks[9], (KVC, H * HD), KVC), 'W_o': w(ks[10], (H * HD, Q_DIM), H * HD)}
    _L0_xattn_all = _L0_xattn_setup()
    _L0_xattn_in = {k: v for k, v in _L0_xattn_all.items() if k in ('W_kvc', 'W_dq', 'W_uq', 'W_qr', 'W_uk', 'W_kr', 'W_uv', 'W_o')}
    del _L0_xattn_all

    def _L0_ffn_setup():
        import jax, jax.numpy as jnp
        import numpy as np
        EPS = 1e-05

        def fwht(x):
            orig_shape = x.shape
            n = orig_shape[-1]
            x = x.reshape(-1, n)
            h = 1
            while h < n:
                x = x.reshape(-1, n // (2 * h), 2, h)
                a, b = (x[:, :, 0, :], x[:, :, 1, :])
                x = jnp.stack([a + b, a - b], axis=2).reshape(-1, n)
                h *= 2
            return (x * (1.0 / np.sqrt(n))).reshape(orig_shape)

        def act_quant(x):
            scale = 127.0 / jnp.clip(jnp.max(jnp.abs(x), axis=-1, keepdims=True), EPS)
            q = jnp.clip(jnp.round(x * scale), -128.0, 127.0) / scale
            return x + jax.lax.stop_gradient(q - x)

        def weight_quant(w):
            scale = jnp.clip(jnp.mean(jnp.abs(w)), EPS)
            q = jnp.clip(jnp.round(w / scale), -1.0, 1.0) * scale
            return w + jax.lax.stop_gradient(q - w)

        def h_bitlinear(x, w):
            xq = act_quant(fwht(x))
            wq = weight_quant(w)
            return jnp.einsum('bsh,oh->bso', xq, wq)
        key = jax.random.key(seed)
        k1, k2, k3, k4 = jax.random.split(key, 4)
        H, I = (512, 2048)
        B, S = (2, 512)
        hidden_states = jax.random.normal(k1, (B, S, H), dtype=jnp.float32)
        w_gate = jax.random.normal(k2, (I, H), dtype=jnp.float32) * 0.02
        w_up = jax.random.normal(k3, (I, H), dtype=jnp.float32) * 0.02
        w_down = jax.random.normal(k4, (H, I), dtype=jnp.float32) * 0.02
        return {'hidden_states': hidden_states, 'w_gate': w_gate, 'w_up': w_up, 'w_down': w_down}
    _L0_ffn_all = _L0_ffn_setup()
    _L0_ffn_in = {k: v for k, v in _L0_ffn_all.items() if k in ('w_gate', 'w_up', 'w_down')}
    del _L0_ffn_all
    return {'x': x, 'ctx_2048': ctx_2048, 'itok_BxS_0_1023': itok_BxS_0_1023, 'L0_attn_wq': _L0_attn_in['wq'], 'L0_attn_wk': _L0_attn_in['wk'], 'L0_attn_wv': _L0_attn_in['wv'], 'L0_attn_wo': _L0_attn_in['wo'], 'L0_xattn_W_kvc': _L0_xattn_in['W_kvc'], 'L0_xattn_W_dq': _L0_xattn_in['W_dq'], 'L0_xattn_W_uq': _L0_xattn_in['W_uq'], 'L0_xattn_W_qr': _L0_xattn_in['W_qr'], 'L0_xattn_W_uk': _L0_xattn_in['W_uk'], 'L0_xattn_W_kr': _L0_xattn_in['W_kr'], 'L0_xattn_W_uv': _L0_xattn_in['W_uv'], 'L0_xattn_W_o': _L0_xattn_in['W_o'], 'L0_ffn_w_gate': _L0_ffn_in['w_gate'], 'L0_ffn_w_up': _L0_ffn_in['w_up'], 'L0_ffn_w_down': _L0_ffn_in['w_down']}

def reference(x, ctx_2048, itok_BxS_0_1023, L0_attn_wq, L0_attn_wk, L0_attn_wv, L0_attn_wo, L0_xattn_W_kvc, L0_xattn_W_dq, L0_xattn_W_uq, L0_xattn_W_qr, L0_xattn_W_uk, L0_xattn_W_kr, L0_xattn_W_uv, L0_xattn_W_o, L0_ffn_w_gate, L0_ffn_w_up, L0_ffn_w_down):
    import jax
    import jax.numpy as jnp

    def _L0_attn_ref(x, wq, wk, wv, wo):
        import jax, jax.numpy as jnp
        import numpy as np
        import math
        DIM = 512
        N_HEADS = 16
        N_KV_HEADS = 8
        HEAD_DIM = DIM // N_HEADS
        N_REP = N_HEADS // N_KV_HEADS
        BLOCK = 128
        TOPK = 8
        NEG_INF = -10000.0
        SEQ = 1024
        BS = 1

        def _rope_tables(seq_len, head_dim, base=10000.0):
            inv_freq = 1.0 / base ** (jnp.arange(0, head_dim, 2, dtype=jnp.float32) / head_dim)
            ang = jnp.arange(seq_len, dtype=jnp.float32)[:, None] * inv_freq[None, :]
            return (jnp.cos(ang), jnp.sin(ang))

        def _apply_rope(t, cos, sin):
            t1 = t[..., 0::2]
            t2 = t[..., 1::2]
            c = cos[None, :, None, :]
            s = sin[None, :, None, :]
            out_even = t1 * c - t2 * s
            out_odd = t1 * s + t2 * c
            out = jnp.stack([out_even, out_odd], axis=-1)
            return out.reshape(t.shape)
        bs, S, _ = x.shape
        inv_sqrt_d = 1.0 / math.sqrt(HEAD_DIM)
        q = (x @ wq).reshape(bs, S, N_HEADS, HEAD_DIM)
        k = (x @ wk).reshape(bs, S, N_KV_HEADS, HEAD_DIM)
        v = (x @ wv).reshape(bs, S, N_KV_HEADS, HEAD_DIM)
        cos, sin = _rope_tables(S, HEAD_DIM)
        q = _apply_rope(q, cos, sin)
        k = _apply_rope(k, cos, sin)
        q = jnp.transpose(q, (0, 2, 1, 3))
        k = jnp.transpose(k, (0, 2, 1, 3))
        v = jnp.transpose(v, (0, 2, 1, 3))
        k_e = jnp.repeat(k, N_REP, axis=1)
        v_e = jnp.repeat(v, N_REP, axis=1)
        num_blocks = S // BLOCK
        k_blocks = k_e.reshape(bs, N_HEADS, num_blocks, BLOCK, HEAD_DIM)
        block_means = k_blocks.mean(axis=3)
        gating = jnp.einsum('bhsd,bhnd->bhsn', q, block_means) * inv_sqrt_d
        q_block_idx = jnp.arange(S) // BLOCK
        future_block = q_block_idx[:, None] < jnp.arange(num_blocks)[None, :]
        gating = jnp.where(future_block[None, None], NEG_INF, gating)
        curr_k = min(TOPK, num_blocks)
        _, sel_idx = jax.lax.top_k(gating, curr_k)
        selected = jnp.sum(jax.nn.one_hot(sel_idx, num_blocks, dtype=jnp.float32), axis=-2) > 0
        token_keep = jnp.repeat(selected, BLOCK, axis=-1)[..., :S]
        token_mask = jnp.where(token_keep, 0.0, NEG_INF)
        scores = jnp.einsum('bhsd,bhtd->bhst', q, k_e) * inv_sqrt_d
        causal = jnp.triu(jnp.ones((S, S), dtype=jnp.float32), k=1)
        final_mask = jnp.maximum(token_mask, causal[None, None] * NEG_INF)
        scores = scores + final_mask
        probs = jax.nn.softmax(scores.astype(jnp.float32), axis=-1).astype(scores.dtype)
        out = jnp.einsum('bhst,bhtd->bhsd', probs, v_e)
        out = jnp.transpose(out, (0, 2, 1, 3)).reshape(bs, S, N_HEADS * HEAD_DIM)
        return out @ wo

    def _L0_xattn_ref(q, kv, seg_id, W_kvc, W_dq, W_uq, W_qr, W_uk, W_kr, W_uv, W_o):
        import jax, jax.numpy as jnp
        import numpy as np
        B, Lq, Lk = (2, 1024, 256)
        Q_DIM, KV_DIM = (512, 512)
        H, HD = (16, 128)
        KVC, QC, R = (128, 192, 64)
        LOOKBACK = 8
        NEG = -1e+30

        def _rope(x, L):
            half = x.shape[-1] // 2
            inv_freq = 1.0 / 10000.0 ** (jnp.arange(half, dtype=jnp.float32) / half)
            ang = jnp.arange(L, dtype=jnp.float32)[:, None] * inv_freq
            cos, sin = (jnp.cos(ang), jnp.sin(ang))
            x1, x2 = (x[..., :half], x[..., half:])
            return jnp.concatenate([x1 * cos - x2 * sin, x1 * sin + x2 * cos], axis=-1)
        b, lq, _ = q.shape
        lk = kv.shape[1]
        kv_c = kv @ W_kvc
        q_c = q @ W_dq
        q_nope = (q_c @ W_uq).reshape(b, lq, H, HD).transpose(0, 2, 1, 3)
        q_rope = (q_c @ W_qr).reshape(b, lq, H, R).transpose(0, 2, 1, 3)
        k_nope = (kv_c @ W_uk).reshape(b, lk, H, HD)
        v = (kv_c @ W_uv).reshape(b, lk, H, HD)
        k_rope = kv_c @ W_kr
        q_rope = _rope(q_rope, lq)
        k_rope = _rope(k_rope, lk)
        scale = 1.0 / np.sqrt(HD + R).astype(np.float32)
        scores = (jnp.einsum('bhqd,bkhd->bhqk', q_nope, k_nope) + jnp.einsum('bhqr,bkr->bhqk', q_rope, k_rope)) * scale
        k_ids = jnp.arange(lk)[None, None, :]
        qs = seg_id[:, :, None]
        good = (k_ids <= qs) & (k_ids >= qs - LOOKBACK)
        scores = jnp.where(good[:, None, :, :], scores, NEG)
        attn = jax.nn.softmax(scores, axis=-1)
        out = jnp.einsum('bhqk,bkhd->bqhd', attn, v).reshape(b, lq, H * HD)
        return out @ W_o

    def _L0_ffn_ref(hidden_states, w_gate, w_up, w_down):
        import jax, jax.numpy as jnp
        import numpy as np
        EPS = 1e-05

        def fwht(x):
            orig_shape = x.shape
            n = orig_shape[-1]
            x = x.reshape(-1, n)
            h = 1
            while h < n:
                x = x.reshape(-1, n // (2 * h), 2, h)
                a, b = (x[:, :, 0, :], x[:, :, 1, :])
                x = jnp.stack([a + b, a - b], axis=2).reshape(-1, n)
                h *= 2
            return (x * (1.0 / np.sqrt(n))).reshape(orig_shape)

        def act_quant(x):
            scale = 127.0 / jnp.clip(jnp.max(jnp.abs(x), axis=-1, keepdims=True), EPS)
            q = jnp.clip(jnp.round(x * scale), -128.0, 127.0) / scale
            return x + jax.lax.stop_gradient(q - x)

        def weight_quant(w):
            scale = jnp.clip(jnp.mean(jnp.abs(w)), EPS)
            q = jnp.clip(jnp.round(w / scale), -1.0, 1.0) * scale
            return w + jax.lax.stop_gradient(q - w)

        def h_bitlinear(x, w):
            xq = act_quant(fwht(x))
            wq = weight_quant(w)
            return jnp.einsum('bsh,oh->bso', xq, wq)
        gate = h_bitlinear(hidden_states, w_gate)
        up = h_bitlinear(hidden_states, w_up)
        return h_bitlinear(jax.nn.silu(gate) * up, w_down)
    x = x + _L0_attn_ref(_layernorm(x, axis=-1), L0_attn_wq, L0_attn_wk, L0_attn_wv, L0_attn_wo)
    x = x + _L0_xattn_ref(_layernorm(x, axis=-1), ctx_2048, itok_BxS_0_1023, L0_xattn_W_kvc, L0_xattn_W_dq, L0_xattn_W_uq, L0_xattn_W_qr, L0_xattn_W_uk, L0_xattn_W_kr, L0_xattn_W_uv, L0_xattn_W_o)
    x = x + _L0_ffn_ref(_layernorm(x, axis=-1), L0_ffn_w_gate, L0_ffn_w_up, L0_ffn_w_down)
    return x

_drawn_inputs = setup_inputs


def setup_inputs(seed=0):
    import zlib

    import numpy as np

    out = dict(_drawn_inputs(seed))
    spreads = {}
    factors = {}
    for name, (base, spread) in spreads.items():
        noise = np.random.default_rng([zlib.crc32(name.encode()), seed]).standard_normal(out[name].shape)
        drawn = base * np.exp(spread * noise) if base else spread * noise
        out[name] = jnp.asarray(drawn.astype(out[name].dtype))
    for name, factor in factors.items():
        out[name] = (out[name] * factor).astype(out[name].dtype)
    return out
```

```python
from contextlib import ExitStack

import concourse.bass as bass
from concourse import mybir

P = 128
F32 = mybir.dt.float32
F32R = mybir.dt.float32r
BF16 = mybir.dt.bfloat16
F8 = mybir.dt.float8e4
I32 = mybir.dt.int32
ALU = mybir.AluOpType
ACT = mybir.ActivationFunctionType
AX = mybir.AxisListType

B, S, D = 8, 512, 512
NT = S // P
KC = D // P
H, G, HD = 16, 8, 32
LK, KVC, QC, R = 64, 128, 192, 64
QC1 = QC - P
HP = H // 2
F = 2048
FC = F // P
FG = F // 512
EPS = 1e-5
NEG = -1e30
MAGIC = 12582912.0
SELF_SCALE = float(HD) ** -0.5
X_SCALE = float(P + R) ** -0.5
C512 = float(D) ** -0.5
C2048 = float(F) ** -0.5
NCOPY = 6

PER = dict(
    x_in=16, seg_in=16, stack=3 * NCOPY * 16, rows_in=32, v_in=16, ak_in=48, store0=32, store1=32,
    mv=12, rstd=12, xn=12, xt_ps=12, xt=12,
    proj=6, v_ps=4, vw=4, rope_m=12, rope_c=6, rope_h=6, rope_l=6,
    smax_ps=16, smax=16, nms=4, nmt_ps=1, nmt=1,
    st_ps=32, probs=32, pv=16, at=8, wo_ps=4, x1=4,
    dq_ps=2, qc=2, xr_ps=16, xcs=16, sc_ps=4, masked=4, centred=4, xexp=4, xden=4, xprob=4,
    pt_ps=8, ptx=8, xo_ps=4, x2=4, maskt=1, ks_ones=1,
    had_ps=4, fsc=4, fround=4, fint=4, fintT_ps=4, fintT=4, gate_ps=16, th=16, hid=16,
    add1=4, add2=4, hidT_ps=16, hidT=16, had2_ps=4, f2sc=4, f2round=4, f2int=4,
    f2intT_ps=8, f2intT=8, down_ps=4, y=4,
    dve_step=92, pool_step=21,
)


def block_kernel(nc, x, seg, ctxT, wq, wk, wv, wo, wkvc, wdq, wuqT, wqr, wukT, wkr2, wkrs2, wuvT, wox,
                 gateT, upT, downT, had, rope, krope, iota, ident, out):
    ctx = ExitStack()
    with ctx:
        base = 16512
        at_byte = [base]

        def place(name, shape, dt, offset=None):
            size = 1
            for n in shape[1:]:
                size *= n
            size *= {F32: 4, F32R: 4, I32: 4, BF16: 2, F8: 1}[dt]
            if offset is None:
                offset = at_byte[0]
                at_byte[0] += (size + 31) // 32 * 32
            return nc.alloc_sbuf_tensor_at(name, shape, dt, offset=offset)

        wq_sb = place("wq_sb", [P, KC, D], F32)
        wk_sb = place("wk_sb", [P, KC, G * HD], F32)
        wv_sb = place("wv_sb", [P, KC, G * HD], F32)
        wo_sb = place("wo_sb", [P, KC, D], F32)
        wdq_sb = place("wdq_sb", [P, KC, QC], F32)
        wqr0 = place("wqr0", [P, H * R], F32)
        wqr1 = place("wqr1", [QC1, H * R], F32)
        had_sb = place("had_sb", [P, KC, D], F32)
        ffn_at = at_byte[0]
        gate_w = place("gate_w", [P, KC, F], F8)
        up_w = place("up_w", [P, KC, F], F8)
        down_w = place("down_w", [P, FC, D], F8)
        rope_sb = place("rope_sb", [P, 4, S], F32)
        ident_f = place("ident_f", [P, P], F32)
        ident_b = place("ident_b", [P, P], BF16)
        iota_sb = place("iota_sb", [P, LK], F32)
        ones_at = at_byte[0]
        maskt = place("maskt", [P, NT, LK], F32)
        mask_lo = place("mask_lo", [P, LK], F32)
        xcur_at = at_byte[0]
        xcur = place("xcur", [P, NT, D], F32)
        xin_at = at_byte[0]
        xin = place("xin", [P, NT, D], F32)
        seg_i = place("seg_i", [P, NT], I32)
        seg_f = place("seg_f", [P, NT], F32)
        seg_8 = place("seg_8", [P, NT], F32)
        stats = place("stats", [P, 12, 6], F32)
        mv = place("mv", [P, 12, 2], F32)
        vare = place("vare", [P, 12], F32)
        rstd = place("rstd", [P, 12], F32)
        mhalf = place("mhalf", [P, 1], F32)
        negmax = place("negmax", [P, NT, H], F32)
        negsplit = place("negsplit", [P, NT, 2 * H], F32R)
        xmax = place("xmax", [P, NT, H], F32)
        xsum = place("xsum", [P, NT, H], F32)
        xrec = place("xrec", [P, NT, H], F32)
        fs = place("fs", [P, NT, 8], F32)
        f2s = place("f2s", [P, NT, 8], F32)
        wsum = place("wsum", [P, 3], F32)
        wsc = place("wsc", [P, 3], F32)
        wthr = place("wthr", [P, 6], F32)
        ones = place("ones", [P, P], F32, ones_at)
        arena = at_byte[0]
        A_ROPE, A_Q = arena, arena + 16384
        A_K = A_Q + 32768
        A_V = A_K + 16384
        A_P = A_V + 4 * (G * P + 32) * 4
        A_XT = A_P + 16384
        A_XN = A_XT + 8192
        A_ROWS = A_RC = A_XN + 4096
        assert A_ROWS + 2048 <= 229344, A_ROWS + 2048 - 229344

        rot = place("rot", [P, 4, S], F32, A_ROPE)
        parts = place("parts", [P, 4, S], F32R, A_ROPE + 8192)
        qs = place("qs", [P, H, S], F32R, A_Q)
        ks = place("ks", [P, G, S], F32R, A_K)
        vw = place("vw", [P, NT, G * P + 32], F32, A_V)
        pt = place("pt", [P, 4, 1024], F32, A_P)
        rcp = place("rcp", [64, S], F32, A_RC)
        xT = place("xT", [P, KC, S], F32, A_XT)
        aT = place("aT", [P, KC, S], F32, A_XT)
        xn = place("xn", [P, 2, D], F32, A_XN)
        rows = place("rows", [2 * H, S], F32R, A_ROWS)
        vp = place("vp", [P, HP, D], F32, A_ROPE)
        xc = place("xc", [P, HP, 256], F32, A_Q)
        xs = place("xs", [P, HP, 256], F32, A_Q + 8192)
        ex = place("ex", [P, 2, H, LK], F32, A_Q + 16384)
        ptx = place("ptx", [P, HP, P], F32, A_Q + 24576)
        qc0 = place("qc0", [P, S], F32, A_Q + 28672)
        qc1 = place("qc1", [QC1, S], F32, A_Q + 30720)
        ak0 = place("ak0", [P, H * LK], F32, A_K)
        ak1 = place("ak1", [QC1, H * LK], F32, A_K + 4096)
        kd = place("kd", [P, 2, P], F32, A_K + 8192)
        xT3 = place("xT3", [P, KC, P], F32, A_K + 9216)
        fv = place("fv", [P, D], F32, A_K + 11264)
        fq = place("fq", [P, D], BF16, A_K + 13312)
        fqT = place("fqT", [P, KC, P], BF16, A_K + 14336)
        hid = place("hid", [P, FG, 512], F32, A_P)
        sd = place("sd", [P, 2, 2, 512], F32, A_P + 8192)
        f2v = place("f2v", [P, F], F32, A_P + 8192)
        th = place("th", [P, 512], F32, A_RC)
        gw = place("gw", [P, 512], F32, A_Q)
        yo = place("yo", [P, 2, 512], F32, A_Q + 2048)
        hidT = place("hidT", [P, FC, P], F32, A_ROPE)
        f2q = place("f2q", [P, F], BF16, A_ROPE + 8192)
        f2qT = place("f2qT", [P, FC, P], BF16, A_ROPE + 12288)
        wox_sb = place("wox_sb", [P, H, D], F32, arena)
        nn = place("nn", [P, H, D], F32, arena + 32768)
        wukT_sb = place("wukT_sb", [P, H, KVC], F32, arena + 65536)
        wuqT_sb = place("wuqT_sb", [P, H, QC], F32, arena + 73728)
        wuvT_sb = place("wuvT_sb", [P, H, KVC], F32, arena + 86016)
        mt = place("mt", [P, H, QC], F32, arena + 94208)
        kd_all = place("kd_all", [P, B, 2, P], F32, arena + 106496)
        ast0 = place("ast0", [P, B, H, LK], F32, arena)
        ast1 = place("ast1", [QC1, B, H, LK], F32, arena + 32768)
        vst = place("vst", [P, 4, D], F32, ffn_at)
        ktmp = place("ktmp", [P, 4, D], F32, ffn_at + 8192)
        ctxT_sb = place("ctxT_sb", [P, KC, D], F32, xcur_at)
        wkvc_sb = place("wkvc_sb", [P, KC, KVC], F32, xin_at)
        kvT = place("kvT", [P, B * LK], F32, xin_at + 2048)
        wkr_sb = place("wkr_sb", [P, 2, P], F32, xin_at + 4096)
        krope_sb = place("krope_sb", [P, 4, LK], F32, xin_at + 5120)
        wst = [place(f"wst{n}", [P, KC * F], F32, arena + 32768 * n) for n in range(3)]
        wlow = place("wlow", [P, KC * F], BF16, arena + 98304)

        ps = ctx.enter_context(nc.psum_tensor("ps", [P, 8, 512], F32))

        v_dram = nc.dram_tensor("v_scratch", [B, H, LK, D], F32, kind="Internal").ap()
        a0_dram = nc.dram_tensor("a0_scratch", [B, P, H * LK], F32, kind="Internal").ap()
        a1_dram = nc.dram_tensor("a1_scratch", [B, QC1, H * LK], F32, kind="Internal").ap()
        k_dram = nc.dram_tensor("k_scratch", [B, P, 2 * P], F32, kind="Internal").ap()

        sems = {n: ctx.enter_context(nc.semaphore(n)) for n in PER}

        def psem(name):
            return ctx.enter_context(nc.semaphore(name))

        in_weights, in_kv, in_ffn, in_const = psem("in_weights"), psem("in_kv"), psem("in_ffn"), psem("in_const")
        p_ps, p_act, p_dve, p_ffn_ps = psem("p_ps"), psem("p_act"), psem("p_dve"), psem("p_ffn_ps")
        p_vstore = [psem(f"p_vstore{n}") for n in range(4)]
        p_store = psem("p_store")
        ffn_step, p_const, kv_done = psem("ffn_step"), psem("p_const"), psem("kv_done")
        p_kzero, ffn_done, vw_const, vw_zero = psem("p_kzero"), psem("ffn_done"), psem("vw_const"), psem("vw_zero")
        passed = psem("passed")

        def at(name, i, k):
            return i * PER[name] + (PER[name] + k)

        def apart(eng):
            eng.sem_inc(passed, 1)

        block = ctx.enter_context(nc.Block())

        @block.sync
        def _(sp):
            for name in PER:
                sp.sem_inc(sems[name], PER[name])
            for dst, src in (
                (ctxT_sb[:, :, :], ctxT.rearrange("(c p) n -> p c n", p=P)),
                (wkvc_sb[:, :, :], wkvc.rearrange("(c p) n -> p c n", p=P)),
                (wkr_sb[:, 0, :], wkr2), (wkr_sb[:, 1, :], wkrs2),
                (krope_sb[:, :, :], krope), (ident_f[:, :], ident),
                (wukT_sb[:, :, :], wukT.rearrange("(h p) n -> p h n", p=P)),
                (wuqT_sb[:, :, :], wuqT.rearrange("(h p) n -> p h n", p=P)),
                (wuvT_sb[:, :, :], wuvT.rearrange("(h p) n -> p h n", p=P)),
                (wox_sb[:, :, :], wox.rearrange("(h p) n -> p h n", p=P)),
            ):
                sp.dma_start(dst, src).then_inc(in_kv, 16)
            for dst, src in (
                (wq_sb[:, :, :], wq.rearrange("(c p) n -> p c n", p=P)),
                (wk_sb[:, :, :], wk.rearrange("(c p) n -> p c n", p=P)),
                (wv_sb[:, :, :], wv.rearrange("(c p) n -> p c n", p=P)),
                (wo_sb[:, :, :], wo.rearrange("(c p) n -> p c n", p=P)),
                (wdq_sb[:, :, :], wdq.rearrange("(c p) n -> p c n", p=P)),
                (wqr0[:, :], wqr[0:P, :]), (wqr1[:, :], wqr[P:QC, :]),
                (had_sb[:, :, :], had.rearrange("(c p) n -> p c n", p=P)),
                (rope_sb[:, :, :], rope), (iota_sb[:, :], iota),
            ):
                sp.dma_start(dst, src).then_inc(in_weights, 16)
            for n in range(4 * H):
                bp, h = n // H, n % H
                sp.wait_ge(p_dve if n % 2 else p_act, PV_DVE[n] if n % 2 else PV_ACT[n])
                sp.dma_start(v_dram[2 * bp:2 * bp + 2, h, :, :],
                             vst[:, n % 4, :]).then_inc(p_vstore[n % 4], 16)
            sp.wait_ge(kv_done, 2)
            sp.dma_start(a0_dram.rearrange("b p n -> p b n"),
                         ast0[:, :, :, :].rearrange("p b h k -> p b (h k)")).then_inc(p_store, 16)
            sp.dma_start(a1_dram.rearrange("b p n -> p b n"),
                         ast1[:, :, :, :].rearrange("p b h k -> p b (h k)")).then_inc(p_store, 16)
            sp.dma_start(k_dram.rearrange("b p n -> p b n"),
                         kd_all[:, :, :, :].rearrange("p b t n -> p b (t n)")).then_inc(p_store, 16)
            for n in range(4):
                sp.wait_ge(p_vstore[n], 16 * H)
            sp.wait_ge(p_store, 48)
            for n, w in enumerate((gateT.rearrange("(c p) n -> p c n", p=P), upT.rearrange("(c p) n -> p c n", p=P),
                                   downT.rearrange("(c p) n -> p c n", p=P))):
                sp.dma_start(wst[n][:, :].rearrange("p (c n) -> p c n", n=w.shape[2]), w).then_inc(in_ffn, 16)
            sp.dma_start(xin[:, :, :], x[0, :, :].rearrange("(t p) d -> p t d", p=P)).then_inc(sems["x_in"], 16)

            def batch_row(i, more):
                def row(t):
                    return t[bass.ds(i, 1)]
                sp.wait_ge(sems["y"], at("y", i, 0))
                sp.dma_start(seg_i[:, :], row(seg).rearrange("o p t -> (o p) t")).then_inc(sems["seg_in"], 16)
                for n in range(2):
                    sp.wait_ge(sems[f"store{n}"], at(f"store{n}", i, 0))
                for j in range(3):
                    dst = ks[:, :, :] if j == 0 else qs[:, G * (j - 1):G * j, :]
                    kinds = (0, 0, 1) if j == 0 else (0, 1, 0)
                    for kind in range(2):
                        sp.wait_ge(sems["rope_l" if kind else "rope_h"], at("rope_l" if kind else "rope_h", i, 2 * j + 2))
                        for c in range(3):
                            if kinds[c] != kind:
                                continue
                            for odd in range(2):
                                r0 = 32 * c + 16 * odd
                                sp.dma_start(dst[r0:r0 + 16, :, :].bitcast(F32),
                                             parts[:, 2 * kind + odd, :].bitcast(F32)).then_inc(sems["stack"], 16)
                sp.wait_ge(sems["stack"], at("stack", i, PER["stack"]))
                sp.dma_start(vp[:, :, :].rearrange("p c n -> p c n"),
                             row(v_dram).rearrange("o (c u) k n -> (o u k) c n", u=2)).then_inc(sems["v_in"], 16)
                sp.wait_ge(sems["nmt"], at("nmt", i, 1))
                for part in range(2):
                    sp.dma_start(qs[96 + part:97 + part, :, :].bitcast(F32),
                                 rows[H * part:H * part + H, :].bitcast(F32)).then_inc(sems["rows_in"], 16)
                sp.wait_ge(sems["st_ps"], at("st_ps", i, PER["st_ps"]))
                sp.dma_start(ak0[:, :], row(a0_dram).rearrange("o p n -> (o p) n")).then_inc(sems["ak_in"], 16)
                sp.dma_start(ak1[:, :], row(a1_dram).rearrange("o p n -> (o p) n")).then_inc(sems["ak_in"], 16)
                sp.dma_start(kd[:, :, :].rearrange("p t n -> p (t n)"),
                             row(k_dram).rearrange("o p n -> (o p) n")).then_inc(sems["ak_in"], 16)
                if more:
                    sp.wait_ge(sems["x1"], at("x1", i, PER["x1"]))
                    sp.dma_start(xin[:, :, :], x[bass.ds(i + 1, 1)].rearrange("o (t p) d -> p (o t) d", p=P)
                                 ).then_inc(sems["x_in"], 16)
                for t in range(NT):
                    sp.wait_ge(sems["y"], at("y", i, t + 1))
                    sp.dma_start(out[bass.ds(i, 1), t * P:(t + 1) * P, :].rearrange("o p d -> (o p) d"),
                                 yo[:, t % 2, :]).then_inc(sems[f"store{t % 2}"], 16)

            with sp.Fori(0, B - 1) as i:
                batch_row(i, True)
            batch_row(B - 1, False)
            for n in range(2):
                sp.wait_ge(sems[f"store{n}"], at(f"store{n}", B, 0))

        @block.tensor
        def _(pe):
            def prologue_bank(n):
                if n >= 8:
                    s, k = PJOBS[n - 8]
                    pe.wait_ge(p_act if s == "act" else p_dve, k)
                return n % 8

            pe.wait_ge(in_kv, 160)
            n = 0
            b_ = prologue_bank(n)
            for c in range(KC):
                mm = pe.matmul(ps[:, b_, :], wkvc_sb[:, c, :], ctxT_sb[:, c, :], start=c == 0, stop=c == KC - 1)
            mm.then_inc(p_ps, 1)
            n += 1
            pe.wait_ge(p_act, 1)
            for s in range(2):
                pe.matmul(ps[:, prologue_bank(n), :], wkr_sb[:, s, :], kvT[:, :], start=True, stop=True).then_inc(p_ps, 1)
                n += 1
            for h in range(H):
                pe.matmul(ps[:, prologue_bank(n), 0:QC], wukT_sb[:, h, :], wuqT_sb[:, h, :], start=True, stop=True
                          ).then_inc(p_ps, 1)
                n += 1
            for h in range(H):
                pe.matmul(ps[:, prologue_bank(n), :], wuvT_sb[:, h, :], wox_sb[:, h, :], start=True, stop=True
                          ).then_inc(p_ps, 1)
                n += 1
            pe.wait_ge(p_dve, NN_DVE)
            for m in range(4 * H):
                bp, h = m // H, m % H
                pe.matmul(ps[:, prologue_bank(n), :], kvT[:, bp * P:(bp + 1) * P], nn[:, h, :], start=True, stop=True
                          ).then_inc(p_ps, 1)
                n += 1
            for h in range(H):
                pe.matmul(ps[:, prologue_bank(n), :], mt[:, h, 0:P], kvT[:, :], start=True, stop=True).then_inc(p_ps, 1)
                n += 1
                pe.matmul(ps[0:QC1, prologue_bank(n), :], mt[:, h, P:QC], kvT[:, :], start=True, stop=True).then_inc(p_ps, 1)
                n += 1
            pe.wait_ge(ffn_step, 3)
            pe.wait_ge(p_const, 2)
            pe.matmul(ps[:, prologue_bank(n), 0:3], ones[:, :], wsum[:, :], start=True, stop=True).then_inc(p_ffn_ps, 1)
            pe.wait_ge(in_weights, 160)
            pe.wait_ge(ffn_done, 1)
            pe.wait_ge(vw_const, 1)

            with pe.Fori(0, B) as i:
                reader = {}

                def take(*banks):
                    need = {}
                    for b in banks:
                        if b in reader:
                            name, k = reader[b]
                            need[name] = max(need.get(name, k), k)
                    for name, k in need.items():
                        pe.wait_ge(sems[name], at(name, i, k))

                def transposes_of_xn(n, b):
                    pe.wait_ge(sems["xn"], at("xn", i, n + 1))
                    take(b)
                    for c in range(KC):
                        mm = pe.transpose(ps[:, b, c * P:(c + 1) * P], xn[:, n % 2, c * P:(c + 1) * P], ident_f[:, :])
                    mm.then_inc(sems["xt_ps"], 1)
                    reader[b] = ("xt", n + 1)

                pe.wait_ge(sems["y"], at("y", i, 0))
                for t in range(NT):
                    transposes_of_xn(t, t % 2)
                pe.wait_ge(sems["xt"], at("xt", i, 4))
                for j in range(3):
                    for odd in range(2):
                        b = 2 + (2 * j + odd) % 6
                        take(b)
                        for c in range(KC):
                            w = wk_sb[:, c, odd * P:(odd + 1) * P] if j == 0 else \
                                wq_sb[:, c, (2 * j - 2 + odd) * P:(2 * j - 1 + odd) * P]
                            mm = pe.matmul(ps[:, b, :], w, xT[:, c, :], start=c == 0, stop=c == KC - 1)
                        mm.then_inc(sems["proj"], 1)
                        reader[b] = ("rope_m", 4 * j + 4)
                for t in range(NT):
                    b = t % 2
                    take(b)
                    for c in range(KC):
                        mm = pe.matmul(ps[:, b, 0:G * HD], xT[:, c, t * P:(t + 1) * P], wv_sb[:, c, :],
                                       start=c == 0, stop=c == KC - 1)
                    mm.then_inc(sems["v_ps"], 1)
                    reader[b] = ("vw", t + 1)
                pe.wait_ge(sems["stack"], at("stack", i, PER["stack"]))
                for n in range(4 * NT):
                    t, hq = n // 4, n % 4
                    b0 = 4 * (n % 2)
                    take(*range(b0, b0 + 4))
                    for u in range(4):
                        h = 4 * hq + u
                        mm = pe.matmul(ps[:, b0 + u, :], qs[0:96, h, t * P:(t + 1) * P], ks[0:96, h // 2, :],
                                       start=True, stop=True)
                        reader[b0 + u] = ("smax", n + 1)
                    mm.then_inc(sems["smax_ps"], 1)
                pe.wait_ge(sems["nms"], at("nms", i, 4))
                take(0)
                for t in range(NT):
                    mm = pe.transpose(ps[0:2 * H, 0, t * P:(t + 1) * P], negsplit[:, t, :].bitcast(F32), ident_f[:, :])
                mm.then_inc(sems["nmt_ps"], 1)
                reader[0] = ("nmt", 1)

                def scores(j):
                    h, half = j // 2, j % 2
                    b0 = 2 * (j % 3)
                    take(b0, b0 + 1)
                    for u in range(2):
                        kt = 2 * half + u
                        mm = pe.matmul(ps[:, b0 + u, :], ks[0:98, h // 2, kt * P:(kt + 1) * P], qs[0:98, h, :],
                                       start=True, stop=True)
                        reader[b0 + u] = ("probs", j + 1)
                    mm.then_inc(sems["st_ps"], 1)

                def weigh(j):
                    h, half = j // 2, j % 2
                    b = 6 + (h // 2) % 2
                    pe.wait_ge(sems["probs"], at("probs", i, j + 1))
                    if j % 4 == 0:
                        take(b)
                    lo = (h // 2) * P + (0 if h % 2 else 32)
                    for u in range(2):
                        kt = 2 * half + u
                        mm = pe.matmul(ps[:, b, :], vw[:, kt, lo:lo + P], pt[:, j % 4, u * 512:(u + 1) * 512],
                                       start=j % 4 == 0 and u == 0, stop=j % 4 == 3 and u == 1)
                    if half:
                        mm.then_inc(sems["pv"], 1)
                    reader[b] = ("at", h // 2 + 1)

                pe.wait_ge(sems["rows_in"], at("rows_in", i, 32))
                pe.wait_ge(sems["ks_ones"], at("ks_ones", i, 1))
                pe.wait_ge(sems["vw"], at("vw", i, 4))
                scores(0)
                scores(1)
                for j in range(2 * H):
                    if j + 2 < 2 * H:
                        scores(j + 2)
                    weigh(j)
                pe.wait_ge(sems["at"], at("at", i, HP))
                for t in range(NT):
                    take(t)
                    for c in range(KC):
                        mm = pe.matmul(ps[:, t, :], aT[:, c, t * P:(t + 1) * P], wo_sb[:, c, :],
                                       start=c == 0, stop=c == KC - 1)
                    mm.then_inc(sems["wo_ps"], 1)
                    reader[t] = ("x1", t + 1)

                for t in range(NT):
                    transposes_of_xn(4 + t, 4 + t % 2)
                pe.wait_ge(sems["xt"], at("xt", i, 8))
                for m, (lo, hi) in enumerate(((0, P), (P, QC))):
                    take(6 + m)
                    for c in range(KC):
                        mm = pe.matmul(ps[0:hi - lo, 6 + m, :], wdq_sb[:, c, lo:hi], xT[:, c, :],
                                       start=c == 0, stop=c == KC - 1)
                    mm.then_inc(sems["dq_ps"], 1)
                    reader[6 + m] = ("qc", m + 1)
                pe.wait_ge(sems["qc"], at("qc", i, 2))

                def rope_queries(half):
                    for p in range(HP):
                        m = HP * half + p
                        b = m % 4
                        take(b)
                        q = slice(256 * half, 256 * half + 256)
                        pe.matmul(ps[:, b, 0:256], wqr0[:, p * P:(p + 1) * P], qc0[:, q], start=True, stop=False)
                        pe.matmul(ps[:, b, 0:256], wqr1[:, p * P:(p + 1) * P], qc1[:, q], start=False, stop=True
                                  ).then_inc(sems["xr_ps"], 1)
                        reader[b] = ("xcs", m + 1)

                def cross_scores(t):
                    pe.wait_ge(sems["xcs"], at("xcs", i, HP * (t // 2 + 1)))
                    q = slice(t * P, t * P + P)
                    ql = slice((t % 2) * P, (t % 2) * P + P)
                    for hb in range(2):
                        b = 4 + 2 * (t % 2) + hb
                        take(b)
                        cols = slice(512 * hb, 512 * hb + 512)
                        pe.matmul(ps[:, b, :], qc0[:, q], ak0[:, cols], start=True, stop=False)
                        pe.matmul(ps[:, b, :], qc1[:, q], ak1[:, cols], start=False, stop=False)
                        for u in range(4):
                            p = 4 * hb + u
                            pe.matmul(ps[:, b, u * P:(u + 1) * P], xc[:, p, ql], kd[:, 0, :], start=False, stop=False)
                            mm = pe.matmul(ps[:, b, u * P:(u + 1) * P], xs[:, p, ql], kd[:, 1, :],
                                           start=False, stop=u == 3)
                        reader[b] = ("masked", t + 1)
                    mm.then_inc(sems["sc_ps"], 1)

                def cross_out(t):
                    pe.wait_ge(sems["xprob"], at("xprob", i, t + 1))
                    for hb in range(2):
                        take(hb)
                        for u in range(4):
                            p = 4 * hb + u
                            mm = pe.transpose(ps[:, hb, u * P:(u + 1) * P],
                                              ex[:, t % 2, 2 * p:2 * p + 2, :].rearrange("p h k -> p (h k)"), ident_f[:, :])
                        mm.then_inc(sems["pt_ps"], 1)
                        reader[hb] = ("ptx", 2 * t + hb + 1)
                    b = 2 + t % 2
                    take(b)
                    pe.wait_ge(sems["ptx"], at("ptx", i, 2 * t + 2))
                    for p in range(HP):
                        mm = pe.matmul(ps[:, b, :], ptx[:, p, :], vp[:, p, :], start=p == 0, stop=p == HP - 1)
                    mm.then_inc(sems["xo_ps"], 1)
                    reader[b] = ("x2", t + 1)

                rope_queries(0)
                pe.wait_ge(sems["ak_in"], at("ak_in", i, 48))
                cross_scores(0)
                cross_scores(1)
                rope_queries(1)
                pe.wait_ge(sems["v_in"], at("v_in", i, 16))
                cross_out(0)
                cross_scores(2)
                cross_out(1)
                cross_scores(3)
                cross_out(2)
                cross_out(3)

                def ffn_rotate(t):
                    take(1)
                    pe.wait_ge(sems["xt"], at("xt", i, 8 + t + 1))
                    for c in range(KC):
                        mm = pe.matmul(ps[:, 1, :], xT3[:, c, :], had_sb[:, c, :], start=c == 0, stop=c == KC - 1)
                    mm.then_inc(sems["had_ps"], 1)
                    reader[1] = ("fround", t + 1)

                def ffn_integers(t):
                    take(0)
                    pe.wait_ge(sems["fint"], at("fint", i, t + 1))
                    for c in range(KC):
                        mm = pe.transpose(ps[:, 0, :].bitcast(BF16)[:, c * P:(c + 1) * P], fq[:, c * P:(c + 1) * P],
                                          ident_b[:, :])
                    mm.then_inc(sems["fintT_ps"], 1)
                    reader[0] = ("fintT", t + 1)

                def ffn_gate_up(t):
                    pe.wait_ge(sems["fintT"], at("fintT", i, t + 1))
                    for g in range(FG):
                        b = 2 * (g % 2)
                        take(b, b + 1)
                        apart(pe)
                        for k, w in ((0, gate_w), (1, up_w)):
                            for c in range(KC):
                                mm = pe.matmul(ps[:, b + k, :], fqT[:, c, :], w[:, c, g * 512:(g + 1) * 512],
                                               start=c == 0, stop=c == KC - 1)
                            reader[b + k] = ("hid", FG * t + g + 1)
                        mm.then_inc(sems["gate_ps"], 1)

                def ffn_hidden_transposes(t):
                    pe.wait_ge(sems["add2"], at("add2", i, t + 1))
                    for g in range(FG):
                        b = 2 + g % 2
                        take(b)
                        for c in range(4):
                            mm = pe.transpose(ps[:, b, c * P:(c + 1) * P], hid[:, g, c * P:(c + 1) * P], ident_f[:, :])
                        mm.then_inc(sems["hidT_ps"], 1)
                        reader[b] = ("hidT", FG * t + g + 1)

                def ffn_hidden_rotate(t):
                    for g in range(FG):
                        take(4 + g)
                        pe.wait_ge(sems["hidT"], at("hidT", i, FG * t + g + 1))
                        for c in range(4):
                            mm = pe.matmul(ps[:, 4 + g, :], hidT[:, 4 * g + c, :], had_sb[:, c, :],
                                           start=c == 0, stop=c == 3)
                        reader[4 + g] = ("f2round", t + 1)
                    mm.then_inc(sems["had2_ps"], 1)

                def ffn_down(t):
                    pe.wait_ge(sems["f2int"], at("f2int", i, t + 1))
                    for half in range(2):
                        take(half)
                        for c in range(8):
                            k = 8 * half + c
                            mm = pe.transpose(ps[:, half, :].bitcast(BF16)[:, c * P:(c + 1) * P],
                                              f2q[:, k * P:(k + 1) * P], ident_b[:, :])
                        mm.then_inc(sems["f2intT_ps"], 1)
                        reader[half] = ("f2intT", 2 * t + half + 1)
                    take(2)
                    for half in range(2):
                        pe.wait_ge(sems["f2intT"], at("f2intT", i, 2 * t + half + 1))
                        apart(pe)
                        for c in range(8):
                            k = 8 * half + c
                            mm = pe.matmul(ps[:, 2, :], f2qT[:, k, :], down_w[:, k, :], start=k == 0, stop=k == FC - 1)
                    mm.then_inc(sems["down_ps"], 1)
                    reader[2] = ("y", t + 1)

                transposes_of_xn(8, 0)
                ffn_rotate(0)
                ffn_integers(0)
                ffn_gate_up(0)
                for t in range(NT):
                    more = t + 1 < NT
                    if more:
                        transposes_of_xn(8 + t + 1, 0)
                    ffn_hidden_transposes(t)
                    if more:
                        ffn_rotate(t + 1)
                    ffn_hidden_rotate(t)
                    if more:
                        ffn_integers(t + 1)
                        ffn_gate_up(t + 1)
                    ffn_down(t)

        @block.scalar
        def _(act):
            for n, (s, k) in enumerate(PJOBS):
                if s != "act":
                    continue
                act.wait_ge(p_ps, n + 1)
                if n == 0:
                    act.copy(kvT[:, :], ps[:, 0, :]).then_inc(p_act, 1)
                elif 3 <= n < 3 + H:
                    act.copy(mt[:, n - 3, :], ps[:, n % 8, 0:QC]).then_inc(p_act, 1)
                elif V0 <= n < A0:
                    m = n - V0
                    if m >= 4:
                        act.wait_ge(p_vstore[m % 4], 16 * (m // 4))
                    act.copy(vst[:, m % 4, :], ps[:, n % 8, :]).then_inc(p_act, 1)
                else:
                    h = (n - A0) // 2
                    act.copy(ast1[:, :, h, :], ps[0:QC1, n % 8, :].rearrange("p (b k) -> p b k", b=B)).then_inc(p_act, 1)
            act.wait_ge(p_act, NACT)
            act.sem_inc(kv_done, 1)
            act.wait_ge(in_kv, 160)
            act.copy(ident_b[:, :], ident_f[:, :]).then_inc(p_const, 1)

            with act.Fori(0, B) as i:
                def evacuate_xt(n, b, out):
                    act.wait_ge(sems["xt_ps"], at("xt_ps", i, n + 1))
                    act.copy(out, ps[:, b, :].rearrange("p (c q) -> p c q", c=KC)).then_inc(sems["xt"], 1)

                for t in range(NT):
                    evacuate_xt(t, t % 2, xT[:, :, t * P:(t + 1) * P])
                for j in range(3):
                    act.wait_ge(sems["rope_c"], at("rope_c", i, 2 * j + 2))
                    if j:
                        act.wait_ge(sems["stack"], at("stack", i, 16 * NCOPY * j))
                    for odd in range(2):
                        act.copy(parts[:, odd, :], rot[:, 2 * odd, :]).then_inc(sems["rope_h"], 1)
                for t in range(NT):
                    act.wait_ge(sems["v_ps"], at("v_ps", i, t + 1))
                    act.copy(vw[:, t, 0:G * P].rearrange("p (g c) -> p g c", c=P)[:, :, 32:64],
                             ps[:, t % 2, 0:G * HD].rearrange("p (g c) -> p g c", c=HD)).then_inc(sems["vw"], 1)
                act.wait_ge(sems["nmt_ps"], at("nmt_ps", i, 1))
                act.copy(rows[:, :], ps[0:2 * H, 0, :]).then_inc(sems["nmt"], 1)
                for j in range(2 * H):
                    act.wait_ge(sems["st_ps"], at("st_ps", i, j + 1))
                    if j >= 4:
                        act.wait_ge(sems["pv"], at("pv", i, (j - 4) // 2 + 1))
                    b0 = 2 * (j % 3)
                    act.activation(pt[:, j % 4, :], ps[:, b0:b0 + 2, :].rearrange("p b q -> p (b q)"), ACT.Exp,
                                   scale=SELF_SCALE).then_inc(sems["probs"], 1)
                for t in range(NT):
                    evacuate_xt(4 + t, 4 + t % 2, xT[:, :, t * P:(t + 1) * P])
                for m, q in enumerate((qc0, qc1)):
                    act.wait_ge(sems["dq_ps"], at("dq_ps", i, m + 1))
                    act.copy(q[:, :], ps[0:q.shape[0], 6 + m, :]).then_inc(sems["qc"], 1)

                def cross_exp(t):
                    act.wait_ge(sems["centred"], at("centred", i, t + 1))
                    e = ex[:, t % 2, :, :].rearrange("p h k -> p (h k)")
                    act.activation(e, e, ACT.Exp, scale=X_SCALE).then_inc(sems["xexp"], 1)

                def cross_evacuate(t):
                    for hb in range(2):
                        act.wait_ge(sems["pt_ps"], at("pt_ps", i, 2 * t + hb + 1))
                        if t:
                            act.wait_ge(sems["xo_ps"], at("xo_ps", i, t))
                        act.copy(ptx[:, 4 * hb:4 * hb + 4, :].rearrange("p c q -> p (c q)"), ps[:, hb, :]
                                 ).then_inc(sems["ptx"], 1)

                cross_exp(0)
                cross_exp(1)
                cross_evacuate(0)
                cross_exp(2)
                cross_evacuate(1)
                cross_exp(3)
                cross_evacuate(2)
                cross_evacuate(3)

                def ffn_xt(t):
                    if t:
                        act.wait_ge(sems["had_ps"], at("had_ps", i, t))
                    evacuate_xt(8 + t, 0, xT3[:, :, :])

                def ffn_round(t):
                    act.wait_ge(sems["fsc"], at("fsc", i, t + 1))
                    if t:
                        act.wait_ge(sems["fint"], at("fint", i, t))
                    act.activation(fv[:, :], ps[:, 1, :], ACT.Copy, bias=MAGIC, scale=fs[:, t, 2:3]
                                   ).then_inc(sems["fround"], 1)

                def ffn_intT(t):
                    act.wait_ge(sems["fintT_ps"], at("fintT_ps", i, t + 1))
                    if t:
                        act.wait_ge(sems["gate_ps"], at("gate_ps", i, FG * t))
                    act.copy(fqT[:, :, :].rearrange("p c q -> p (c q)"), ps[:, 0, :].bitcast(BF16)[:, 0:512]
                             ).then_inc(sems["fintT"], 1)

                def ffn_tanh(t):
                    for g in range(FG):
                        n = FG * t + g
                        act.wait_ge(sems["gate_ps"], at("gate_ps", i, n + 1))
                        if n:
                            act.wait_ge(sems["hid"], at("hid", i, n))
                        act.activation(th[:, :], ps[:, 2 * (g % 2), :], ACT.Tanh, scale=fs[:, t, 3:4]
                                       ).then_inc(sems["th"], 1)

                def ffn_hidT(t):
                    if t:
                        act.wait_ge(sems["had2_ps"], at("had2_ps", i, t))
                    for g in range(FG):
                        act.wait_ge(sems["hidT_ps"], at("hidT_ps", i, FG * t + g + 1))
                        act.copy(hidT[:, 4 * g:4 * g + 4, :].rearrange("p c q -> p (c q)"), ps[:, 2 + g % 2, :]
                                 ).then_inc(sems["hidT"], 1)

                def ffn_round2(t):
                    act.wait_ge(sems["f2sc"], at("f2sc", i, t + 1))
                    act.activation(f2v[:, :], ps[:, 4:8, :].rearrange("p b q -> p (b q)"), ACT.Copy, bias=MAGIC,
                                   scale=f2s[:, t, 2:3]).then_inc(sems["f2round"], 1)

                def ffn_int2T(t):
                    for half in range(2):
                        act.wait_ge(sems["f2intT_ps"], at("f2intT_ps", i, 2 * t + half + 1))
                        if t:
                            act.wait_ge(sems["down_ps"], at("down_ps", i, t))
                        act.copy(f2qT[:, 8 * half:8 * half + 8, :].rearrange("p c q -> p (c q)"),
                                 ps[:, half, :].bitcast(BF16)).then_inc(sems["f2intT"], 1)

                ffn_xt(0)
                ffn_round(0)
                ffn_intT(0)
                ffn_tanh(0)
                for t in range(NT):
                    more = t + 1 < NT
                    if more:
                        ffn_xt(t + 1)
                    ffn_hidT(t)
                    if more:
                        ffn_round(t + 1)
                    ffn_round2(t)
                    if more:
                        ffn_intT(t + 1)
                        ffn_tanh(t + 1)
                    ffn_int2T(t)

        @block.vector
        def _(dve):
            dve.wait_ge(in_kv, 160)
            for n, (s, k) in enumerate(PJOBS):
                if s != "dve":
                    continue
                dve.wait_ge(p_ps, n + 1)
                if n in (1, 2):
                    b3 = ps[:, n, :].rearrange("p (b k) -> p b k", b=B)
                    for v in range(2):
                        tab = krope_sb[:, 2 * v + n - 1:2 * v + n, :].broadcast_to([P, B, LK])
                        last = dve.tensor_tensor(ktmp[:, 2 * v + n - 1, :].rearrange("p (b k) -> p b k", b=B), b3, tab,
                                                 ALU.mult)
                    last.then_inc(p_dve, 1)
                    if n == 2:
                        dve.wait_ge(p_dve, 2)
                        dve.wait_ge(p_kzero, 1)
                        for v in range(2):
                            for u in range(2):
                                q = slice(64 * u, 64 * u + 64)
                                last = dve.tensor_tensor(
                                    kd_all[q, :, v, q],
                                    ktmp[q, 2 * v, :].rearrange("p (b k) -> p b k", b=B),
                                    ktmp[q, 2 * v + 1, :].rearrange("p (b k) -> p b k", b=B), ALU.add)
                elif 3 + H <= n < V0:
                    dve.tensor_copy(nn[:, n - 3 - H, :], ps[:, n % 8, :]).then_inc(p_dve, 1)
                elif V0 <= n < A0:
                    m = n - V0
                    if m >= 4:
                        dve.wait_ge(p_vstore[m % 4], 16 * (m // 4))
                    dve.tensor_copy(vst[:, m % 4, :], ps[:, n % 8, :]).then_inc(p_dve, 1)
                else:
                    h = (n - A0) // 2
                    if h == 0:
                        dve.wait_ge(p_ps, A0)
                    dve.tensor_copy(ast0[:, :, h, :], ps[:, n % 8, :].rearrange("p (b k) -> p b k", b=B)).then_inc(p_dve, 1)
            dve.wait_ge(p_dve, NDVE)
            dve.sem_inc(kv_done, 1)
            dve.wait_ge(in_ffn, 48)
            for n in range(3):
                dve.tensor_reduce(wsum[:, n:n + 1], wst[n][:, :], AX.X, ALU.add, apply_absolute_value=True
                                  ).then_inc(ffn_step, 1)
            dve.wait_ge(p_ffn_ps, 1)
            dve.tensor_scalar(wsc[:, :], ps[:, NJOBS % 8, 0:3], 1.0 / (F * D), EPS, ALU.mult, ALU.max).then_inc(ffn_step, 1)
            dve.wait_ge(ffn_step, 4)
            dve.tensor_scalar(wthr[:, 0:3], wsc[:, :], 0.5, None, ALU.mult).then_inc(ffn_step, 1)
            dve.tensor_scalar(wthr[:, 3:6], wsc[:, :], -0.5, None, ALU.mult).then_inc(ffn_step, 1)
            for n, w in enumerate((gate_w, up_w, down_w)):
                dve.wait_ge(ffn_step, 6 + 2 * n)
                dve.tensor_scalar(wlow[:, :], wst[n][:, :], wthr[:, 3 + n:4 + n], None, ALU.is_lt).then_inc(ffn_step, 1)
                dve.wait_ge(ffn_step, 7 + 2 * n)
                dve.scalar_tensor_tensor(w[:, :, :].rearrange("p c n -> p (c n)"), wst[n][:, :], wthr[:, n:n + 1],
                                         wlow[:, :], ALU.is_gt, ALU.subtract, saturate=False).then_inc(ffn_step, 1)
            dve.wait_ge(ffn_step, 12)
            dve.sem_inc(ffn_done, 1)
            dve.wait_ge(in_weights, 160)

            with dve.Fori(0, B) as i:
                steps = [0]

                def step(ins):
                    steps[0] += 1
                    ins.then_inc(sems["dve_step"], 1)

                def settle():
                    dve.wait_ge(sems["dve_step"], at("dve_step", i, steps[0]))

                def ln_stats(n, src):
                    step(dve.bn_stats(stats[:, n, :], src))
                    settle()
                    apart(dve)
                    dve.bn_aggr(mv[:, n, :], stats[:, n, :]).then_inc(sems["mv"], 1)

                def ln_normalise(n, src):
                    dve.wait_ge(sems["rstd"], at("rstd", i, n + 1))
                    dve.wait_ge(sems["xt_ps"], at("xt_ps", i, n - 1))
                    dve.tensor_scalar(xn[:, n % 2, :], src, mv[:, n, 0:1], rstd[:, n:n + 1], ALU.subtract, ALU.mult
                                      ).then_inc(sems["xn"], 1)

                dve.wait_ge(sems["x_in"], at("x_in", i, 16))
                dve.wait_ge(sems["y"], at("y", i, 0))
                for t in range(NT):
                    ln_stats(t, xin[:, t, :])
                for t in range(NT):
                    ln_normalise(t, xin[:, t, :])
                for j in range(3):
                    dve.wait_ge(sems["proj"], at("proj", i, 2 * j + 2))
                    if j:
                        dve.wait_ge(sems["rope_l"], at("rope_l", i, 2 * j))
                    for v in range(4):
                        b = 2 + (2 * j + v % 2) % 6
                        dve.tensor_tensor(rot[:, v, :], ps[:, b, :], rope_sb[:, (v + v // 2) % 2, :], ALU.mult
                                          ).then_inc(sems["rope_m"], 1)
                    for odd in range(2):
                        dve.wait_ge(sems["rope_h"], at("rope_h", i, 2 * j + odd + 1))
                        dve.tensor_tensor(parts[:, 2 + odd, :], rot[:, 2 * odd, :], parts[:, odd, :].bitcast(F32),
                                          ALU.subtract).then_inc(sems["rope_l"], 1)
                for n in range(4 * NT):
                    t, hq = n // 4, n % 4
                    dve.wait_ge(sems["smax_ps"], at("smax_ps", i, n + 1))
                    b0 = 4 * (n % 2)
                    dve.tensor_reduce(negmax[:, t, 4 * hq:4 * hq + 4], ps[:, b0:b0 + 4, :], AX.X, ALU.max, negate=True
                                      ).then_inc(sems["smax"], 1)
                    if hq == 3:
                        dve.wait_ge(sems["smax"], at("smax", i, n + 1))
                        step(dve.tensor_copy(negsplit[:, t, 0:H], negmax[:, t, :]))
                        settle()
                        dve.tensor_tensor(negsplit[:, t, H:2 * H], negmax[:, t, :], negsplit[:, t, 0:H].bitcast(F32),
                                          ALU.subtract).then_inc(sems["nms"], 1)
                for p in range(HP):
                    b = 6 + p % 2
                    dve.wait_ge(sems["pv"], at("pv", i, 2 * p + 2))
                    if p:
                        dve.wait_ge(sems["at"], at("at", i, p))
                    step(dve.reciprocal(rcp[:, :], ps[64:128, b, :]))
                    settle()
                    r0 = 64 * (p % 2)
                    dve.tensor_tensor(aT[r0:r0 + 64, p // 2, :], ps[0:64, b, :], rcp[:, :], ALU.mult
                                      ).then_inc(sems["at"], 1)
                for t in range(NT):
                    dve.wait_ge(sems["wo_ps"], at("wo_ps", i, t + 1))
                    dve.tensor_tensor(xcur[:, t, :], ps[:, t, :], xin[:, t, :], ALU.add).then_inc(sems["x1"], 1)
                for t in range(NT):
                    dve.wait_ge(sems["x1"], at("x1", i, t + 1))
                    ln_stats(4 + t, xcur[:, t, :])
                for t in range(NT):
                    ln_normalise(4 + t, xcur[:, t, :])

                def rotate_queries(half):
                    if half:
                        dve.wait_ge(sems["sc_ps"], at("sc_ps", i, 2))
                    for p in range(HP):
                        m = HP * half + p
                        dve.wait_ge(sems["xr_ps"], at("xr_ps", i, m + 1))
                        q = slice(256 * half, 256 * half + 256)
                        dve.tensor_tensor(xc[:, p, :], ps[:, m % 4, 0:256], rope_sb[:, 2, q], ALU.mult)
                        dve.tensor_tensor(xs[:, p, :], ps[:, m % 4, 0:256], rope_sb[:, 3, q], ALU.mult
                                          ).then_inc(sems["xcs"], 1)

                def mask_and_centre(t):
                    dve.wait_ge(sems["sc_ps"], at("sc_ps", i, t + 1))
                    if t == 0:
                        dve.wait_ge(sems["maskt"], at("maskt", i, 1))
                    if t >= 2:
                        dve.wait_ge(sems["pt_ps"], at("pt_ps", i, 2 * (t - 1)))
                    b0 = 4 + 2 * (t % 2)
                    e = ex[:, t % 2, :, :]
                    dve.tensor_tensor(e, ps[:, b0:b0 + 2, :].rearrange("p b (h k) -> p (b h) k", k=LK),
                                      maskt[:, t:t + 1, :].broadcast_to([P, H, LK]), ALU.add).then_inc(sems["masked"], 1)
                    dve.wait_ge(sems["masked"], at("masked", i, t + 1))
                    step(dve.tensor_reduce(xmax[:, t, :], e, AX.X, ALU.max))
                    settle()
                    dve.tensor_tensor(e, e, xmax[:, t, :].unsqueeze(2).broadcast_to([P, H, LK]), ALU.subtract
                                      ).then_inc(sems["centred"], 1)

                def denominators(t):
                    dve.wait_ge(sems["xexp"], at("xexp", i, t + 1))
                    step(dve.tensor_reduce(xsum[:, t, :], ex[:, t % 2, :, :], AX.X, ALU.add))
                    settle()
                    dve.reciprocal(xrec[:, t, :], xsum[:, t, :]).then_inc(sems["xden"], 1)

                def residual2(t):
                    dve.wait_ge(sems["xo_ps"], at("xo_ps", i, t + 1))
                    dve.tensor_tensor(xcur[:, t, :], ps[:, 2 + t % 2, :], xcur[:, t, :], ALU.add).then_inc(sems["x2"], 1)

                rotate_queries(0)
                mask_and_centre(0)
                mask_and_centre(1)
                denominators(0)
                rotate_queries(1)
                denominators(1)
                mask_and_centre(2)
                residual2(0)
                denominators(2)
                mask_and_centre(3)
                residual2(1)
                denominators(3)
                residual2(2)
                residual2(3)

                def ffn_ln(t):
                    dve.wait_ge(sems["x2"], at("x2", i, t + 1))
                    ln_stats(8 + t, xcur[:, t, :])
                    ln_normalise(8 + t, xcur[:, t, :])

                def scales(s, t, src, c, weights):
                    step(dve.tensor_reduce(s[:, t, 0:1], src, AX.X, ALU.max, apply_absolute_value=True))
                    settle()
                    step(dve.tensor_scalar(s[:, t, 1:2], s[:, t, 0:1], c, EPS, ALU.mult, ALU.max))
                    settle()
                    step(dve.reciprocal(s[:, t, 4:5], s[:, t, 1:2]))
                    for k, w in enumerate(weights):
                        step(dve.tensor_scalar(s[:, t, 5 + k:6 + k], s[:, t, 1:2], wsc[:, w:w + 1],
                                               (0.5 if w == 0 else 1.0) / 127.0, ALU.mult, ALU.mult))
                    settle()
                    if len(weights) == 2:
                        step(dve.tensor_copy(s[:, t, 3:4], s[:, t, 5:6]))
                        step(dve.tensor_tensor(s[:, t, 7:8], s[:, t, 5:6], s[:, t, 6:7], ALU.mult))
                    return dve.tensor_scalar(s[:, t, 2:3], s[:, t, 4:5], 127.0 * c, None, ALU.mult)

                def ffn_scales(t):
                    dve.wait_ge(sems["had_ps"], at("had_ps", i, t + 1))
                    scales(fs, t, ps[:, 1, :], C512, (0, 1)).then_inc(sems["fsc"], 1)

                def ffn_int(t):
                    dve.wait_ge(sems["fround"], at("fround", i, t + 1))
                    if t:
                        dve.wait_ge(sems["fintT_ps"], at("fintT_ps", i, t))
                    dve.tensor_scalar(fq[:, :], fv[:, :], MAGIC, None, ALU.subtract).then_inc(sems["fint"], 1)

                def ffn_hidden(t):
                    if t:
                        dve.wait_ge(sems["hidT_ps"], at("hidT_ps", i, FG * t))
                    for g in range(FG):
                        n = FG * t + g
                        b = 2 * (g % 2)
                        dve.wait_ge(sems["th"], at("th", i, n + 1))
                        dve.wait_ge(sems["hid"], at("hid", i, n))
                        step(dve.scalar_tensor_tensor(gw[:, :], th[:, :], 1.0, ps[:, b, :], ALU.add, ALU.mult))
                        settle()
                        dve.scalar_tensor_tensor(hid[:, g, :], gw[:, :], fs[:, t, 7:8], ps[:, b + 1, :],
                                                 ALU.mult, ALU.mult).then_inc(sems["hid"], 1)

                def ffn_add2(t):
                    dve.wait_ge(sems["add1"], at("add1", i, t + 1))
                    dve.tensor_tensor(hid[:, 0:2, :], sd[:, :, 0, :], sd[:, :, 1, :], ALU.add)
                    dve.tensor_tensor(hid[:, 2:4, :], sd[:, :, 0, :], sd[:, :, 1, :], ALU.subtract).then_inc(sems["add2"], 1)

                def ffn_scales2(t):
                    dve.wait_ge(sems["had2_ps"], at("had2_ps", i, t + 1))
                    scales(f2s, t, ps[:, 4:8, :].rearrange("p b q -> p (b q)"), C2048, (2,)).then_inc(sems["f2sc"], 1)

                def ffn_int2(t):
                    dve.wait_ge(sems["f2round"], at("f2round", i, t + 1))
                    if t:
                        dve.wait_ge(sems["f2intT_ps"], at("f2intT_ps", i, 2 * t))
                    dve.tensor_scalar(f2q[:, :], f2v[:, :], MAGIC, None, ALU.subtract).then_inc(sems["f2int"], 1)

                def ffn_out(t):
                    dve.wait_ge(sems["down_ps"], at("down_ps", i, t + 1))
                    n = f"store{t % 2}"
                    dve.wait_ge(sems[n], at(n, i, 16 * (t // 2)))
                    dve.scalar_tensor_tensor(yo[:, t % 2, :], ps[:, 2, :], f2s[:, t, 5:6], xcur[:, t, :],
                                             ALU.mult, ALU.add).then_inc(sems["y"], 1)

                ffn_ln(0)
                ffn_scales(0)
                ffn_int(0)
                ffn_hidden(0)
                ffn_add2(0)
                for t in range(NT):
                    more = t + 1 < NT
                    if more:
                        ffn_ln(t + 1)
                        ffn_scales(t + 1)
                        ffn_int(t + 1)
                    ffn_scales2(t)
                    ffn_int2(t)
                    if more:
                        ffn_hidden(t + 1)
                        ffn_add2(t + 1)
                    ffn_out(t)
                assert steps[0] == PER["dve_step"], steps

        @block.gpsimd
        def _(pool):
            pool.memset(mhalf[:, :], -0.5).then_inc(sems["pool_step"], 1)
            pool.memset(ones[:, :], 1.0).then_inc(p_const, 1)
            pool.memset(kd_all[:, :, :, :], 0.0).then_inc(p_kzero, 1)
            pool.wait_ge(ffn_done, 1)
            pool.memset(vw[:, :, :], 0.0).then_inc(vw_zero, 1)
            pool.wait_ge(vw_zero, 1)
            pool.memset(vw[:, :, 0:G * P].rearrange("p t (g c) -> p t g c", c=P)[:, :, :, 96:128], 1.0).then_inc(vw_const, 1)
            with pool.Fori(0, B) as i:
                steps = [1]

                def step(ins):
                    steps[0] += 1
                    ins.then_inc(sems["pool_step"], 1)

                def settle():
                    pool.wait_ge(sems["pool_step"], at("pool_step", i, steps[0]))
                    apart(pool)

                def rsqrt(n):
                    pool.wait_ge(sems["mv"], at("mv", i, n + 1))
                    apart(pool)
                    step(pool.tensor_scalar(vare[:, n:n + 1], mv[:, n, 1:2], EPS, None, ALU.add))
                    settle()
                    pool.tensor_tensor(rstd[:, n:n + 1], vare[:, n:n + 1], mhalf[:, :], ALU.pow).then_inc(sems["rstd"], 1)

                for t in range(NT):
                    rsqrt(t)
                pool.wait_ge(sems["y"], at("y", i, 0))
                pool.wait_ge(sems["rstd"], at("rstd", i, 4))
                apart(pool)
                pool.memset(ks[96:98, :, :].bitcast(F32), 1.0).then_inc(sems["ks_ones"], 1)
                pool.wait_ge(sems["ks_ones"], at("ks_ones", i, 1))
                apart(pool)
                for j in range(3):
                    pool.wait_ge(sems["rope_m"], at("rope_m", i, 4 * j + 4))
                    apart(pool)
                    pool.tensor_tensor(rot[:, 0, :], rot[:, 0, :], rot[:, 1, :], ALU.subtract).then_inc(sems["rope_c"], 1)
                    pool.tensor_tensor(rot[:, 2, :], rot[:, 2, :], rot[:, 3, :], ALU.add).then_inc(sems["rope_c"], 1)
                pool.wait_ge(sems["seg_in"], at("seg_in", i, 16))
                pool.wait_ge(sems["masked"], at("masked", i, 0))
                apart(pool)
                step(pool.tensor_copy(seg_f[:, :], seg_i[:, :]))
                settle()
                step(pool.tensor_scalar(seg_8[:, :], seg_f[:, :], -8.0, None, ALU.add))
                settle()
                for t in range(NT):
                    pool.tensor_scalar(maskt[:, t, :], iota_sb[:, :], seg_f[:, t:t + 1], NEG, ALU.is_gt, ALU.mult)
                    step(pool.tensor_scalar(mask_lo[:, :], iota_sb[:, :], seg_8[:, t:t + 1], NEG, ALU.is_lt, ALU.mult))
                    settle()
                    last = pool.tensor_tensor(maskt[:, t, :], maskt[:, t, :], mask_lo[:, :], ALU.add)
                    if t < NT - 1:
                        step(last)
                        settle()
                last.then_inc(sems["maskt"], 1)
                for t in range(NT):
                    rsqrt(4 + t)

                def normalise(t):
                    pool.wait_ge(sems["xden"], at("xden", i, t + 1))
                    apart(pool)
                    e = ex[:, t % 2, :, :]
                    pool.tensor_tensor(e, e, xrec[:, t, :].unsqueeze(2).broadcast_to([P, H, LK]), ALU.mult
                                       ).then_inc(sems["xprob"], 1)

                for t in range(NT):
                    normalise(t)

                def add1(t):
                    pool.wait_ge(sems["hid"], at("hid", i, FG * t + FG))
                    apart(pool)
                    if t:
                        pool.wait_ge(sems["f2int"], at("f2int", i, t))
                        apart(pool)
                    a = hid[:, :, :].rearrange("p (r u) n -> p r u n", u=2)
                    pool.tensor_tensor(sd[:, 0, :, :], a[:, :, 0, :], a[:, :, 1, :], ALU.add)
                    pool.tensor_tensor(sd[:, 1, :, :], a[:, :, 0, :], a[:, :, 1, :], ALU.subtract).then_inc(sems["add1"], 1)

                rsqrt(8)
                add1(0)
                for t in range(1, NT):
                    rsqrt(8 + t)
                    add1(t)
                assert steps[0] - 1 == PER["pool_step"], steps


V0 = 3 + 2 * H
A0 = V0 + 4 * H
NJOBS = A0 + 2 * H


def _jobs():
    jobs, count = [], {"act": 0, "dve": 0}
    for n in range(NJOBS):
        if n == 0 or 3 <= n < 3 + H:
            s = "act"
        elif n in (1, 2) or 3 + H <= n < V0:
            s = "dve"
        elif n < A0:
            s = "dve" if (n - V0) % 2 else "act"
        else:
            s = "act" if (n - A0) % 2 else "dve"
        count[s] += 1
        jobs.append((s, count[s]))
    return jobs, count


PJOBS, _COUNT = _jobs()
NACT, NDVE = _COUNT["act"], _COUNT["dve"]
NN_DVE = PJOBS[V0 - 1][1]
PV_ACT = {m: PJOBS[V0 + m][1] for m in range(4 * H)}
PV_DVE = PV_ACT


def _tables(np):
    f = np.float32
    had = np.array([[1.0]], f)
    while had.shape[0] < D:
        had = np.block([[had, had], [had, -had]]).astype(f)
    inv = (f(1.0) / np.power(f(10000.0), np.arange(0, HD, 2, dtype=f) / f(HD))).astype(f)
    ang = (np.arange(S, dtype=f)[:, None] * inv[None, :]).T.astype(f)
    selfrope = np.stack([np.cos(ang), np.sin(ang)]).repeat(8, axis=1)
    inv2 = (f(1.0) / np.power(f(10000.0), np.arange(R // 2, dtype=f) / f(R // 2))).astype(f)
    ang2 = (np.arange(S, dtype=f)[:, None] * inv2[None, :]).T.astype(f)
    xrope = np.tile(np.stack([np.cos(ang2), np.sin(ang2)]), (1, 4, 1))
    rope = np.concatenate([selfrope, xrope]).transpose(1, 0, 2).astype(f)
    c, s = np.cos(ang2[:, :LK]), np.sin(ang2[:, :LK])
    krope = np.stack([np.concatenate([c, c]), np.concatenate([-s, s]), np.concatenate([s, s]),
                      np.concatenate([c, -c])])
    krope = np.tile(krope, (1, 2, 1)).transpose(1, 0, 2).astype(f)
    iota = np.tile(np.arange(LK, dtype=f), (P, 1))
    return dict(had=had, rope=rope, krope=krope, iota=iota, ident=np.eye(P, dtype=f))


def kernel(x, ctx_2048, itok_BxS_0_1023, L0_attn_wq, L0_attn_wk, L0_attn_wv, L0_attn_wo, L0_xattn_W_kvc,
           L0_xattn_W_dq, L0_xattn_W_uq, L0_xattn_W_qr, L0_xattn_W_uk, L0_xattn_W_kr, L0_xattn_W_uv,
           L0_xattn_W_o, L0_ffn_w_gate, L0_ffn_w_up, L0_ffn_w_down):
    import numpy as np
    import concourse.bacc as bacc
    from concourse.bass_utils import run_bass_kernel_spmd as run

    a = np.asarray
    wkr = a(L0_xattn_W_kr)
    swapped = np.concatenate([wkr[:, R // 2:], wkr[:, :R // 2]], axis=1)
    data = dict(
        x=a(x),
        seg=a(itok_BxS_0_1023).reshape(B, NT, P).transpose(0, 2, 1),
        ctxT=a(ctx_2048).reshape(B * LK, D).T,
        wq=a(L0_attn_wq).reshape(D, 2, 8, HD // 2, 2).transpose(0, 1, 4, 3, 2).reshape(D, D),
        wk=a(L0_attn_wk).reshape(D, G, HD // 2, 2).transpose(0, 3, 2, 1).reshape(D, G * HD),
        wv=a(L0_attn_wv), wo=a(L0_attn_wo), wkvc=a(L0_xattn_W_kvc), wdq=a(L0_xattn_W_dq),
        wuqT=a(L0_xattn_W_uq).T, wqr=a(L0_xattn_W_qr), wukT=a(L0_xattn_W_uk).T,
        wkr2=np.concatenate([wkr, wkr], axis=1), wkrs2=np.concatenate([swapped, swapped], axis=1),
        wuvT=a(L0_xattn_W_uv).T, wox=a(L0_xattn_W_o),
        gateT=a(L0_ffn_w_gate).T, upT=a(L0_ffn_w_up).T, downT=a(L0_ffn_w_down).T,
        **_tables(np),
    )
    nc = bacc.Bacc("TRN2", target_bir_lowering=False, num_devices=1)
    arrays, args = {}, {}
    for name, v in data.items():
        v = np.ascontiguousarray(v)
        arrays[f"in_{name}"] = v
        args[name] = nc.dram_tensor(f"in_{name}", v.shape, mybir.dt.from_np(v.dtype), kind="ExternalInput").ap()
    out = nc.dram_tensor("out_0", (B, S, D), F32, kind="ExternalOutput").ap()
    block_kernel(nc, out=out, **args)
    r = run(nc, [arrays], core_ids=[0])
    return r.results[0]["out_0"]
```

```python
from contextlib import ExitStack

import concourse.bass as bass
from concourse import mybir

P = 128
F32 = mybir.dt.float32
F32R = mybir.dt.float32r
BF16 = mybir.dt.bfloat16
F8 = mybir.dt.float8e4
I32 = mybir.dt.int32
ALU = mybir.AluOpType
ACT = mybir.ActivationFunctionType
AX = mybir.AxisListType

B, S, D = 8, 512, 512
NT = S // P
KC = D // P
H, G, HD = 16, 8, 32
LK, KVC, QC, R = 64, 128, 192, 64
QC1 = QC - P
HP = H // 2
F = 2048
FC = F // P
FG = F // 512
EPS = 1e-5
NEG = -1e30
MAGIC = 12582912.0
SELF_SCALE = float(HD) ** -0.5
X_SCALE = float(P + R) ** -0.5
C512 = float(D) ** -0.5
C2048 = float(F) ** -0.5
NCOPY = 6

PER = dict(
    x_in=16, seg_in=16, stack=3 * NCOPY * 16, rows_in=64, v_in=16, ak_in=48, store0=32, store1=32,
    mv=12, rstd=12, xn=12, xt_ps=12, xt=12,
    proj=6, v_ps=4, vw=4, rope_m=12, rope_cv=4, rope_c=2, rope_h=6, rope_l=6,
    smax_ps=32, smax=32, nms=2, nmt_ps=2, nmt=2,
    st_ps=32, probs=32, pv=16, at=8, wo_ps=4, x1=4,
    dq_ps=2, qc=2, xr_ps=16, xcs=16, sc_ps=4, masked=4, centred=4, xexp=4, xden=4, xprob=4,
    pt_ps=8, ptx=8, xo_ps=4, x2=4, maskt=1, ks_ones=1,
    had_ps=4, fsc=4, fround=4, fint=4, fintT_ps=4, fintT=4, gate_ps=16, up_ps=16, th=16, gated=16, hid=16,
    xt_lo=4, sum1=4, diff1=4, sum2=4, diff2=4, hidT_ps=16, hidT=16, hidT_lo=16, had2_ps=16, f2sc=4, f2round=8, f2int=8,
    f2intT_ps=8, f2intT=8, down_ps=4, y=4,
    dve_step=98, pool_step=21,
)


def block_kernel(nc, x, seg, ctxT, wq, wk, wv, wo, wkvc, wdq, wuqT, wqr, wukT, wkr2, wkrs2, wuvT, wox,
                 gateT, upT, downT, had, rope, krope, iota, ident, out):
    ctx = ExitStack()
    with ctx:
        base = 16512
        at_byte = [base]

        def place(name, shape, dt, offset=None):
            size = 1
            for n in shape[1:]:
                size *= n
            size *= {F32: 4, F32R: 4, I32: 4, BF16: 2, F8: 1}[dt]
            if offset is None:
                offset = at_byte[0]
                at_byte[0] += (size + 31) // 32 * 32
            return nc.alloc_sbuf_tensor_at(name, shape, dt, offset=offset)

        wq_sb = place("wq_sb", [P, KC, D], F32)
        wk_sb = place("wk_sb", [P, KC, G * HD], F32)
        wv_sb = place("wv_sb", [P, KC, G * HD], F32)
        wo_sb = place("wo_sb", [P, KC, D], F32)
        wdq_sb = place("wdq_sb", [P, KC, QC], F32)
        wqr0 = place("wqr0", [P, H * R], F32)
        wqr1 = place("wqr1", [QC1, H * R], F32)
        had_sb = place("had_sb", [P, KC, D], F32R)
        ffn_at = at_byte[0]
        gate_w = place("gate_w", [P, KC, F], F8)
        up_w = place("up_w", [P, KC, F], F8)
        down_w = place("down_w", [P, FC, D], F8)
        rope_sb = place("rope_sb", [P, 4, S], F32)
        ident_f = place("ident_f", [P, P], F32)
        ident_b = place("ident_b", [P, P], BF16)
        iota_sb = place("iota_sb", [P, LK], F32)
        ones_at = at_byte[0]
        maskt = place("maskt", [P, NT, LK], F32)
        mask_lo = place("mask_lo", [P, LK], F32)
        xcur_at = at_byte[0]
        xcur = place("xcur", [P, NT, D], F32)
        had_in = place("had_in", [P, KC, D], F32, xcur_at)
        xin_at = at_byte[0]
        xin = place("xin", [P, NT, D], F32)
        seg_i = place("seg_i", [P, NT], I32)
        seg_f = place("seg_f", [P, NT], F32)
        seg_8 = place("seg_8", [P, NT], F32)
        stats = place("stats", [P, 12, 6], F32)
        mv = place("mv", [P, 12, 2], F32)
        vare = place("vare", [P, 12], F32)
        rstd = place("rstd", [P, 12], F32)
        mhalf = place("mhalf", [P, 1], F32)
        negmax = place("negmax", [P, NT, H], F32)
        negsplit = place("negsplit", [P, 2, NT, H], F32R)
        xmax = place("xmax", [P, NT, H], F32)
        xsum = place("xsum", [P, NT, H], F32)
        xrec = place("xrec", [P, NT, H], F32)
        fs = place("fs", [P, NT, 8], F32)
        f2s = place("f2s", [P, NT, 8], F32)
        gmax = place("gmax", [P, NT, FG], F32)
        wsum = place("wsum", [P, 3], F32)
        wsc = place("wsc", [P, 3], F32)
        wthr = place("wthr", [P, 6], F32)
        ones = place("ones", [P, P], F32, ones_at)
        arena = at_byte[0]
        A_ROPE, A_Q = arena, arena + 16384
        A_K = A_Q + 32768
        A_V = A_K + 16384
        A_P = A_V + 4 * (G * P + 32) * 4
        A_XT = A_P + 16384
        A_XN = A_XT + 8192
        A_RC = A_XN + 4096
        assert A_RC + 2048 <= 229344, A_RC + 2048 - 229344

        rot = place("rot", [P, 4, S], F32, A_ROPE)
        parts = place("parts", [P, 4, S], F32R, A_ROPE + 8192)
        qs = place("qs", [P, H, S], F32R, A_Q)
        ks = place("ks", [P, G, S], F32R, A_K)
        vw = place("vw", [P, NT, G * P + 32], F32, A_V)
        pt = place("pt", [P, 4, 1024], F32, A_P)
        rcp = place("rcp", [64, S], F32, A_RC)
        xT = place("xT", [P, KC, S], F32, A_XT)
        aT = place("aT", [P, KC, S], F32, A_XT)
        xn = place("xn", [P, 2, D], F32, A_XN)
        rows = place("rows", [H, S], F32R, A_XN)
        vp = place("vp", [P, HP, D], F32, A_ROPE)
        xc = place("xc", [P, HP, 256], F32, A_Q)
        xs = place("xs", [P, HP, 256], F32, A_Q + 8192)
        ex = place("ex", [P, 2, H, LK], F32, A_Q + 16384)
        ptx = place("ptx", [P, HP, P], F32, A_Q + 24576)
        qc0 = place("qc0", [P, S], F32, A_Q + 28672)
        qc1 = place("qc1", [QC1, S], F32, A_Q + 30720)
        ak0 = place("ak0", [P, H * LK], F32, A_K)
        ak1 = place("ak1", [QC1, H * LK], F32, A_K + 4096)
        kd = place("kd", [P, 2, P], F32, A_K + 8192)
        xT3 = place("xT3", [P, KC, P], F32R, A_K + 9216)
        xT3_lo = place("xT3_lo", [P, KC, P], F32R, A_RC)
        fv = place("fv", [P, D], F32, A_K + 11264)
        fq = place("fq", [P, D], BF16, A_K + 13312)
        fqT = place("fqT", [P, KC, P], BF16, A_K + 14336)
        hid = [place(f"hid{n}", [P, FG, 512], F32, (A_P, A_K)[n]) for n in range(2)]
        sd = place("sd", [P, 2, 2, 512], F32, A_P + 8192)
        th = place("th", [P, 2, 512], F32, A_Q + 8192)
        gw = place("gw", [P, 2, 512], F32, A_Q + 12288)
        hidT = place("hidT", [P, FC, P], F32R, A_Q)
        hidT_lo = place("hidT_lo", [P, FC, P], F32R, A_Q + 16384)
        f2q = place("f2q", [P, F], BF16, A_Q + 24576)
        f2qT = place("f2qT", [P, FC, P], BF16, A_Q + 28672)
        wox_sb = place("wox_sb", [P, H, D], F32, arena)
        nn = place("nn", [P, H, D], F32, arena + 32768)
        wukT_sb = place("wukT_sb", [P, H, KVC], F32, arena + 65536)
        wuqT_sb = place("wuqT_sb", [P, H, QC], F32, arena + 73728)
        wuvT_sb = place("wuvT_sb", [P, H, KVC], F32, arena + 86016)
        mt = place("mt", [P, H, QC], F32, arena + 94208)
        kd_all = place("kd_all", [P, B, 2, P], F32, arena + 106496)
        ast0 = place("ast0", [P, B, H, LK], F32, arena)
        ast1 = place("ast1", [QC1, B, H, LK], F32, arena + 32768)
        vst = place("vst", [P, 4, D], F32, ffn_at)
        ktmp = place("ktmp", [P, 4, D], F32, ffn_at + 8192)
        ctxT_sb = place("ctxT_sb", [P, KC, D], F32, xcur_at)
        wkvc_sb = place("wkvc_sb", [P, KC, KVC], F32, xin_at)
        kvT = place("kvT", [P, B * LK], F32, xin_at + 2048)
        wkr_sb = place("wkr_sb", [P, 2, P], F32, xin_at + 4096)
        krope_sb = place("krope_sb", [P, 4, LK], F32, xin_at + 5120)
        wst = [place(f"wst{n}", [P, KC * F], F32, arena + 32768 * n) for n in range(3)]
        wlow = place("wlow", [P, KC * F], BF16, arena + 98304)

        ps = ctx.enter_context(nc.psum_tensor("ps", [P, 8, 512], F32))

        v_dram = nc.dram_tensor("v_scratch", [B, H, LK, D], F32, kind="Internal").ap()
        a0_dram = nc.dram_tensor("a0_scratch", [B, P, H * LK], F32, kind="Internal").ap()
        a1_dram = nc.dram_tensor("a1_scratch", [B, QC1, H * LK], F32, kind="Internal").ap()
        k_dram = nc.dram_tensor("k_scratch", [B, P, 2 * P], F32, kind="Internal").ap()

        sems = {n: ctx.enter_context(nc.semaphore(n)) for n in PER}

        def psem(name):
            return ctx.enter_context(nc.semaphore(name))

        in_weights, in_kv, in_ffn, in_const = psem("in_weights"), psem("in_kv"), psem("in_ffn"), psem("in_const")
        p_ps, p_act, p_dve, p_ffn_ps = psem("p_ps"), psem("p_act"), psem("p_dve"), psem("p_ffn_ps")
        p_vstore = [psem(f"p_vstore{n}") for n in range(4)]
        p_store = psem("p_store")
        ffn_step, p_const, kv_done = psem("ffn_step"), psem("p_const"), psem("kv_done")
        p_kzero, ffn_done, vw_const, vw_zero = psem("p_kzero"), psem("ffn_done"), psem("vw_const"), psem("vw_zero")
        passed, in_had, had_ready = psem("passed"), psem("in_had"), psem("had_ready")

        def at(name, i, k):
            return i * PER[name] + (PER[name] + k)

        def apart(eng):
            eng.sem_inc(passed, 1)

        block = ctx.enter_context(nc.Block())

        @block.sync
        def _(sp):
            for name in PER:
                sp.sem_inc(sems[name], PER[name])
            for dst, src in (
                (ctxT_sb[:, :, :], ctxT.rearrange("(c p) n -> p c n", p=P)),
                (wkvc_sb[:, :, :], wkvc.rearrange("(c p) n -> p c n", p=P)),
                (wkr_sb[:, 0, :], wkr2), (wkr_sb[:, 1, :], wkrs2),
                (krope_sb[:, :, :], krope), (ident_f[:, :], ident),
                (wukT_sb[:, :, :], wukT.rearrange("(h p) n -> p h n", p=P)),
                (wuqT_sb[:, :, :], wuqT.rearrange("(h p) n -> p h n", p=P)),
                (wuvT_sb[:, :, :], wuvT.rearrange("(h p) n -> p h n", p=P)),
                (wox_sb[:, :, :], wox.rearrange("(h p) n -> p h n", p=P)),
            ):
                sp.dma_start(dst, src).then_inc(in_kv, 16)
            for dst, src in (
                (wq_sb[:, :, :], wq.rearrange("(c p) n -> p c n", p=P)),
                (wk_sb[:, :, :], wk.rearrange("(c p) n -> p c n", p=P)),
                (wv_sb[:, :, :], wv.rearrange("(c p) n -> p c n", p=P)),
                (wo_sb[:, :, :], wo.rearrange("(c p) n -> p c n", p=P)),
                (wdq_sb[:, :, :], wdq.rearrange("(c p) n -> p c n", p=P)),
                (wqr0[:, :], wqr[0:P, :]), (wqr1[:, :], wqr[P:QC, :]),
                (rope_sb[:, :, :], rope), (iota_sb[:, :], iota),
            ):
                sp.dma_start(dst, src).then_inc(in_weights, 16)
            for n in range(4 * H):
                bp, h = n // H, n % H
                sp.wait_ge(p_dve if n % 2 else p_act, PV_DVE[n] if n % 2 else PV_ACT[n])
                sp.dma_start(v_dram[2 * bp:2 * bp + 2, h, :, :],
                             vst[:, n % 4, :]).then_inc(p_vstore[n % 4], 16)
            sp.wait_ge(kv_done, 2)
            sp.dma_start(a0_dram.rearrange("b p n -> p b n"),
                         ast0[:, :, :, :].rearrange("p b h k -> p b (h k)")).then_inc(p_store, 16)
            sp.dma_start(a1_dram.rearrange("b p n -> p b n"),
                         ast1[:, :, :, :].rearrange("p b h k -> p b (h k)")).then_inc(p_store, 16)
            sp.dma_start(k_dram.rearrange("b p n -> p b n"),
                         kd_all[:, :, :, :].rearrange("p b t n -> p b (t n)")).then_inc(p_store, 16)
            for n in range(4):
                sp.wait_ge(p_vstore[n], 16 * H)
            sp.wait_ge(p_store, 48)
            for n, w in enumerate((gateT.rearrange("(c p) n -> p c n", p=P), upT.rearrange("(c p) n -> p c n", p=P),
                                   downT.rearrange("(c p) n -> p c n", p=P))):
                sp.dma_start(wst[n][:, :].rearrange("p (c n) -> p c n", n=w.shape[2]), w).then_inc(in_ffn, 16)
            sp.dma_start(had_in[:, :, :], had.rearrange("(c p) n -> p c n", p=P)).then_inc(in_had, 16)
            sp.dma_start(xin[:, :, :], x[0, :, :].rearrange("(t p) d -> p t d", p=P)).then_inc(sems["x_in"], 16)

            def stack(i, j, ahead=0):
                dst = ks[:, :, :] if j == 0 else qs[:, G * (j - 1):G * j, :]
                kinds = (0, 0, 1) if j == 0 else (0, 1, 0)
                for kind in range(2):
                    name = "rope_l" if kind else "rope_h"
                    sp.wait_ge(sems[name], at(name, i, ahead * 6 + 2 * j + 2))
                    for c in range(3):
                        if kinds[c] != kind:
                            continue
                        for odd in range(2):
                            r0 = 32 * c + 16 * odd
                            sp.dma_start(dst[r0:r0 + 16, :, :].bitcast(F32),
                                         parts[:, 2 * kind + odd, :].bitcast(F32)).then_inc(sems["stack"], 16)
            stack(0, 0)
            stack(0, 1)

            def batch_row(i, more):
                def row(t):
                    return t[bass.ds(i, 1)]
                sp.wait_ge(sems["maskt"], at("maskt", i, 0))
                apart(sp)
                sp.dma_start(seg_i[:, :], row(seg).rearrange("o p t -> (o p) t")).then_inc(sems["seg_in"], 16)
                sp.wait_ge(sems["y"], at("y", i, 0))
                apart(sp)
                stack(i, 2)
                for hg in range(2):
                    sp.wait_ge(sems["nmt"], at("nmt", i, hg + 1))
                    for part in range(2):
                        sp.dma_start(qs[96 + part:97 + part, 8 * hg:8 * hg + 8, :].bitcast(F32),
                                     rows[8 * part:8 * part + 8, :].bitcast(F32)).then_inc(sems["rows_in"], 16)
                    if hg == 0:
                        sp.wait_ge(sems["stack"], at("stack", i, PER["stack"]))
                        sp.dma_start(vp[:, :, :], row(v_dram).rearrange("o (c u) k n -> (o u k) c n", u=2)
                                     ).then_inc(sems["v_in"], 16)
                sp.wait_ge(sems["st_ps"], at("st_ps", i, PER["st_ps"]))
                sp.dma_start(ak0[:, :], row(a0_dram).rearrange("o p n -> (o p) n")).then_inc(sems["ak_in"], 16)
                sp.dma_start(ak1[:, :], row(a1_dram).rearrange("o p n -> (o p) n")).then_inc(sems["ak_in"], 16)
                sp.dma_start(kd[:, :, :].rearrange("p t n -> p (t n)"),
                             row(k_dram).rearrange("o p n -> (o p) n")).then_inc(sems["ak_in"], 16)
                sp.wait_ge(sems["x1"], at("x1", i, PER["x1"]))
                sp.dma_start(xin[:, :, :], x[bass.ds(i + 1 if more else i, 1)].rearrange("o (t p) d -> p (o t) d", p=P)
                             ).then_inc(sems["x_in"], 16)
                for t in range(NT):
                    if t == NT - 1:
                        sp.wait_ge(sems["hidT_ps"], at("hidT_ps", i, PER["hidT_ps"]))
                        apart(sp)
                        stack(i, 0, 1)
                        sp.wait_ge(sems["had2_ps"], at("had2_ps", i, PER["had2_ps"]))
                        apart(sp)
                        stack(i, 1, 1)
                    sp.wait_ge(sems["y"], at("y", i, t + 1))
                    sp.dma_start(out[bass.ds(i, 1), t * P:(t + 1) * P, :].rearrange("o p d -> (o p) d"),
                                 xcur[:, t, :]).then_inc(sems[f"store{t % 2}"], 16)

            with sp.Fori(0, B - 1) as i:
                batch_row(i, True)
            batch_row(B - 1, False)
            for n in range(2):
                sp.wait_ge(sems[f"store{n}"], at(f"store{n}", B, 0))

        @block.tensor
        def _(pe):
            def prologue_bank(n):
                if n >= 8:
                    s, k = PJOBS[n - 8]
                    pe.wait_ge(p_act if s == "act" else p_dve, k)
                return n % 8

            pe.wait_ge(in_kv, 160)
            n = 0
            b_ = prologue_bank(n)
            for c in range(KC):
                mm = pe.matmul(ps[:, b_, :], wkvc_sb[:, c, :], ctxT_sb[:, c, :], start=c == 0, stop=c == KC - 1)
            mm.then_inc(p_ps, 1)
            n += 1
            pe.wait_ge(p_act, 1)
            for s in range(2):
                pe.matmul(ps[:, prologue_bank(n), :], wkr_sb[:, s, :], kvT[:, :], start=True, stop=True).then_inc(p_ps, 1)
                n += 1
            for h in range(H):
                pe.matmul(ps[:, prologue_bank(n), 0:QC], wukT_sb[:, h, :], wuqT_sb[:, h, :], start=True, stop=True
                          ).then_inc(p_ps, 1)
                n += 1
            for h in range(H):
                pe.matmul(ps[:, prologue_bank(n), :], wuvT_sb[:, h, :], wox_sb[:, h, :], start=True, stop=True
                          ).then_inc(p_ps, 1)
                n += 1
            pe.wait_ge(p_dve, NN_DVE)
            for m in range(4 * H):
                bp, h = m // H, m % H
                pe.matmul(ps[:, prologue_bank(n), :], kvT[:, bp * P:(bp + 1) * P], nn[:, h, :], start=True, stop=True
                          ).then_inc(p_ps, 1)
                n += 1
            for h in range(H):
                pe.matmul(ps[:, prologue_bank(n), :], mt[:, h, 0:P], kvT[:, :], start=True, stop=True).then_inc(p_ps, 1)
                n += 1
                pe.matmul(ps[0:QC1, prologue_bank(n), :], mt[:, h, P:QC], kvT[:, :], start=True, stop=True).then_inc(p_ps, 1)
                n += 1
            pe.wait_ge(ffn_step, 3)
            pe.wait_ge(p_const, 2)
            pe.matmul(ps[:, prologue_bank(n), 0:3], ones[:, :], wsum[:, :], start=True, stop=True).then_inc(p_ffn_ps, 1)
            pe.wait_ge(in_weights, 144)
            pe.wait_ge(ffn_done, 1)
            pe.wait_ge(vw_const, 1)
            pe.wait_ge(had_ready, 1)

            i = 0
            reader = {}

            def take(*banks):
                need = {}
                for b in banks:
                    if b in reader:
                        name, k = reader[b]
                        need[name] = max(need.get(name, k), k)
                for name, k in need.items():
                    pe.wait_ge(sems[name], at(name, i, k))

            def transposes_of_xn(n, b, ahead=0):
                pe.wait_ge(sems["xn"], at("xn", i, 12 * ahead + n + 1))
                take(b)
                for c in range(KC):
                    mm = pe.transpose(ps[:, b, c * P:(c + 1) * P], xn[:, n % 2, c * P:(c + 1) * P], ident_f[:, :])
                mm.then_inc(sems["xt_ps"], 1)
                reader[b] = ("xt", 12 * ahead + n + 1) if n < 8 else ("xt_lo", n - 7)

            def project(j, ahead=0):
                if j == 0:
                    pe.wait_ge(sems["xt"], at("xt", i, 12 * ahead + 4))
                for odd in range(2):
                    b = 2 + 2 * j + odd
                    take(b)
                    for c in range(KC):
                        w = wk_sb[:, c, odd * P:(odd + 1) * P] if j == 0 else \
                            wq_sb[:, c, (2 * j - 2 + odd) * P:(2 * j - 1 + odd) * P]
                        mm = pe.matmul(ps[:, b, :], w, xT[:, c, :], start=c == 0, stop=c == KC - 1)
                    mm.then_inc(sems["proj"], 1)
                    reader[b] = ("rope_m", 12 * ahead + 4 * j + 4)

            for t in range(NT):
                transposes_of_xn(t, t % 2)
            project(0)
            project(1)

            with pe.Fori(0, B) as i:
                reader.clear()
                reader.update({0: ("y", 0), 1: ("y", 0), 2: ("rope_m", 4), 3: ("rope_m", 4),
                               4: ("rope_m", 8), 5: ("rope_m", 8), 6: ("f2int", 0), 7: ("f2int", 0)})

                def values(t):
                    b = 6 + t % 2
                    take(b)
                    for c in range(KC):
                        mm = pe.matmul(ps[:, b, 0:G * HD], xT[:, c, t * P:(t + 1) * P], wv_sb[:, c, :],
                                       start=c == 0, stop=c == KC - 1)
                    mm.then_inc(sems["v_ps"], 1)
                    reader[b] = ("vw", t + 1)

                def scores_for_max(n):
                    h, t, b0 = MAX_JOBS[n]
                    take(b0, b0 + 1)
                    for u in range(2):
                        mm = pe.matmul(ps[:, b0 + u, :], qs[0:96, h + u, t * P:(t + 1) * P], ks[0:96, h // 2, :],
                                       start=True, stop=True)
                        reader[b0 + u] = ("smax", n + 1)
                    mm.then_inc(sems["smax_ps"], 1)

                def maxima_to_rows(hg):
                    pe.wait_ge(sems["nms"], at("nms", i, hg + 1))
                    take(0)
                    for t in range(NT):
                        mm = pe.transpose(ps[0:H, 0, t * P:(t + 1) * P], negsplit[:, hg, t, :].bitcast(F32), ident_f[:, :])
                    mm.then_inc(sems["nmt_ps"], 1)
                    reader[0] = ("nmt", hg + 1)

                project(2)
                pe.wait_ge(sems["stack"], at("stack", i, 2 * NCOPY * 16))
                for n in range(16):
                    scores_for_max(n)
                    if n in (8, 12):
                        values((n - 8) // 4)
                pe.wait_ge(sems["stack"], at("stack", i, PER["stack"]))
                scores_for_max(16)
                scores_for_max(17)
                maxima_to_rows(0)
                values(2)
                scores_for_max(18)
                scores_for_max(19)
                values(3)

                def scores(j):
                    h, half = j // 2, j % 2
                    b0 = 2 + 2 * (j % 2)
                    take(b0, b0 + 1)
                    for u in range(2):
                        kt = 2 * half + u
                        mm = pe.matmul(ps[:, b0 + u, :], ks[0:98, h // 2, kt * P:(kt + 1) * P], qs[0:98, h, :],
                                       start=True, stop=True)
                        reader[b0 + u] = ("probs", j + 1)
                    mm.then_inc(sems["st_ps"], 1)

                def weigh(j):
                    h, half = j // 2, j % 2
                    b = 6 + (h // 2) % 2
                    pe.wait_ge(sems["probs"], at("probs", i, j + 1))
                    if j % 4 == 0:
                        take(b)
                    lo = (h // 2) * P + (0 if h % 2 else 32)
                    for u in range(2):
                        kt = 2 * half + u
                        mm = pe.matmul(ps[:, b, :], vw[:, kt, lo:lo + P], pt[:, j % 4, u * 512:(u + 1) * 512],
                                       start=j % 4 == 0 and u == 0, stop=j % 4 == 3 and u == 1)
                    if half:
                        mm.then_inc(sems["pv"], 1)
                    reader[b] = ("at", h // 2 + 1)

                pe.wait_ge(sems["rows_in"], at("rows_in", i, 32))
                pe.wait_ge(sems["ks_ones"], at("ks_ones", i, 1))
                pe.wait_ge(sems["vw"], at("vw", i, 4))
                scores(0)
                for j in range(2 * H):
                    if j + 1 == H:
                        pe.wait_ge(sems["rows_in"], at("rows_in", i, 64))
                    if j + 1 < 2 * H:
                        scores(j + 1)
                    for n in MAX_AT.get(j, ()):
                        scores_for_max(n)
                    if j == 13:
                        maxima_to_rows(1)
                    weigh(j)
                pe.wait_ge(sems["at"], at("at", i, HP))

                def project_out(t):
                    take(t)
                    for c in range(KC):
                        mm = pe.matmul(ps[:, t, :], aT[:, c, t * P:(t + 1) * P], wo_sb[:, c, :],
                                       start=c == 0, stop=c == KC - 1)
                    mm.then_inc(sems["wo_ps"], 1)
                    reader[t] = ("x1", t + 1)

                for t in range(3):
                    project_out(t)
                transposes_of_xn(4, 4)
                project_out(3)
                for t in range(1, NT):
                    transposes_of_xn(4 + t, 4 + t % 2)
                pe.wait_ge(sems["xt"], at("xt", i, 8))
                for m, (lo, hi) in enumerate(((0, P), (P, QC))):
                    take(6 + m)
                    for c in range(KC):
                        mm = pe.matmul(ps[0:hi - lo, 6 + m, :], wdq_sb[:, c, lo:hi], xT[:, c, :],
                                       start=c == 0, stop=c == KC - 1)
                    mm.then_inc(sems["dq_ps"], 1)
                    reader[6 + m] = ("qc", m + 1)
                pe.wait_ge(sems["qc"], at("qc", i, 2))

                def rope_queries(half):
                    for p in range(HP):
                        m = HP * half + p
                        b = m % 4
                        take(b)
                        q = slice(256 * half, 256 * half + 256)
                        pe.matmul(ps[:, b, 0:256], wqr0[:, p * P:(p + 1) * P], qc0[:, q], start=True, stop=False)
                        pe.matmul(ps[:, b, 0:256], wqr1[:, p * P:(p + 1) * P], qc1[:, q], start=False, stop=True
                                  ).then_inc(sems["xr_ps"], 1)
                        reader[b] = ("xcs", m + 1)

                def cross_scores(t):
                    pe.wait_ge(sems["xcs"], at("xcs", i, HP * (t // 2 + 1)))
                    q = slice(t * P, t * P + P)
                    ql = slice((t % 2) * P, (t % 2) * P + P)
                    for hb in range(2):
                        b = 4 + 2 * (t % 2) + hb
                        take(b)
                        cols = slice(512 * hb, 512 * hb + 512)
                        pe.matmul(ps[:, b, :], qc0[:, q], ak0[:, cols], start=True, stop=False)
                        pe.matmul(ps[:, b, :], qc1[:, q], ak1[:, cols], start=False, stop=False)
                        for u in range(4):
                            p = 4 * hb + u
                            pe.matmul(ps[:, b, u * P:(u + 1) * P], xc[:, p, ql], kd[:, 0, :], start=False, stop=False)
                            mm = pe.matmul(ps[:, b, u * P:(u + 1) * P], xs[:, p, ql], kd[:, 1, :],
                                           start=False, stop=u == 3)
                        reader[b] = ("masked", t + 1)
                    mm.then_inc(sems["sc_ps"], 1)

                def cross_transposes(t):
                    pe.wait_ge(sems["xprob"], at("xprob", i, t + 1))
                    for hb in range(2):
                        take(hb)
                        for u in range(4):
                            p = 4 * hb + u
                            mm = pe.transpose(ps[:, hb, u * P:(u + 1) * P],
                                              ex[:, t % 2, 2 * p:2 * p + 2, :].rearrange("p h k -> p (h k)"), ident_f[:, :])
                        mm.then_inc(sems["pt_ps"], 1)
                        reader[hb] = ("ptx", 2 * t + hb + 1)

                def cross_out(t):
                    b = 2 + t % 2
                    take(b)
                    pe.wait_ge(sems["ptx"], at("ptx", i, 2 * t + 2))
                    for p in range(HP):
                        mm = pe.matmul(ps[:, b, :], ptx[:, p, :], vp[:, p, :], start=p == 0, stop=p == HP - 1)
                    mm.then_inc(sems["xo_ps"], 1)
                    reader[b] = ("x2", t + 1)

                def ffn_rotate(t):
                    b = ROT_BANK[t]
                    take(b)
                    pe.wait_ge(sems["xt"], at("xt", i, 8 + t + 1))
                    pe.wait_ge(sems["xt_lo"], at("xt_lo", i, t + 1))
                    for c in range(KC):
                        pe.matmul(ps[:, b, :], xT3[:, c, :], had_sb[:, c, :], start=c == 0, stop=False)
                        mm = pe.matmul(ps[:, b, :], xT3_lo[:, c, :], had_sb[:, c, :], start=False, stop=c == KC - 1)
                    mm.then_inc(sems["had_ps"], 1)
                    reader[b] = ("fround", t + 1)

                def ffn_integers(t):
                    b = INT_BANK[t]
                    take(b)
                    pe.wait_ge(sems["fint"], at("fint", i, t + 1))
                    for c in range(KC):
                        mm = pe.transpose(ps[:, b, :].bitcast(BF16)[:, c * P:(c + 1) * P], fq[:, c * P:(c + 1) * P],
                                          ident_b[:, :])
                    mm.then_inc(sems["fintT_ps"], 1)
                    reader[b] = ("fintT", t + 1)

                def ffn_gate_up(t):
                    pe.wait_ge(sems["fintT"], at("fintT", i, t + 1))
                    for g in range(FG):
                        n = FG * t + g + 1
                        for b, w, sem, user in ((GU_BANK[t][g], gate_w, "gate_ps", "gated"),
                                                (GU_BANK[t][g] + 1, up_w, "up_ps", "hid")):
                            take(b)
                            apart(pe)
                            for c in range(KC):
                                mm = pe.matmul(ps[:, b, :], fqT[:, c, :], w[:, c, g * 512:(g + 1) * 512],
                                               start=c == 0, stop=c == KC - 1)
                            mm.then_inc(sems[sem], 1)
                            reader[b] = (user, n)

                def ffn_hidden_transposes(t):
                    pe.wait_ge(sems["sum2"], at("sum2", i, t + 1))
                    pe.wait_ge(sems["diff2"], at("diff2", i, t + 1))
                    for g in range(FG):
                        b = HT_BANK[t] + g % 2
                        take(b)
                        for c in range(4):
                            mm = pe.transpose(ps[:, b, c * P:(c + 1) * P], hid[t % 2][:, g, c * P:(c + 1) * P], ident_f[:, :])
                        mm.then_inc(sems["hidT_ps"], 1)
                        reader[b] = ("hidT_lo", FG * t + g + 1)

                def ffn_hidden_rotate(t):
                    for g in range(FG):
                        take(4 + g)
                        pe.wait_ge(sems["hidT"], at("hidT", i, FG * t + g + 1))
                        pe.wait_ge(sems["hidT_lo"], at("hidT_lo", i, FG * t + g + 1))
                        for c in range(4):
                            pe.matmul(ps[:, 4 + g, :], hidT[:, 4 * g + c, :], had_sb[:, c, :], start=c == 0, stop=False)
                            mm = pe.matmul(ps[:, 4 + g, :], hidT_lo[:, 4 * g + c, :], had_sb[:, c, :],
                                           start=False, stop=c == 3)
                        mm.then_inc(sems["had2_ps"], 1)
                        reader[4 + g] = ("f2int", 2 * t + g // 2 + 1)

                def ffn_down(t):
                    b0 = DOWN_BANK[t]
                    for half in range(2):
                        b = b0 + half
                        take(b)
                        pe.wait_ge(sems["f2int"], at("f2int", i, 2 * t + half + 1))
                        for c in range(8):
                            k = 8 * half + c
                            mm = pe.transpose(ps[:, b, :].bitcast(BF16)[:, c * P:(c + 1) * P],
                                              f2q[:, k * P:(k + 1) * P], ident_b[:, :])
                        mm.then_inc(sems["f2intT_ps"], 1)
                        reader[b] = ("f2intT", 2 * t + half + 1)
                    pe.wait_ge(sems["f2intT"], at("f2intT", i, 2 * t + 2))
                    apart(pe)
                    for k in range(FC):
                        mm = pe.matmul(ps[:, b0, :], f2qT[:, k, :], down_w[:, k, :], start=k == 0, stop=k == FC - 1)
                    mm.then_inc(sems["down_ps"], 1)
                    reader[b0] = ("y", t + 1)

                rope_queries(0)
                pe.wait_ge(sems["ak_in"], at("ak_in", i, 48))
                cross_scores(0)
                cross_scores(1)
                rope_queries(1)
                pe.wait_ge(sems["v_in"], at("v_in", i, 16))
                cross_transposes(0)
                cross_scores(2)
                cross_out(0)
                cross_transposes(1)
                cross_scores(3)
                cross_out(1)
                cross_transposes(2)
                transposes_of_xn(8, XT_BANK[0])
                cross_out(2)
                cross_transposes(3)
                ffn_rotate(0)
                transposes_of_xn(9, XT_BANK[1])
                cross_out(3)
                ffn_integers(0)
                ffn_rotate(1)
                ffn_gate_up(0)
                ffn_integers(1)
                transposes_of_xn(10, XT_BANK[2])
                ffn_rotate(2)
                ffn_gate_up(1)
                ffn_hidden_transposes(0)
                ffn_integers(2)
                for t in range(NT):
                    ffn_hidden_rotate(t)
                    if t + 3 < NT:
                        transposes_of_xn(8 + t + 3, XT_BANK[t + 3])
                        ffn_rotate(t + 3)
                    if t == 2:
                        transposes_of_xn(0, 0, 1)
                        transposes_of_xn(1, 1, 1)
                    if t + 1 < NT:
                        ffn_hidden_transposes(t + 1)
                    if t == 2:
                        transposes_of_xn(2, 0, 1)
                        transposes_of_xn(3, 1, 1)
                    if t + 2 < NT:
                        ffn_gate_up(t + 2)
                    if t == 3:
                        project(0, 1)
                        project(1, 1)
                    ffn_down(t)
                    if t + 3 < NT:
                        ffn_integers(t + 3)

        @block.scalar
        def _(act):
            for n, (s, k) in enumerate(PJOBS):
                if s != "act":
                    continue
                act.wait_ge(p_ps, n + 1)
                if n == 0:
                    act.copy(kvT[:, :], ps[:, 0, :]).then_inc(p_act, 1)
                elif 3 <= n < 3 + H:
                    act.copy(mt[:, n - 3, :], ps[:, n % 8, 0:QC]).then_inc(p_act, 1)
                elif V0 <= n < A0:
                    m = n - V0
                    if m >= 4:
                        act.wait_ge(p_vstore[m % 4], 16 * (m // 4))
                    act.copy(vst[:, m % 4, :], ps[:, n % 8, :]).then_inc(p_act, 1)
                else:
                    h = (n - A0) // 2
                    act.copy(ast1[:, :, h, :], ps[0:QC1, n % 8, :].rearrange("p (b k) -> p b k", b=B)).then_inc(p_act, 1)
            act.wait_ge(p_act, NACT)
            act.sem_inc(kv_done, 1)
            act.wait_ge(in_kv, 160)
            act.copy(ident_b[:, :], ident_f[:, :]).then_inc(p_const, 1)
            act.wait_ge(in_had, 16)
            act.copy(had_sb[:, :, :], had_in[:, :, :]).then_inc(had_ready, 1)

            i = 0
            def evacuate_xt(n, b, out, ahead=0):
                act.wait_ge(sems["xt_ps"], at("xt_ps", i, 12 * ahead + n + 1))
                act.copy(out, ps[:, b, :].rearrange("p (c q) -> p c q", c=KC)).then_inc(sems["xt"], 1)

            def high_parts(j, ahead=0):
                if j < 2:
                    act.wait_ge(sems["rope_cv"], at("rope_cv", i, 4 * ahead + 2 * j + 2))
                else:
                    act.wait_ge(sems["rope_c"], at("rope_c", i, 2))
                if j:
                    act.wait_ge(sems["stack"], at("stack", i, 16 * NCOPY * (3 * ahead + j)))
                for odd in range(2):
                    act.copy(parts[:, odd, :], rot[:, 2 * odd, :]).then_inc(sems["rope_h"], 1)

            for t in range(NT):
                evacuate_xt(t, t % 2, xT[:, :, t * P:(t + 1) * P])
            high_parts(0)
            high_parts(1)

            with act.Fori(0, B) as i:
                def values(t):
                    act.wait_ge(sems["v_ps"], at("v_ps", i, t + 1))
                    act.copy(vw[:, t, 0:G * P].rearrange("p (g c) -> p g c", c=P)[:, :, 32:64],
                             ps[:, 6 + t % 2, 0:G * HD].rearrange("p (g c) -> p g c", c=HD)).then_inc(sems["vw"], 1)

                def maxima(hg):
                    act.wait_ge(sems["nmt_ps"], at("nmt_ps", i, hg + 1))
                    if hg:
                        act.wait_ge(sems["rows_in"], at("rows_in", i, 32))
                    act.copy(rows[:, :], ps[0:H, 0, :]).then_inc(sems["nmt"], 1)

                def exponentials(j):
                    act.wait_ge(sems["st_ps"], at("st_ps", i, j + 1))
                    if j >= 4:
                        act.wait_ge(sems["pv"], at("pv", i, (j - 4) // 2 + 1))
                    b0 = 2 + 2 * (j % 2)
                    act.activation(pt[:, j % 4, :], ps[:, b0:b0 + 2, :].rearrange("p b q -> p (b q)"), ACT.Exp,
                                   scale=SELF_SCALE).then_inc(sems["probs"], 1)

                high_parts(2)
                values(0)
                values(1)
                maxima(0)
                values(2)
                values(3)
                for j in range(2 * H):
                    if j == H:
                        maxima(1)
                    exponentials(j)
                for t in range(NT):
                    evacuate_xt(4 + t, 4 + t % 2, xT[:, :, t * P:(t + 1) * P])
                for m, q in enumerate((qc0, qc1)):
                    act.wait_ge(sems["dq_ps"], at("dq_ps", i, m + 1))
                    act.copy(q[:, :], ps[0:q.shape[0], 6 + m, :]).then_inc(sems["qc"], 1)

                def cross_exp(t):
                    act.wait_ge(sems["centred"], at("centred", i, t + 1))
                    e = ex[:, t % 2, :, :].rearrange("p h k -> p (h k)")
                    act.activation(e, e, ACT.Exp, scale=X_SCALE).then_inc(sems["xexp"], 1)

                def cross_evacuate(t):
                    for hb in range(2):
                        act.wait_ge(sems["pt_ps"], at("pt_ps", i, 2 * t + hb + 1))
                        if t:
                            act.wait_ge(sems["xo_ps"], at("xo_ps", i, t))
                        act.copy(ptx[:, 4 * hb:4 * hb + 4, :].rearrange("p c q -> p (c q)"), ps[:, hb, :]
                                 ).then_inc(sems["ptx"], 1)

                def ffn_xt(t):
                    if t:
                        act.wait_ge(sems["had_ps"], at("had_ps", i, t))
                    evacuate_xt(8 + t, XT_BANK[t], xT3[:, :, :])

                def ffn_round(t):
                    act.wait_ge(sems["fsc"], at("fsc", i, t + 1))
                    if t:
                        act.wait_ge(sems["fint"], at("fint", i, t))
                    act.activation(fv[:, :], ps[:, ROT_BANK[t], :], ACT.Copy, bias=MAGIC, scale=fs[:, t, 2:3]
                                   ).then_inc(sems["fround"], 1)

                def ffn_intT(t):
                    act.wait_ge(sems["fintT_ps"], at("fintT_ps", i, t + 1))
                    if t:
                        act.wait_ge(sems["up_ps"], at("up_ps", i, FG * t))
                    act.copy(fqT[:, :, :].rearrange("p c q -> p (c q)"), ps[:, INT_BANK[t], :].bitcast(BF16)[:, 0:512]
                             ).then_inc(sems["fintT"], 1)

                def ffn_tanh(t, groups):
                    for g in groups:
                        n = FG * t + g
                        act.wait_ge(sems["gate_ps"], at("gate_ps", i, n + 1))
                        if n > 1:
                            act.wait_ge(sems["gated"], at("gated", i, n - 1))
                        act.activation(th[:, n % 2, :], ps[:, GU_BANK[t][g], :], ACT.Tanh, scale=fs[:, t, 3:4]
                                       ).then_inc(sems["th"], 1)

                def ffn_hidT(t):
                    if t:
                        act.wait_ge(sems["had2_ps"], at("had2_ps", i, FG * t))
                    for g in range(FG):
                        act.wait_ge(sems["hidT_ps"], at("hidT_ps", i, FG * t + g + 1))
                        act.copy(hidT[:, 4 * g:4 * g + 4, :].rearrange("p c q -> p (c q)"), ps[:, HT_BANK[t] + g % 2, :]
                                 ).then_inc(sems["hidT"], 1)

                def ffn_round2(t):
                    act.wait_ge(sems["f2sc"], at("f2sc", i, t + 1))
                    for half in range(2):
                        b0 = 4 + 2 * half
                        v = ps[:, b0:b0 + 2, :].rearrange("p b q -> p (b q)")
                        act.activation(v, v, ACT.Copy, bias=MAGIC, scale=f2s[:, t, 2:3]).then_inc(sems["f2round"], 1)

                def ffn_int2T(t):
                    for half in range(2):
                        act.wait_ge(sems["f2intT_ps"], at("f2intT_ps", i, 2 * t + half + 1))
                        if t:
                            act.wait_ge(sems["down_ps"], at("down_ps", i, t))
                        act.copy(f2qT[:, 8 * half:8 * half + 8, :].rearrange("p c q -> p (c q)"),
                                 ps[:, DOWN_BANK[t] + half, :].bitcast(BF16)).then_inc(sems["f2intT"], 1)

                cross_exp(0)
                cross_exp(1)
                cross_evacuate(0)
                cross_exp(2)
                cross_evacuate(1)
                cross_exp(3)
                cross_evacuate(2)
                ffn_xt(0)
                cross_evacuate(3)
                ffn_round(0)
                ffn_xt(1)
                ffn_intT(0)
                ffn_round(1)
                ffn_tanh(0, range(FG))
                ffn_intT(1)
                ffn_xt(2)
                ffn_tanh(1, range(0, 2))
                ffn_round(2)
                ffn_tanh(1, range(2, FG))
                ffn_hidT(0)
                ffn_intT(2)
                for t in range(NT):
                    if t + 3 < NT:
                        ffn_xt(t + 3)
                    if t == 2:
                        evacuate_xt(0, 0, xT[:, :, 0:P], 1)
                        evacuate_xt(1, 1, xT[:, :, P:2 * P], 1)
                    if t + 1 < NT:
                        ffn_hidT(t + 1)
                    if t == 2:
                        evacuate_xt(2, 0, xT[:, :, 2 * P:3 * P], 1)
                        evacuate_xt(3, 1, xT[:, :, 3 * P:4 * P], 1)
                    ffn_round2(t)
                    if t + 2 < NT:
                        ffn_tanh(t + 2, range(0, 2))
                    if t + 3 < NT:
                        ffn_round(t + 3)
                    if t + 2 < NT:
                        ffn_tanh(t + 2, range(2, FG))
                    if t == 3:
                        high_parts(0, 1)
                    ffn_int2T(t)
                    if t + 3 < NT:
                        ffn_intT(t + 3)
                high_parts(1, 1)

        @block.vector
        def _(dve):
            dve.wait_ge(in_kv, 160)
            for n, (s, k) in enumerate(PJOBS):
                if s != "dve":
                    continue
                dve.wait_ge(p_ps, n + 1)
                if n in (1, 2):
                    b3 = ps[:, n, :].rearrange("p (b k) -> p b k", b=B)
                    for v in range(2):
                        tab = krope_sb[:, 2 * v + n - 1:2 * v + n, :].broadcast_to([P, B, LK])
                        last = dve.tensor_tensor(ktmp[:, 2 * v + n - 1, :].rearrange("p (b k) -> p b k", b=B), b3, tab,
                                                 ALU.mult)
                    last.then_inc(p_dve, 1)
                    if n == 2:
                        dve.wait_ge(p_dve, 2)
                        dve.wait_ge(p_kzero, 1)
                        for v in range(2):
                            for u in range(2):
                                q = slice(64 * u, 64 * u + 64)
                                last = dve.tensor_tensor(
                                    kd_all[q, :, v, q],
                                    ktmp[q, 2 * v, :].rearrange("p (b k) -> p b k", b=B),
                                    ktmp[q, 2 * v + 1, :].rearrange("p (b k) -> p b k", b=B), ALU.add)
                elif 3 + H <= n < V0:
                    dve.tensor_copy(nn[:, n - 3 - H, :], ps[:, n % 8, :]).then_inc(p_dve, 1)
                elif V0 <= n < A0:
                    m = n - V0
                    if m >= 4:
                        dve.wait_ge(p_vstore[m % 4], 16 * (m // 4))
                    dve.tensor_copy(vst[:, m % 4, :], ps[:, n % 8, :]).then_inc(p_dve, 1)
                else:
                    h = (n - A0) // 2
                    if h == 0:
                        dve.wait_ge(p_ps, A0)
                    dve.tensor_copy(ast0[:, :, h, :], ps[:, n % 8, :].rearrange("p (b k) -> p b k", b=B)).then_inc(p_dve, 1)
            dve.wait_ge(p_dve, NDVE)
            dve.sem_inc(kv_done, 1)
            dve.wait_ge(in_ffn, 48)
            for n in range(3):
                dve.tensor_reduce(wsum[:, n:n + 1], wst[n][:, :], AX.X, ALU.add, apply_absolute_value=True
                                  ).then_inc(ffn_step, 1)
            dve.wait_ge(p_ffn_ps, 1)
            dve.tensor_scalar(wsc[:, :], ps[:, NJOBS % 8, 0:3], 1.0 / (F * D), EPS, ALU.mult, ALU.max).then_inc(ffn_step, 1)
            dve.wait_ge(ffn_step, 4)
            dve.tensor_scalar(wthr[:, 0:3], wsc[:, :], 0.5, None, ALU.mult).then_inc(ffn_step, 1)
            dve.tensor_scalar(wthr[:, 3:6], wsc[:, :], -0.5, None, ALU.mult).then_inc(ffn_step, 1)
            for n, w in enumerate((gate_w, up_w, down_w)):
                dve.wait_ge(ffn_step, 6 + 2 * n)
                dve.tensor_scalar(wlow[:, :], wst[n][:, :], wthr[:, 3 + n:4 + n], None, ALU.is_lt).then_inc(ffn_step, 1)
                dve.wait_ge(ffn_step, 7 + 2 * n)
                dve.scalar_tensor_tensor(w[:, :, :].rearrange("p c n -> p (c n)"), wst[n][:, :], wthr[:, n:n + 1],
                                         wlow[:, :], ALU.is_gt, ALU.subtract, saturate=False).then_inc(ffn_step, 1)
            dve.wait_ge(ffn_step, 12)
            dve.sem_inc(ffn_done, 1)
            dve.wait_ge(in_weights, 144)

            i = 0
            steps = [0]

            def step(ins):
                steps[0] += 1
                ins.then_inc(sems["dve_step"], 1)

            def settle():
                dve.wait_ge(sems["dve_step"], at("dve_step", i, steps[0]))

            def ln_stats(n, src):
                step(dve.bn_stats(stats[:, n, :], src))
                settle()
                apart(dve)
                dve.bn_aggr(mv[:, n, :], stats[:, n, :]).then_inc(sems["mv"], 1)

            def ln_normalise(n, src, ahead=0):
                dve.wait_ge(sems["rstd"], at("rstd", i, 12 * ahead + n + 1))
                dve.wait_ge(sems["xt_ps"], at("xt_ps", i, 12 * ahead + n - 1))
                dve.tensor_scalar(xn[:, n % 2, :], src, mv[:, n, 0:1], rstd[:, n:n + 1], ALU.subtract, ALU.mult
                                  ).then_inc(sems["xn"], 1)

            def rotate(j, ahead=0):
                dve.wait_ge(sems["proj"], at("proj", i, 6 * ahead + 2 * j + 2))
                if j:
                    dve.wait_ge(sems["rope_l"], at("rope_l", i, 6 * ahead + 2 * j))
                for v in range(4):
                    dve.tensor_tensor(rot[:, v, :], ps[:, 2 + 2 * j + v % 2, :], rope_sb[:, (v + v // 2) % 2, :],
                                      ALU.mult).then_inc(sems["rope_m"], 1)

            def low_parts(j, ahead=0):
                for odd in range(2):
                    dve.wait_ge(sems["rope_h"], at("rope_h", i, 6 * ahead + 2 * j + odd + 1))
                    dve.tensor_tensor(parts[:, 2 + odd, :], rot[:, 2 * odd, :], parts[:, odd, :].bitcast(F32),
                                      ALU.subtract).then_inc(sems["rope_l"], 1)

            def combine(j, ahead=0):
                dve.wait_ge(sems["rope_m"], at("rope_m", i, 12 * ahead + 4 * j + 4))
                dve.tensor_tensor(rot[:, 0, :], rot[:, 0, :], rot[:, 1, :], ALU.subtract).then_inc(sems["rope_cv"], 1)
                dve.tensor_tensor(rot[:, 2, :], rot[:, 2, :], rot[:, 3, :], ALU.add).then_inc(sems["rope_cv"], 1)

            def first_stats(ahead=0):
                dve.wait_ge(sems["x_in"], at("x_in", i, 16 * ahead + 16))
                for t in range(NT):
                    ln_stats(t, xin[:, t, :])

            first_stats()
            for t in range(NT):
                ln_normalise(t, xin[:, t, :])
            for j in range(2):
                rotate(j)
                combine(j)
                low_parts(j)
            steps_before = steps[0]

            with dve.Fori(0, B) as i:
                steps[0] = steps_before
                def maximum(n):
                    h, t, b0 = MAX_JOBS[n]
                    dve.wait_ge(sems["smax_ps"], at("smax_ps", i, n + 1))
                    dve.tensor_reduce(negmax[:, t, h:h + 2], ps[:, b0:b0 + 2, :], AX.X, ALU.max, negate=True
                                      ).then_inc(sems["smax"], 1)

                def split_maxima(hg):
                    dve.wait_ge(sems["smax"], at("smax", i, 16 * (hg + 1)))
                    m = negmax[:, :, 8 * hg:8 * hg + 8]
                    step(dve.tensor_copy(negsplit[:, hg, :, 0:8], m))
                    settle()
                    dve.tensor_tensor(negsplit[:, hg, :, 8:16], m, negsplit[:, hg, :, 0:8].bitcast(F32), ALU.subtract
                                      ).then_inc(sems["nms"], 1)

                def denominators_of_heads(p, half):
                    if half == 0:
                        dve.wait_ge(sems["pv"], at("pv", i, 2 * p + 2))
                        if p:
                            dve.wait_ge(sems["at"], at("at", i, p))
                    q = slice(256 * half, 256 * half + 256)
                    step(dve.reciprocal(rcp[:, q], ps[64:128, 6 + p % 2, q]))

                def normalise_heads(p):
                    b = 6 + p % 2
                    settle()
                    r0 = 64 * (p % 2)
                    dve.tensor_tensor(aT[r0:r0 + 64, p // 2, :], ps[0:64, b, :], rcp[:, :], ALU.mult
                                      ).then_inc(sems["at"], 1)

                for n in range(16):
                    if n == 3:
                        rotate(2)
                    elif n == 8:
                        low_parts(2)
                    maximum(n)
                split_maxima(0)
                for n in range(16, 20):
                    maximum(n)
                for j in range(2 * H):
                    for n in MAX_AT.get(j, ()):
                        maximum(n)
                    if j == 12:
                        split_maxima(1)
                    if j % 4 == 0 and j:
                        denominators_of_heads(j // 4 - 1, 1)
                        normalise_heads(j // 4 - 1)
                    elif j % 4 == 3:
                        denominators_of_heads(j // 4, 0)
                denominators_of_heads(HP - 1, 1)
                normalise_heads(HP - 1)
                for t in range(NT):
                    dve.wait_ge(sems["wo_ps"], at("wo_ps", i, t + 1))
                    if t < 2:
                        dve.wait_ge(sems[f"store{t}"], at(f"store{t}", i, 0))
                    dve.tensor_tensor(xcur[:, t, :], ps[:, t, :], xin[:, t, :], ALU.add).then_inc(sems["x1"], 1)
                    dve.wait_ge(sems["x1"], at("x1", i, t + 1))
                    ln_stats(4 + t, xcur[:, t, :])
                    if t >= 2:
                        ln_normalise(4 + t - 2, xcur[:, t - 2, :])
                for t in range(2, NT):
                    ln_normalise(4 + t, xcur[:, t, :])

                def rotate_queries(half):
                    if half:
                        dve.wait_ge(sems["sc_ps"], at("sc_ps", i, 2))
                    for p in range(HP):
                        m = HP * half + p
                        dve.wait_ge(sems["xr_ps"], at("xr_ps", i, m + 1))
                        q = slice(256 * half, 256 * half + 256)
                        dve.tensor_tensor(xc[:, p, :], ps[:, m % 4, 0:256], rope_sb[:, 2, q], ALU.mult)
                        dve.tensor_tensor(xs[:, p, :], ps[:, m % 4, 0:256], rope_sb[:, 3, q], ALU.mult
                                          ).then_inc(sems["xcs"], 1)

                def mask_and_centre(t):
                    dve.wait_ge(sems["sc_ps"], at("sc_ps", i, t + 1))
                    if t == 0:
                        dve.wait_ge(sems["maskt"], at("maskt", i, 1))
                    if t >= 2:
                        dve.wait_ge(sems["pt_ps"], at("pt_ps", i, 2 * (t - 1)))
                    b0 = 4 + 2 * (t % 2)
                    e = ex[:, t % 2, :, :]
                    dve.tensor_tensor(e, ps[:, b0:b0 + 2, :].rearrange("p b (h k) -> p (b h) k", k=LK),
                                      maskt[:, t:t + 1, :].broadcast_to([P, H, LK]), ALU.add).then_inc(sems["masked"], 1)
                    dve.wait_ge(sems["masked"], at("masked", i, t + 1))
                    step(dve.tensor_reduce(xmax[:, t, :], e, AX.X, ALU.max))
                    settle()
                    dve.tensor_tensor(e, e, xmax[:, t, :].unsqueeze(2).broadcast_to([P, H, LK]), ALU.subtract
                                      ).then_inc(sems["centred"], 1)

                def denominators(t):
                    dve.wait_ge(sems["xexp"], at("xexp", i, t + 1))
                    step(dve.tensor_reduce(xsum[:, t, :], ex[:, t % 2, :, :], AX.X, ALU.add))
                    settle()
                    dve.reciprocal(xrec[:, t, :], xsum[:, t, :]).then_inc(sems["xden"], 1)

                def residual2(t):
                    dve.wait_ge(sems["xo_ps"], at("xo_ps", i, t + 1))
                    dve.tensor_tensor(xcur[:, t, :], ps[:, 2 + t % 2, :], xcur[:, t, :], ALU.add).then_inc(sems["x2"], 1)

                def ffn_stats(t):
                    dve.wait_ge(sems["x2"], at("x2", i, t + 1))
                    ln_stats(8 + t, xcur[:, t, :])

                def ffn_ln(t):
                    ln_normalise(8 + t, xcur[:, t, :])

                def scales(s, t, src, c, weights):
                    if src is not None:
                        step(dve.tensor_reduce(s[:, t, 0:1], src, AX.X, ALU.max, apply_absolute_value=True))
                        settle()
                    step(dve.tensor_scalar(s[:, t, 1:2], s[:, t, 0:1], c, EPS, ALU.mult, ALU.max))
                    settle()
                    step(dve.reciprocal(s[:, t, 4:5], s[:, t, 1:2]))
                    for k, w in enumerate(weights):
                        step(dve.tensor_scalar(s[:, t, 5 + k:6 + k], s[:, t, 1:2], wsc[:, w:w + 1],
                                               (0.5 if w == 0 else 1.0) / 127.0, ALU.mult, ALU.mult))
                    settle()
                    if len(weights) == 2:
                        step(dve.tensor_copy(s[:, t, 3:4], s[:, t, 5:6]))
                        step(dve.tensor_tensor(s[:, t, 7:8], s[:, t, 5:6], s[:, t, 6:7], ALU.mult))
                    return dve.tensor_scalar(s[:, t, 2:3], s[:, t, 4:5], 127.0 * c, None, ALU.mult)

                def ffn_scales(t):
                    dve.wait_ge(sems["had_ps"], at("had_ps", i, t + 1))
                    scales(fs, t, ps[:, ROT_BANK[t], :], C512, (0, 1)).then_inc(sems["fsc"], 1)

                def ffn_int(t):
                    dve.wait_ge(sems["fround"], at("fround", i, t + 1))
                    if t:
                        dve.wait_ge(sems["fintT_ps"], at("fintT_ps", i, t))
                    dve.tensor_scalar(fq[:, :], fv[:, :], MAGIC, None, ALU.subtract).then_inc(sems["fint"], 1)

                def ffn_xt_low(t):
                    dve.wait_ge(sems["xt"], at("xt", i, 8 + t + 1))
                    dve.tensor_tensor(xT3_lo[:, :, :].rearrange("p c q -> p (c q)"), ps[:, XT_BANK[t], :],
                                      xT3[:, :, :].bitcast(F32).rearrange("p c q -> p (c q)"), ALU.subtract
                                      ).then_inc(sems["xt_lo"], 1)

                def ffn_hidT_low(t):
                    for g in range(FG):
                        dve.wait_ge(sems["hidT"], at("hidT", i, FG * t + g + 1))
                        hi = hidT[:, 4 * g:4 * g + 4, :].bitcast(F32).rearrange("p c q -> p (c q)")
                        dve.tensor_tensor(hidT_lo[:, 4 * g:4 * g + 4, :].rearrange("p c q -> p (c q)"),
                                          ps[:, HT_BANK[t] + g % 2, :], hi, ALU.subtract).then_inc(sems["hidT_lo"], 1)

                def ffn_hidden(t):
                    if t > 1:
                        dve.wait_ge(sems["hidT_ps"], at("hidT_ps", i, FG * (t - 1)))
                    elif t == 1:
                        dve.wait_ge(sems["sc_ps"], at("sc_ps", i, NT))

                    def second(g):
                        dve.wait_ge(sems["gated"], at("gated", i, FG * t + g + 1))
                        dve.wait_ge(sems["up_ps"], at("up_ps", i, FG * t + g + 1))
                        dve.scalar_tensor_tensor(hid[t % 2][:, g, :], gw[:, g % 2, :], fs[:, t, 7:8],
                                                 ps[:, GU_BANK[t][g] + 1, :], ALU.mult, ALU.mult).then_inc(sems["hid"], 1)

                    for g in range(FG):
                        n = FG * t + g
                        dve.wait_ge(sems["th"], at("th", i, n + 1))
                        dve.wait_ge(sems["hid"], at("hid", i, n - 1))
                        dve.scalar_tensor_tensor(gw[:, g % 2, :], th[:, n % 2, :], 1.0, ps[:, GU_BANK[t][g], :],
                                                 ALU.add, ALU.mult).then_inc(sems["gated"], 1)
                        if g:
                            second(g - 1)
                    second(FG - 1)

                def ffn_sum1(t):
                    dve.wait_ge(sems["hid"], at("hid", i, FG * t + FG))
                    if t:
                        dve.wait_ge(sems["diff2"], at("diff2", i, t))
                    a = hid[t % 2][:, :, :].rearrange("p (r u) n -> p r u n", u=2)
                    dve.tensor_tensor(sd[:, 0, :, :], a[:, :, 0, :], a[:, :, 1, :], ALU.add).then_inc(sems["sum1"], 1)

                def ffn_sum2(t):
                    dve.wait_ge(sems["sum1"], at("sum1", i, t + 1))
                    dve.wait_ge(sems["diff1"], at("diff1", i, t + 1))
                    dve.tensor_tensor(hid[t % 2][:, 0:2, :], sd[:, :, 0, :], sd[:, :, 1, :], ALU.add).then_inc(sems["sum2"], 1)

                def ffn_scales2(t):
                    for g in range(FG):
                        dve.wait_ge(sems["had2_ps"], at("had2_ps", i, FG * t + g + 1))
                        step(dve.tensor_reduce(gmax[:, t, g:g + 1], ps[:, 4 + g, :], AX.X, ALU.max,
                                               apply_absolute_value=True))
                    settle()
                    step(dve.tensor_reduce(f2s[:, t, 0:1], gmax[:, t, :], AX.X, ALU.max))
                    settle()
                    scales(f2s, t, None, C2048, (2,)).then_inc(sems["f2sc"], 1)

                def ffn_int2(t):
                    for half in range(2):
                        dve.wait_ge(sems["f2round"], at("f2round", i, 2 * t + half + 1))
                        if t and half == 0:
                            dve.wait_ge(sems["f2intT_ps"], at("f2intT_ps", i, 2 * t))
                        cols = slice(1024 * half, 1024 * half + 1024)
                        b0 = 4 + 2 * half
                        dve.tensor_scalar(f2q[:, cols], ps[:, b0:b0 + 2, :].rearrange("p b q -> p (b q)"), MAGIC, None,
                                          ALU.subtract).then_inc(sems["f2int"], 1)

                def ffn_out(t):
                    dve.wait_ge(sems["down_ps"], at("down_ps", i, t + 1))
                    dve.scalar_tensor_tensor(xcur[:, t, :], ps[:, DOWN_BANK[t], :], f2s[:, t, 5:6], xcur[:, t, :],
                                             ALU.mult, ALU.add).then_inc(sems["y"], 1)

                rotate_queries(0)
                mask_and_centre(0)
                mask_and_centre(1)
                denominators(0)
                rotate_queries(1)
                denominators(1)
                mask_and_centre(2)
                residual2(0)
                ffn_stats(0)
                denominators(2)
                ffn_ln(0)
                mask_and_centre(3)
                residual2(1)
                ffn_stats(1)
                denominators(3)
                ffn_xt_low(0)
                ffn_ln(1)
                residual2(2)
                ffn_scales(0)
                ffn_int(0)
                ffn_xt_low(1)
                residual2(3)
                ffn_stats(2)
                ffn_stats(3)
                ffn_scales(1)
                ffn_int(1)
                ffn_ln(2)
                ffn_hidden(0)
                ffn_xt_low(2)
                ffn_sum1(0)
                ffn_scales(2)
                ffn_int(2)
                ffn_sum2(0)
                ffn_hidden(1)
                ffn_sum1(1)
                ffn_hidT_low(0)
                for t in range(NT):
                    if t + 1 < NT:
                        ffn_sum2(t + 1)
                    if t + 3 < NT:
                        ffn_ln(t + 3)
                    ffn_scales2(t)
                    if t + 3 < NT:
                        ffn_xt_low(t + 3)
                    if t + 1 < NT:
                        ffn_hidT_low(t + 1)
                    if t == 2:
                        ln_normalise(2, xin[:, 2, :], 1)
                        ln_normalise(3, xin[:, 3, :], 1)
                    ffn_int2(t)
                    if t == 3:
                        for j in range(2):
                            rotate(j, 1)
                            combine(j, 1)
                            low_parts(j, 1)
                    if t + 3 < NT:
                        ffn_scales(t + 3)
                        ffn_int(t + 3)
                    if t + 2 < NT:
                        ffn_hidden(t + 2)
                        ffn_sum1(t + 2)
                    ffn_out(t)
                    if t == 0:
                        first_stats(1)
                    elif t == 1:
                        ln_normalise(0, xin[:, 0, :], 1)
                        ln_normalise(1, xin[:, 1, :], 1)
                assert steps[0] - steps_before == PER["dve_step"], steps

        @block.gpsimd
        def _(pool):
            pool.memset(mhalf[:, :], -0.5).then_inc(sems["pool_step"], 1)
            pool.memset(ones[:, :], 1.0).then_inc(p_const, 1)
            pool.memset(kd_all[:, :, :, :], 0.0).then_inc(p_kzero, 1)
            pool.wait_ge(ffn_done, 1)
            pool.memset(vw[:, :, :], 0.0).then_inc(vw_zero, 1)
            pool.wait_ge(vw_zero, 1)
            pool.memset(vw[:, :, 0:G * P].rearrange("p t (g c) -> p t g c", c=P)[:, :, :, 96:128], 1.0).then_inc(vw_const, 1)
            i = 0
            steps = [1]

            def step(ins):
                steps[0] += 1
                ins.then_inc(sems["pool_step"], 1)

            def settle():
                pool.wait_ge(sems["pool_step"], at("pool_step", i, steps[0]))
                apart(pool)

            def rsqrt(n, ahead=0):
                pool.wait_ge(sems["mv"], at("mv", i, 12 * ahead + n + 1))
                apart(pool)
                step(pool.tensor_scalar(vare[:, n:n + 1], mv[:, n, 1:2], EPS, None, ALU.add))
                settle()
                pool.tensor_tensor(rstd[:, n:n + 1], vare[:, n:n + 1], mhalf[:, :], ALU.pow).then_inc(sems["rstd"], 1)

            for t in range(NT):
                rsqrt(t)
            steps_before = steps[0]

            with pool.Fori(0, B) as i:
                steps[0] = steps_before
                pool.wait_ge(sems["rope_m"], at("rope_m", i, 12))
                apart(pool)
                pool.tensor_tensor(rot[:, 0, :], rot[:, 0, :], rot[:, 1, :], ALU.subtract).then_inc(sems["rope_c"], 1)
                pool.tensor_tensor(rot[:, 2, :], rot[:, 2, :], rot[:, 3, :], ALU.add).then_inc(sems["rope_c"], 1)

                pool.wait_ge(sems["hidT_ps"], at("hidT_ps", i, 0))
                pool.wait_ge(sems["rope_c"], at("rope_c", i, 2))
                apart(pool)
                pool.memset(ks[96:98, :, :].bitcast(F32), 1.0).then_inc(sems["ks_ones"], 1)
                pool.wait_ge(sems["ks_ones"], at("ks_ones", i, 1))
                apart(pool)
                pool.wait_ge(sems["seg_in"], at("seg_in", i, 16))
                pool.wait_ge(sems["masked"], at("masked", i, 0))
                apart(pool)
                step(pool.tensor_copy(seg_f[:, :], seg_i[:, :]))
                settle()
                step(pool.tensor_scalar(seg_8[:, :], seg_f[:, :], -8.0, None, ALU.add))
                settle()
                for t in range(NT):
                    pool.tensor_scalar(maskt[:, t, :], iota_sb[:, :], seg_f[:, t:t + 1], NEG, ALU.is_gt, ALU.mult)
                    step(pool.tensor_scalar(mask_lo[:, :], iota_sb[:, :], seg_8[:, t:t + 1], NEG, ALU.is_lt, ALU.mult))
                    settle()
                    last = pool.tensor_tensor(maskt[:, t, :], maskt[:, t, :], mask_lo[:, :], ALU.add)
                    if t < NT - 1:
                        step(last)
                        settle()
                last.then_inc(sems["maskt"], 1)
                for t in range(NT):
                    rsqrt(4 + t)

                def normalise(t):
                    pool.wait_ge(sems["xden"], at("xden", i, t + 1))
                    apart(pool)
                    e = ex[:, t % 2, :, :]
                    pool.tensor_tensor(e, e, xrec[:, t, :].unsqueeze(2).broadcast_to([P, H, LK]), ALU.mult
                                       ).then_inc(sems["xprob"], 1)

                for t in range(3):
                    normalise(t)
                rsqrt(8)
                normalise(3)
                for t in range(1, NT):
                    rsqrt(8 + t)

                def differences(t):
                    pool.wait_ge(sems["hid"], at("hid", i, FG * t + FG))
                    if t:
                        pool.wait_ge(sems["sum2"], at("sum2", i, t))
                    pool.wait_ge(sems["diff2"], at("diff2", i, t))
                    apart(pool)
                    a = hid[t % 2][:, :, :].rearrange("p (r u) n -> p r u n", u=2)
                    pool.tensor_tensor(sd[:, 1, :, :], a[:, :, 0, :], a[:, :, 1, :], ALU.subtract).then_inc(sems["diff1"], 1)
                    pool.wait_ge(sems["sum1"], at("sum1", i, t + 1))
                    pool.wait_ge(sems["diff1"], at("diff1", i, t + 1))
                    apart(pool)
                    pool.tensor_tensor(hid[t % 2][:, 2:4, :], sd[:, :, 0, :], sd[:, :, 1, :], ALU.subtract).then_inc(sems["diff2"], 1)

                for t in range(NT):
                    differences(t)
                    if t == 2:
                        for n in range(NT):
                            rsqrt(n, 1)
                assert steps[0] - steps_before == PER["pool_step"], steps


MAX_AT = {j: (20 + j,) for j in range(12)}
MAX_JOBS = [(8 * (n // 16) + 2 * (n % 4), (n % 16) // 4, 2 * (n % 3) if n < 16 else 2 + 2 * (n % 2) if n < 20 else 0) for n in range(32)]
XT_BANK = [4, 6, 2, 0]
ROT_BANK = [5, 7, 3, 1]
INT_BANK = [4, 0, 0, 0]
GU_BANK = [[0, 2, 4, 6], [4, 6, 0, 2], [2, 4, 6, 0], [0, 2, 4, 6]]
HT_BANK = [4, 2, 2, 2]
DOWN_BANK = [2, 0, 0, 0]
V0 = 3 + 2 * H
A0 = V0 + 4 * H
NJOBS = A0 + 2 * H


def _jobs():
    jobs, count = [], {"act": 0, "dve": 0}
    for n in range(NJOBS):
        if n == 0 or 3 <= n < 3 + H:
            s = "act"
        elif n in (1, 2) or 3 + H <= n < V0:
            s = "dve"
        elif n < A0:
            s = "dve" if (n - V0) % 2 else "act"
        else:
            s = "act" if (n - A0) % 2 else "dve"
        count[s] += 1
        jobs.append((s, count[s]))
    return jobs, count


PJOBS, _COUNT = _jobs()
NACT, NDVE = _COUNT["act"], _COUNT["dve"]
NN_DVE = PJOBS[V0 - 1][1]
PV_ACT = {m: PJOBS[V0 + m][1] for m in range(4 * H)}
PV_DVE = PV_ACT


def _tables(np):
    f = np.float32
    had = np.array([[1.0]], f)
    while had.shape[0] < D:
        had = np.block([[had, had], [had, -had]]).astype(f)
    inv = (f(1.0) / np.power(f(10000.0), np.arange(0, HD, 2, dtype=f) / f(HD))).astype(f)
    ang = (np.arange(S, dtype=f)[:, None] * inv[None, :]).T.astype(f)
    selfrope = np.stack([np.cos(ang), np.sin(ang)]).repeat(8, axis=1)
    inv2 = (f(1.0) / np.power(f(10000.0), np.arange(R // 2, dtype=f) / f(R // 2))).astype(f)
    ang2 = (np.arange(S, dtype=f)[:, None] * inv2[None, :]).T.astype(f)
    xrope = np.tile(np.stack([np.cos(ang2), np.sin(ang2)]), (1, 4, 1))
    rope = np.concatenate([selfrope, xrope]).transpose(1, 0, 2).astype(f)
    c, s = np.cos(ang2[:, :LK]), np.sin(ang2[:, :LK])
    krope = np.stack([np.concatenate([c, c]), np.concatenate([-s, s]), np.concatenate([s, s]),
                      np.concatenate([c, -c])])
    krope = np.tile(krope, (1, 2, 1)).transpose(1, 0, 2).astype(f)
    iota = np.tile(np.arange(LK, dtype=f), (P, 1))
    return dict(had=had, rope=rope, krope=krope, iota=iota, ident=np.eye(P, dtype=f))


def kernel(x, ctx_2048, itok_BxS_0_1023, L0_attn_wq, L0_attn_wk, L0_attn_wv, L0_attn_wo, L0_xattn_W_kvc,
           L0_xattn_W_dq, L0_xattn_W_uq, L0_xattn_W_qr, L0_xattn_W_uk, L0_xattn_W_kr, L0_xattn_W_uv,
           L0_xattn_W_o, L0_ffn_w_gate, L0_ffn_w_up, L0_ffn_w_down):
    import numpy as np
    import concourse.bacc as bacc
    from concourse.bass_utils import run_bass_kernel_spmd as run

    a = np.asarray
    wkr = a(L0_xattn_W_kr)
    swapped = np.concatenate([wkr[:, R // 2:], wkr[:, :R // 2]], axis=1)
    data = dict(
        x=a(x),
        seg=a(itok_BxS_0_1023).reshape(B, NT, P).transpose(0, 2, 1),
        ctxT=a(ctx_2048).reshape(B * LK, D).T,
        wq=a(L0_attn_wq).reshape(D, 2, 8, HD // 2, 2).transpose(0, 1, 4, 3, 2).reshape(D, D),
        wk=a(L0_attn_wk).reshape(D, G, HD // 2, 2).transpose(0, 3, 2, 1).reshape(D, G * HD),
        wv=a(L0_attn_wv), wo=a(L0_attn_wo), wkvc=a(L0_xattn_W_kvc), wdq=a(L0_xattn_W_dq),
        wuqT=a(L0_xattn_W_uq).T, wqr=a(L0_xattn_W_qr), wukT=a(L0_xattn_W_uk).T,
        wkr2=np.concatenate([wkr, wkr], axis=1), wkrs2=np.concatenate([swapped, swapped], axis=1),
        wuvT=a(L0_xattn_W_uv).T, wox=a(L0_xattn_W_o),
        gateT=a(L0_ffn_w_gate).T, upT=a(L0_ffn_w_up).T, downT=a(L0_ffn_w_down).T,
        **_tables(np),
    )
    nc = bacc.Bacc("TRN2", target_bir_lowering=False, num_devices=1)
    arrays, args = {}, {}
    for name, v in data.items():
        v = np.ascontiguousarray(v)
        arrays[f"in_{name}"] = v
        args[name] = nc.dram_tensor(f"in_{name}", v.shape, mybir.dt.from_np(v.dtype), kind="ExternalInput").ap()
    out = nc.dram_tensor("out_0", (B, S, D), F32, kind="ExternalOutput").ap()
    block_kernel(nc, out=out, **args)
    r = run(nc, [arrays], core_ids=[0])
    return r.results[0]["out_0"]
```

```python
from contextlib import ExitStack

import concourse.bass as bass
from concourse import mybir

P = 128
F32 = mybir.dt.float32
F32R = mybir.dt.float32r
BF16 = mybir.dt.bfloat16
F8 = mybir.dt.float8e4
I32 = mybir.dt.int32
ALU = mybir.AluOpType
ACT = mybir.ActivationFunctionType
AX = mybir.AxisListType

B, S, D = 8, 512, 512
NT = S // P
KC = D // P
H, G, HD = 16, 8, 32
LK, KVC, QC, R = 64, 128, 192, 64
QC1 = QC - P
HP = H // 2
F = 2048
FC = F // P
FG = F // 512
EPS = 1e-5
NEG = -1e30
MAGIC = 12582912.0
SELF_SCALE = float(HD) ** -0.5
X_SCALE = float(P + R) ** -0.5
C512 = float(D) ** -0.5
C2048 = float(F) ** -0.5
NCOPY = 6

PER = dict(
    x_in=16, seg_in=16, stack=3 * NCOPY * 16, rows_in=64, v_in=16, ak_in=48, store0=32, store1=32,
    mv=12, rstd=12, xn=12, xt_ps=12, xt=12,
    proj=6, v_ps=4, vw=4, rope_m=12, rope_cv=4, rope_c=2, rope_h=6, rope_l=6,
    smax_ps=32, smax=32, nms=2, nmt_ps=2, nmt=2,
    st_ps=32, probs=32, pv=16, at=8, wo_ps=4, x1=4,
    dq_ps=4, qc=4, xr_ps=16, xcs=16, sc_ps=4, masked=4, centred=4, xexp=4, xden=4, xprob=4,
    pt_ps=8, ptx=8, xo_ps=4, x2=4, maskt=1, ks_ones=1,
    had_ps=4, fsc=4, fround=4, fint=4, fintT_ps=4, fintT=4, gate_ps=16, up_ps=16, th=16, gated=16, hid=16,
    xt_lo=4, sum1=4, diff1=4, sum2=4, diff2=4, hidT_ps=16, hidT=16, hidT_lo=16, had2_ps=16, f2sc=4, f2round=8, f2int=8,
    f2intT_ps=8, f2intT=8, down_ps=4, y=4,
    dve_step=98, pool_step=21,
)


def block_kernel(nc, x, seg, ctxT, wq, wk, wv, wo, wkvc, wdq, wuqT, wqr, wukT, wkr2, wkrs2, wuvT, wox,
                 gateT, upT, downT, had, rope, krope, iota, ident, out):
    ctx = ExitStack()
    with ctx:
        base = 16512
        at_byte = [base]

        def place(name, shape, dt, offset=None):
            size = 1
            for n in shape[1:]:
                size *= n
            size *= {F32: 4, F32R: 4, I32: 4, BF16: 2, F8: 1}[dt]
            if offset is None:
                offset = at_byte[0]
                at_byte[0] += (size + 31) // 32 * 32
            return nc.alloc_sbuf_tensor_at(name, shape, dt, offset=offset)

        wq_sb = place("wq_sb", [P, KC, D], F32)
        wk_sb = place("wk_sb", [P, KC, G * HD], F32)
        wv_sb = place("wv_sb", [P, KC, G * HD], F32)
        wo_sb = place("wo_sb", [P, KC, D], F32)
        wdq_sb = place("wdq_sb", [P, KC, QC], F32)
        wqr0 = place("wqr0", [P, H * R], F32)
        wqr1 = place("wqr1", [QC1, H * R], F32)
        had_sb = place("had_sb", [P, KC, D], F32R)
        gate_w = place("gate_w", [P, KC, F], F8)
        up_w = place("up_w", [P, KC, F], F8)
        down_w = place("down_w", [P, FC, D], F8)
        rope_at = at_byte[0]
        rope_sb = place("rope_sb", [P, 4, S], F32)
        ident_f = place("ident_f", [P, P], F32)
        ident_b = place("ident_b", [P, P], BF16)
        iota_sb = place("iota_sb", [P, LK], F32)
        ones_at = at_byte[0]
        maskt = place("maskt", [P, NT, LK], F32)
        mask_lo = place("mask_lo", [P, LK], F32)
        xcur_at = at_byte[0]
        xcur = place("xcur", [P, NT, D], F32)
        had_in = place("had_in", [P, KC, D], F32, xcur_at)
        xin_at = at_byte[0]
        xin = place("xin", [P, NT, D], F32)
        seg_i = place("seg_i", [P, NT], I32)
        seg_f = place("seg_f", [P, NT], F32)
        seg_8 = place("seg_8", [P, NT], F32)
        stats = place("stats", [P, 12, 6], F32)
        mv = place("mv", [P, 12, 2], F32)
        vare = place("vare", [P, 12], F32)
        rstd = place("rstd", [P, 12], F32)
        mhalf = place("mhalf", [P, 1], F32)
        negmax = place("negmax", [P, NT, H], F32)
        negsplit = place("negsplit", [P, 2, NT, H], F32R)
        xmax = place("xmax", [P, NT, H], F32)
        xsum = place("xsum", [P, NT, H], F32)
        xrec = place("xrec", [P, NT, H], F32)
        fs = place("fs", [P, NT, 8], F32)
        f2s = place("f2s", [P, NT, 8], F32)
        gmax = place("gmax", [P, NT, FG], F32)
        wsum = place("wsum", [P, 3], F32)
        wsc = place("wsc", [P, 3], F32)
        wthr = place("wthr", [P, 6], F32)
        ones = place("ones", [P, P], F32, ones_at)
        arena = at_byte[0]
        A_ROPE, A_Q = arena, arena + 16384
        A_K = A_Q + 32768
        A_V = A_K + 16384
        A_P = A_V + 4 * (G * P + 32) * 4
        A_XT = A_P + 16384
        A_XN = A_XT + 8192
        A_RC = A_XN + 4096
        assert A_RC + 2048 <= 229344, A_RC + 2048 - 229344

        rot = place("rot", [P, 4, S], F32, A_ROPE)
        parts = place("parts", [P, 4, S], F32R, A_ROPE + 8192)
        qs = place("qs", [P, H, S], F32R, A_Q)
        ks = place("ks", [P, G, S], F32R, A_K)
        vw = place("vw", [P, NT, G * P + 32], F32, A_V)
        pt = place("pt", [P, 4, 1024], F32, A_P)
        rcp = place("rcp", [64, S], F32, A_RC)
        xT = place("xT", [P, KC, S], F32, A_XT)
        aT = place("aT", [P, KC, S], F32, A_XT)
        xn = place("xn", [P, 2, D], F32, A_XN)
        rows = place("rows", [H, S], F32R, A_XN)
        vp = place("vp", [P, HP, D], F32, A_ROPE)
        xc = place("xc", [P, HP, 256], F32, A_Q)
        xs = place("xs", [P, HP, 256], F32, A_Q + 8192)
        ex = place("ex", [P, 2, H, LK], F32, A_Q + 16384)
        ptx = place("ptx", [P, HP, P], F32, A_Q + 24576)
        qc0 = place("qc0", [P, S], F32, A_Q + 28672)
        qc1 = place("qc1", [QC1, S], F32, A_Q + 30720)
        ak0 = place("ak0", [P, H * LK], F32, A_K)
        ak1 = place("ak1", [QC1, H * LK], F32, A_K + 4096)
        kd = place("kd", [P, 2, P], F32, A_K + 8192)
        xT3 = place("xT3", [P, KC, P], F32R, A_K + 9216)
        xT3_lo = place("xT3_lo", [P, KC, P], F32R, A_RC)
        fv = place("fv", [P, D], F32, A_K + 11264)
        fq = place("fq", [P, D], BF16, A_K + 13312)
        fqT = place("fqT", [P, KC, P], BF16, A_K + 14336)
        hid = [place(f"hid{n}", [P, FG, 512], F32, (A_P, A_K)[n]) for n in range(2)]
        sd = place("sd", [P, 2, 2, 512], F32, A_P + 8192)
        th = place("th", [P, 2, 512], F32, A_Q + 8192)
        gw = place("gw", [P, 2, 512], F32, A_Q + 12288)
        hidT = place("hidT", [P, FC, P], F32R, A_Q)
        hidT_lo = place("hidT_lo", [P, FC, P], F32R, A_Q + 16384)
        f2q = place("f2q", [P, F], BF16, A_Q + 24576)
        f2qT = place("f2qT", [P, FC, P], BF16, A_Q + 28672)
        wox_sb = place("wox_sb", [P, H, D], F32, arena)
        nn = place("nn", [P, H, D], F32, arena + 32768)
        wukT_sb = place("wukT_sb", [P, H, KVC], F32, arena + 65536)
        wuqT_sb = place("wuqT_sb", [P, H, QC], F32, arena + 73728)
        wuvT_sb = place("wuvT_sb", [P, H, KVC], F32, arena + 86016)
        mt = place("mt", [P, H, QC], F32, arena + 98304)
        kd_all = place("kd_all", [P, B, 2, P], F32, rope_at)
        ast0 = place("ast0", [P, B, H, LK], F32, arena + 65536)
        ast1 = place("ast1", [QC1, B, H, LK], F32, arena + 32768)
        vst = place("vst", [P, 4, D], F32, xcur_at)
        ktmp = place("ktmp", [P, 4, D], F32, arena + 32768)
        ctxT_sb = place("ctxT_sb", [P, KC, D], F32, xcur_at)
        wkvc_sb = place("wkvc_sb", [P, KC, KVC], F32, xin_at)
        kvT = place("kvT", [P, B * LK], F32, base + 40960)
        wkr_sb = place("wkr_sb", [P, 2, P], F32, xin_at + 4096)
        krope_sb = place("krope_sb", [P, 4, LK], F32, xin_at + 5120)
        wst = [place(f"wst{n}", [P, KC * F], F32, arena if n == 1 else base) for n in range(3)]
        wlow = place("wlow", [P, KC * F], F8, base + 32768)

        ps = ctx.enter_context(nc.psum_tensor("ps", [P, 8, 512], F32))

        v_dram = nc.dram_tensor("v_scratch", [B, H, LK, D], F32, kind="Internal").ap()
        a0_dram = nc.dram_tensor("a0_scratch", [B, P, H * LK], F32, kind="Internal").ap()
        a1_dram = nc.dram_tensor("a1_scratch", [B, QC1, H * LK], F32, kind="Internal").ap()
        k_dram = nc.dram_tensor("k_scratch", [B, P, 2 * P], F32, kind="Internal").ap()

        sems = {n: ctx.enter_context(nc.semaphore(n)) for n in PER}

        def psem(name):
            return ctx.enter_context(nc.semaphore(name))

        in_ctx, in_mt, in_nn, in_qkv, in_weights = (psem(n) for n in ("in_ctx", "in_mt", "in_nn", "in_qkv", "in_weights"))
        in_rope = psem("in_rope")
        in_ffn = [psem(f"in_ffn{n}") for n in range(3)]
        p_ps, p_act, p_dve, p_ffn_ps = psem("p_ps"), psem("p_act"), psem("p_dve"), psem("p_ffn_ps")
        p_vstore = [psem(f"p_vstore{n}") for n in range(4)]
        p_store = psem("p_store")
        ffn_step, p_const, kd_made = psem("ffn_step"), psem("p_const"), psem("kd_made")
        arena_free = psem("arena_free")
        p_kzero, ffn_done, vw_const, vw_zero = psem("p_kzero"), psem("ffn_done"), psem("vw_const"), psem("vw_zero")
        passed, in_had, had_ready = psem("passed"), psem("in_had"), psem("had_ready")

        def at(name, i, k):
            return i * PER[name] + (PER[name] + k)

        def apart(eng):
            eng.sem_inc(passed, 1)

        block = ctx.enter_context(nc.Block())

        @block.sync
        def _(sp):
            def load(sem, *pairs):
                for dst, src in pairs:
                    sp.dma_start(dst, src).then_inc(sem, 16)

            def load_ffn(n, quarter):
                w = (gateT, upT, downT)[n].rearrange("(c p) n -> p c n", p=P)
                c = slice(w.shape[1] // 4 * quarter, w.shape[1] // 4 * (quarter + 1))
                load(in_ffn[n], (wst[n][:, :].rearrange("p (c n) -> p c n", n=w.shape[2])[:, c, :], w[:, c, :]))

            load(in_ctx, (ctxT_sb[:, :, :], ctxT.rearrange("(c p) n -> p c n", p=P)),
                 (wkvc_sb[:, :, :], wkvc.rearrange("(c p) n -> p c n", p=P)),
                 (wkr_sb[:, 0, :], wkr2), (wkr_sb[:, 1, :], wkrs2), (krope_sb[:, :, :], krope), (ident_f[:, :], ident))
            load(in_mt, (wukT_sb[:, :, :], wukT.rearrange("(h p) n -> p h n", p=P)),
                 (wuqT_sb[:, :, :], wuqT.rearrange("(h p) n -> p h n", p=P)))
            load(in_nn, (wuvT_sb[:, :, :], wuvT.rearrange("(h p) n -> p h n", p=P)),
                 (wox_sb[:, :, :], wox.rearrange("(h p) n -> p h n", p=P)))
            for quarter in range(4):
                load_ffn(0, quarter)
            for name in PER:
                sp.sem_inc(sems[name], PER[name])
            sp.wait_ge(p_dve, 2)
            load(sems["x_in"], (xin[:, :, :], x[0, :, :].rearrange("(t p) d -> p t d", p=P)))
            sp.wait_ge(kd_made, 4)
            load(p_store, (k_dram.rearrange("b p n -> p b n"), kd_all[:, :, :, :].rearrange("p b t n -> p b (t n)")))
            sp.wait_ge(p_ps, V0)
            for n in range(4 * H):
                bp, h = n // H, n % H
                if n in (0, 6, 12, 18):
                    load_ffn(1, n // 6)
                sp.wait_ge(p_act, PV_ACT[n])
                sp.dma_start(v_dram[2 * bp:2 * bp + 2, h, :, :],
                             vst[:, n % 4, :]).then_inc(p_vstore[n % 4], 16)
                if n in (36, 42, 48, 54):
                    sp.wait_ge(ffn_step, 6)
                    load_ffn(2, n // 6 - 6)
            for g in range(4):
                sp.wait_ge(p_act, A_ACT[g])
                hk = slice(4 * LK * g, 4 * LK * (g + 1))
                load(p_store,
                     (a0_dram.rearrange("b p n -> p b n")[:, :, hk],
                      ast0[:, :, :, :].rearrange("p b h k -> p b (h k)")[:, :, hk]),
                     (a1_dram.rearrange("b p n -> p b n")[:, :, hk],
                      ast1[:, :, :, :].rearrange("p b h k -> p b (h k)")[:, :, hk]))
                if g == 2:
                    sp.wait_ge(ffn_done, 1)
                    load(in_qkv, (wk_sb[:, :, :], wk.rearrange("(c p) n -> p c n", p=P)),
                         (wq_sb[:, :, :], wq.rearrange("(c p) n -> p c n", p=P)),
                         (wv_sb[:, :, :], wv.rearrange("(c p) n -> p c n", p=P)), (iota_sb[:, :], iota))
            for n in range(4):
                sp.wait_ge(p_vstore[n], 16 * H)
            load(in_had, (had_in[:, :, :], had.rearrange("(c p) n -> p c n", p=P)))
            sp.wait_ge(p_store, 144)
            sp.sem_inc(arena_free, 1)
            load(in_rope, (rope_sb[:, :, :], rope))
            load(in_weights, (wo_sb[:, :, :], wo.rearrange("(c p) n -> p c n", p=P)),
                 (wdq_sb[:, :, :], wdq.rearrange("(c p) n -> p c n", p=P)),
                 (wqr0[:, :], wqr[0:P, :]), (wqr1[:, :], wqr[P:QC, :]))

            def stack(i, j, ahead=0):
                dst = ks[:, :, :] if j == 0 else qs[:, G * (j - 1):G * j, :]
                kinds = (0, 0, 1) if j == 0 else (0, 1, 0)
                for kind in range(2):
                    name = "rope_l" if kind else "rope_h"
                    sp.wait_ge(sems[name], at(name, i, ahead * 6 + 2 * j + 2))
                    for c in range(3):
                        if kinds[c] != kind:
                            continue
                        for odd in range(2):
                            r0 = 32 * c + 16 * odd
                            sp.dma_start(dst[r0:r0 + 16, :, :].bitcast(F32),
                                         parts[:, 2 * kind + odd, :].bitcast(F32)).then_inc(sems["stack"], 16)
            stack(0, 0)
            stack(0, 1)

            def batch_row(i, more):
                def row(t):
                    return t[bass.ds(i, 1)]
                sp.wait_ge(sems["maskt"], at("maskt", i, 0))
                apart(sp)
                sp.dma_start(seg_i[:, :], row(seg).rearrange("o p t -> (o p) t")).then_inc(sems["seg_in"], 16)
                sp.wait_ge(sems["y"], at("y", i, 0))
                apart(sp)
                stack(i, 2)
                for hg in range(2):
                    sp.wait_ge(sems["nmt"], at("nmt", i, hg + 1))
                    for part in range(2):
                        sp.dma_start(qs[96 + part:97 + part, 8 * hg:8 * hg + 8, :].bitcast(F32),
                                     rows[8 * part:8 * part + 8, :].bitcast(F32)).then_inc(sems["rows_in"], 16)
                    if hg == 0:
                        sp.wait_ge(sems["stack"], at("stack", i, PER["stack"]))
                        sp.dma_start(vp[:, :, :], row(v_dram).rearrange("o (c u) k n -> (o u k) c n", u=2)
                                     ).then_inc(sems["v_in"], 16)
                sp.wait_ge(sems["st_ps"], at("st_ps", i, PER["st_ps"]))
                sp.dma_start(ak0[:, :], row(a0_dram).rearrange("o p n -> (o p) n")).then_inc(sems["ak_in"], 16)
                sp.dma_start(ak1[:, :], row(a1_dram).rearrange("o p n -> (o p) n")).then_inc(sems["ak_in"], 16)
                sp.dma_start(kd[:, :, :].rearrange("p t n -> p (t n)"),
                             row(k_dram).rearrange("o p n -> (o p) n")).then_inc(sems["ak_in"], 16)
                sp.wait_ge(sems["x1"], at("x1", i, PER["x1"]))
                sp.dma_start(xin[:, :, :], x[bass.ds(i + 1 if more else i, 1)].rearrange("o (t p) d -> p (o t) d", p=P)
                             ).then_inc(sems["x_in"], 16)
                for t in range(NT):
                    if t == NT - 1:
                        sp.wait_ge(sems["hidT_ps"], at("hidT_ps", i, PER["hidT_ps"]))
                        apart(sp)
                        stack(i, 0, 1)
                        sp.wait_ge(sems["had2_ps"], at("had2_ps", i, PER["had2_ps"]))
                        apart(sp)
                        stack(i, 1, 1)
                    sp.wait_ge(sems["y"], at("y", i, t + 1))
                    sp.dma_start(out[bass.ds(i, 1), t * P:(t + 1) * P, :].rearrange("o p d -> (o p) d"),
                                 xcur[:, t, :]).then_inc(sems[f"store{t % 2}"], 16)

            with sp.Fori(0, B - 1) as i:
                batch_row(i, True)
            batch_row(B - 1, False)
            for n in range(2):
                sp.wait_ge(sems[f"store{n}"], at(f"store{n}", B, 0))

        @block.tensor
        def _(pe):
            def prologue_bank(n):
                if n >= PBANKS:
                    s, k = PJOBS[n - PBANKS]
                    pe.wait_ge(p_act if s == "act" else p_dve, k)
                return n % PBANKS

            def sum_ffn_weights(m):
                pe.wait_ge(ffn_step, 6 * m + 1)
                pe.matmul(ps[:, PBANKS, m:m + 1], ones[:, :], wsum[:, m:m + 1], start=True, stop=True).then_inc(p_ffn_ps, 1)

            pe.wait_ge(in_ctx, 96)
            n = 0
            b_ = prologue_bank(n)
            for c in range(KC):
                mm = pe.matmul(ps[:, b_, :], wkvc_sb[:, c, :], ctxT_sb[:, c, :], start=c == 0, stop=c == KC - 1)
            mm.then_inc(p_ps, 1)
            n += 1
            pe.wait_ge(p_act, 1)
            for s in range(2):
                pe.matmul(ps[:, prologue_bank(n), :], wkr_sb[:, s, :], kvT[:, :], start=True, stop=True).then_inc(p_ps, 1)
                n += 1
            pe.wait_ge(in_mt, 32)
            for h in range(H):
                pe.matmul(ps[:, prologue_bank(n), 0:QC], wukT_sb[:, h, :], wuqT_sb[:, h, :], start=True, stop=True
                          ).then_inc(p_ps, 1)
                n += 1
            pe.wait_ge(in_nn, 32)
            for h in range(H):
                pe.matmul(ps[:, prologue_bank(n), :], wuvT_sb[:, h, :], wox_sb[:, h, :], start=True, stop=True
                          ).then_inc(p_ps, 1)
                n += 1
            pe.wait_ge(p_act, NN_ACT)
            pe.wait_ge(p_const, 1)
            for m in range(4 * H):
                bp, h = m // H, m % H
                if m in (18, 48):
                    sum_ffn_weights(0 if m == 18 else 1)
                pe.matmul(ps[:, prologue_bank(n), :], kvT[:, bp * P:(bp + 1) * P], nn[:, h, :], start=True, stop=True
                          ).then_inc(p_ps, 1)
                n += 1
            for h in range(H):
                if h == 5:
                    sum_ffn_weights(2)
                pe.matmul(ps[:, prologue_bank(n), :], mt[:, h, 0:P], kvT[:, :], start=True, stop=True).then_inc(p_ps, 1)
                n += 1
                pe.matmul(ps[0:QC1, prologue_bank(n), :], mt[:, h, P:QC], kvT[:, :], start=True, stop=True).then_inc(p_ps, 1)
                n += 1
            pe.wait_ge(p_act, NACT)
            pe.wait_ge(in_qkv, 64)
            pe.wait_ge(ffn_done, 1)

            i = 0
            reader = {}

            def take(*banks):
                need = {}
                for b in banks:
                    if b in reader:
                        name, k = reader[b]
                        need[name] = max(need.get(name, k), k)
                for name, k in need.items():
                    pe.wait_ge(sems[name], at(name, i, k))

            def transposes_of_xn(n, b, ahead=0):
                pe.wait_ge(sems["xn"], at("xn", i, 12 * ahead + n + 1))
                take(b)
                for c in range(KC):
                    mm = pe.transpose(ps[:, b, c * P:(c + 1) * P], xn[:, n % 2, c * P:(c + 1) * P], ident_f[:, :])
                mm.then_inc(sems["xt_ps"], 1)
                reader[b] = ("xt", 12 * ahead + n + 1) if n < 8 else ("xt_lo", n - 7)

            def project(j, ahead=0):
                if j == 0:
                    pe.wait_ge(sems["xt"], at("xt", i, 12 * ahead + 4))
                for odd in range(2):
                    b = 2 + 2 * j + odd
                    take(b)
                    for c in range(KC):
                        w = wk_sb[:, c, odd * P:(odd + 1) * P] if j == 0 else \
                            wq_sb[:, c, (2 * j - 2 + odd) * P:(2 * j - 1 + odd) * P]
                        mm = pe.matmul(ps[:, b, :], w, xT[:, c, :], start=c == 0, stop=c == KC - 1)
                    mm.then_inc(sems["proj"], 1)
                    reader[b] = ("rope_m", 12 * ahead + 4 * j + 4)

            for t in range(NT):
                transposes_of_xn(t, t % 2)
            project(0)
            project(1)
            pe.wait_ge(vw_const, 1)
            pe.wait_ge(had_ready, 1)
            pe.wait_ge(in_weights, 64)

            with pe.Fori(0, B) as i:
                reader.clear()
                reader.update({0: ("y", 0), 1: ("y", 0), 2: ("rope_m", 4), 3: ("rope_m", 4),
                               4: ("rope_m", 8), 5: ("rope_m", 8), 6: ("f2int", 0), 7: ("f2int", 0)})

                def values(t):
                    b = 6 + t % 2
                    take(b)
                    for c in range(KC):
                        mm = pe.matmul(ps[:, b, 0:G * HD], xT[:, c, t * P:(t + 1) * P], wv_sb[:, c, :],
                                       start=c == 0, stop=c == KC - 1)
                    mm.then_inc(sems["v_ps"], 1)
                    reader[b] = ("vw", t + 1)

                def scores_for_max(n):
                    h, t, b0 = MAX_JOBS[n]
                    take(b0, b0 + 1)
                    for u in range(2):
                        mm = pe.matmul(ps[:, b0 + u, :], qs[0:96, h + u, t * P:(t + 1) * P], ks[0:96, h // 2, :],
                                       start=True, stop=True)
                        reader[b0 + u] = ("smax", n + 1)
                    mm.then_inc(sems["smax_ps"], 1)

                def maxima_to_rows(hg):
                    pe.wait_ge(sems["nms"], at("nms", i, hg + 1))
                    take(0)
                    for t in range(NT):
                        mm = pe.transpose(ps[0:H, 0, t * P:(t + 1) * P], negsplit[:, hg, t, :].bitcast(F32), ident_f[:, :])
                    mm.then_inc(sems["nmt_ps"], 1)
                    reader[0] = ("nmt", hg + 1)

                project(2)
                pe.wait_ge(sems["stack"], at("stack", i, 2 * NCOPY * 16))
                for n in range(16):
                    scores_for_max(n)
                    if n in (8, 12):
                        values((n - 8) // 4)
                pe.wait_ge(sems["stack"], at("stack", i, PER["stack"]))
                scores_for_max(16)
                scores_for_max(17)
                maxima_to_rows(0)
                values(2)
                scores_for_max(18)
                scores_for_max(19)
                values(3)

                def scores(j):
                    h, half = j // 2, j % 2
                    b0 = 2 + 2 * (j % 2)
                    take(b0, b0 + 1)
                    for u in range(2):
                        kt = 2 * half + u
                        mm = pe.matmul(ps[:, b0 + u, :], ks[0:98, h // 2, kt * P:(kt + 1) * P], qs[0:98, h, :],
                                       start=True, stop=True)
                        reader[b0 + u] = ("probs", j + 1)
                    mm.then_inc(sems["st_ps"], 1)

                def weigh(j):
                    h, half = j // 2, j % 2
                    b = 6 + (h // 2) % 2
                    pe.wait_ge(sems["probs"], at("probs", i, j + 1))
                    if j % 4 == 0:
                        take(b)
                    lo = (h // 2) * P + (0 if h % 2 else 32)
                    for u in range(2):
                        kt = 2 * half + u
                        mm = pe.matmul(ps[:, b, :], vw[:, kt, lo:lo + P], pt[:, j % 4, u * 512:(u + 1) * 512],
                                       start=j % 4 == 0 and u == 0, stop=j % 4 == 3 and u == 1)
                    if half:
                        mm.then_inc(sems["pv"], 1)
                    reader[b] = ("at", h // 2 + 1)

                pe.wait_ge(sems["rows_in"], at("rows_in", i, 32))
                pe.wait_ge(sems["ks_ones"], at("ks_ones", i, 1))
                pe.wait_ge(sems["vw"], at("vw", i, 4))
                scores(0)
                for j in range(2 * H):
                    if j + 1 == H:
                        pe.wait_ge(sems["rows_in"], at("rows_in", i, 64))
                    if j + 1 < 2 * H:
                        scores(j + 1)
                    for n in MAX_AT.get(j, ()):
                        scores_for_max(n)
                    if j == 12:
                        maxima_to_rows(1)
                    weigh(j)

                def project_out(t, chunks):
                    take(t)
                    for c in chunks:
                        mm = pe.matmul(ps[:, t, :], aT[:, c, t * P:(t + 1) * P], wo_sb[:, c, :],
                                       start=c == 0, stop=c == KC - 1)
                    if KC - 1 in chunks:
                        mm.then_inc(sems["wo_ps"], 1)
                        reader[t] = ("x1", t + 1)
                    else:
                        reader.pop(t, None)

                pe.wait_ge(sems["at"], at("at", i, HP - 2))
                for t in range(2):
                    project_out(t, range(KC - 1))
                pe.wait_ge(sems["at"], at("at", i, HP))
                for t in range(2):
                    project_out(t, (KC - 1,))
                for t in range(2, NT):
                    project_out(t, range(KC))

                def latent_queries(half):
                    pe.wait_ge(sems["xt"], at("xt", i, 4 + 2 * half + 2))
                    for m, (lo, hi) in enumerate(((0, P), (P, QC))):
                        take(6 + m)
                        for c in range(KC):
                            mm = pe.matmul(ps[0:hi - lo, 6 + m, 0:256], wdq_sb[:, c, lo:hi],
                                           xT[:, c, 256 * half:256 * half + 256], start=c == 0, stop=c == KC - 1)
                        mm.then_inc(sems["dq_ps"], 1)
                        reader[6 + m] = ("qc", 2 * half + m + 1)

                transposes_of_xn(4, 4)
                transposes_of_xn(5, 5)
                latent_queries(0)
                transposes_of_xn(6, 4)
                transposes_of_xn(7, 5)

                def rope_queries(half):
                    pe.wait_ge(sems["qc"], at("qc", i, 2 * half + 2))
                    for p in range(HP):
                        m = HP * half + p
                        b = m % 4
                        take(b)
                        q = slice(256 * half, 256 * half + 256)
                        pe.matmul(ps[:, b, 0:256], wqr0[:, p * P:(p + 1) * P], qc0[:, q], start=True, stop=False)
                        pe.matmul(ps[:, b, 0:256], wqr1[:, p * P:(p + 1) * P], qc1[:, q], start=False, stop=True
                                  ).then_inc(sems["xr_ps"], 1)
                        reader[b] = ("xcs", m + 1)

                def cross_scores(t):
                    pe.wait_ge(sems["xcs"], at("xcs", i, HP * (t // 2 + 1)))
                    q = slice(t * P, t * P + P)
                    ql = slice((t % 2) * P, (t % 2) * P + P)
                    for hb in range(2):
                        b = 4 + 2 * (t % 2) + hb
                        take(b)
                        cols = slice(512 * hb, 512 * hb + 512)
                        pe.matmul(ps[:, b, :], qc0[:, q], ak0[:, cols], start=True, stop=False)
                        pe.matmul(ps[:, b, :], qc1[:, q], ak1[:, cols], start=False, stop=False)
                        for u in range(4):
                            p = 4 * hb + u
                            pe.matmul(ps[:, b, u * P:(u + 1) * P], xc[:, p, ql], kd[:, 0, :], start=False, stop=False)
                            mm = pe.matmul(ps[:, b, u * P:(u + 1) * P], xs[:, p, ql], kd[:, 1, :],
                                           start=False, stop=u == 3)
                        reader[b] = ("masked", t + 1)
                    mm.then_inc(sems["sc_ps"], 1)

                def cross_transposes(t):
                    pe.wait_ge(sems["xprob"], at("xprob", i, t + 1))
                    for hb in range(2):
                        take(hb)
                        for u in range(4):
                            p = 4 * hb + u
                            mm = pe.transpose(ps[:, hb, u * P:(u + 1) * P],
                                              ex[:, t % 2, 2 * p:2 * p + 2, :].rearrange("p h k -> p (h k)"), ident_f[:, :])
                        mm.then_inc(sems["pt_ps"], 1)
                        reader[hb] = ("ptx", 2 * t + hb + 1)

                def cross_out(t):
                    b = 2 + t % 2
                    take(b)
                    pe.wait_ge(sems["ptx"], at("ptx", i, 2 * t + 2))
                    for p in range(HP):
                        mm = pe.matmul(ps[:, b, :], ptx[:, p, :], vp[:, p, :], start=p == 0, stop=p == HP - 1)
                    mm.then_inc(sems["xo_ps"], 1)
                    reader[b] = ("x2", t + 1)

                def ffn_rotate(t):
                    b = ROT_BANK[t]
                    take(b)
                    pe.wait_ge(sems["xt"], at("xt", i, 8 + t + 1))
                    pe.wait_ge(sems["xt_lo"], at("xt_lo", i, t + 1))
                    for c in range(KC):
                        pe.matmul(ps[:, b, :], xT3[:, c, :], had_sb[:, c, :], start=c == 0, stop=False)
                        mm = pe.matmul(ps[:, b, :], xT3_lo[:, c, :], had_sb[:, c, :], start=False, stop=c == KC - 1)
                    mm.then_inc(sems["had_ps"], 1)
                    reader[b] = ("fround", t + 1)

                def ffn_integers(t):
                    b = INT_BANK[t]
                    take(b)
                    pe.wait_ge(sems["fint"], at("fint", i, t + 1))
                    for c in range(KC):
                        mm = pe.transpose(ps[:, b, :].bitcast(BF16)[:, c * P:(c + 1) * P], fq[:, c * P:(c + 1) * P],
                                          ident_b[:, :])
                    mm.then_inc(sems["fintT_ps"], 1)
                    reader[b] = ("fintT", t + 1)

                def ffn_gate_up(t):
                    pe.wait_ge(sems["fintT"], at("fintT", i, t + 1))
                    for g in range(FG):
                        n = FG * t + g + 1
                        for b, w, sem, user in ((GU_BANK[t][g], gate_w, "gate_ps", "gated"),
                                                (GU_BANK[t][g] + 1, up_w, "up_ps", "hid")):
                            take(b)
                            apart(pe)
                            for c in range(KC):
                                mm = pe.matmul(ps[:, b, :], fqT[:, c, :], w[:, c, g * 512:(g + 1) * 512],
                                               start=c == 0, stop=c == KC - 1)
                            mm.then_inc(sems[sem], 1)
                            reader[b] = (user, n)

                def ffn_hidden_transposes(t):
                    pe.wait_ge(sems["sum2"], at("sum2", i, t + 1))
                    pe.wait_ge(sems["diff2"], at("diff2", i, t + 1))
                    for g in range(FG):
                        b = HT_BANK[t][g]
                        take(b)
                        for c in range(4):
                            mm = pe.transpose(ps[:, b, c * P:(c + 1) * P], hid[t % 2][:, g, c * P:(c + 1) * P], ident_f[:, :])
                        mm.then_inc(sems["hidT_ps"], 1)
                        reader[b] = ("hidT_lo", FG * t + g + 1)

                def ffn_hidden_rotate(t):
                    for g in range(FG):
                        take(4 + g)
                        pe.wait_ge(sems["hidT"], at("hidT", i, FG * t + g + 1))
                        pe.wait_ge(sems["hidT_lo"], at("hidT_lo", i, FG * t + g + 1))
                        for c in range(4):
                            pe.matmul(ps[:, 4 + g, :], hidT[:, 4 * g + c, :], had_sb[:, c, :], start=c == 0, stop=False)
                            mm = pe.matmul(ps[:, 4 + g, :], hidT_lo[:, 4 * g + c, :], had_sb[:, c, :],
                                           start=False, stop=c == 3)
                        mm.then_inc(sems["had2_ps"], 1)
                        reader[4 + g] = ("f2int", 2 * t + g // 2 + 1)

                def ffn_down(t):
                    b0 = DOWN_BANK[t]
                    for half in range(2):
                        b = b0 + half
                        take(b)
                        pe.wait_ge(sems["f2int"], at("f2int", i, 2 * t + half + 1))
                        for c in range(8):
                            k = 8 * half + c
                            mm = pe.transpose(ps[:, b, :].bitcast(BF16)[:, c * P:(c + 1) * P],
                                              f2q[:, k * P:(k + 1) * P], ident_b[:, :])
                        mm.then_inc(sems["f2intT_ps"], 1)
                        reader[b] = ("f2intT", 2 * t + half + 1)
                    for half in range(2):
                        pe.wait_ge(sems["f2intT"], at("f2intT", i, 2 * t + half + 1))
                        apart(pe)
                        for c in range(8):
                            k = 8 * half + c
                            mm = pe.matmul(ps[:, b0, :], f2qT[:, k, :], down_w[:, k, :], start=k == 0, stop=k == FC - 1)
                    mm.then_inc(sems["down_ps"], 1)
                    reader[b0] = ("y", t + 1)

                rope_queries(0)
                latent_queries(1)
                pe.wait_ge(sems["ak_in"], at("ak_in", i, 48))
                cross_scores(0)
                cross_scores(1)
                rope_queries(1)
                pe.wait_ge(sems["v_in"], at("v_in", i, 16))
                cross_scores(2)
                cross_transposes(0)
                cross_scores(3)
                cross_out(0)
                cross_transposes(1)
                cross_out(1)
                cross_transposes(2)
                transposes_of_xn(8, XT_BANK[0])
                cross_out(2)
                cross_transposes(3)
                ffn_rotate(0)
                transposes_of_xn(9, XT_BANK[1])
                cross_out(3)
                ffn_integers(0)
                ffn_rotate(1)
                ffn_gate_up(0)
                ffn_integers(1)
                transposes_of_xn(10, XT_BANK[2])
                ffn_gate_up(1)
                ffn_rotate(2)
                ffn_hidden_transposes(0)
                for t in range(NT):
                    ffn_hidden_rotate(t)
                    if t == 0:
                        ffn_integers(2)
                    if t + 3 < NT:
                        transposes_of_xn(8 + t + 3, XT_BANK[t + 3])
                    if t == 2:
                        transposes_of_xn(0, 0, 1)
                        transposes_of_xn(1, 1, 1)
                    if t + 1 < NT:
                        ffn_hidden_transposes(t + 1)
                    if t + 3 < NT:
                        ffn_rotate(t + 3)
                    if t == 2:
                        transposes_of_xn(2, 2, 1)
                        transposes_of_xn(3, 3, 1)
                    if t + 2 < NT:
                        ffn_gate_up(t + 2)
                    if t == 3:
                        project(0, 1)
                        project(1, 1)
                    ffn_down(t)
                    if t + 3 < NT:
                        ffn_integers(t + 3)

        @block.scalar
        def _(act):
            for n, (s, k) in enumerate(PJOBS):
                if s != "act":
                    continue
                act.wait_ge(p_ps, n + 1)
                if n == 3 + H:
                    act.wait_ge(kd_made, 4)
                if n == 0:
                    act.copy(kvT[:, :], ps[:, 0, :]).then_inc(p_act, 1)
                elif 3 <= n < 3 + H:
                    act.copy(mt[:, n - 3, :], ps[:, n % PBANKS, 0:QC]).then_inc(p_act, 1)
                elif n < V0:
                    act.copy(nn[:, n - 3 - H, :], ps[:, n % PBANKS, :]).then_inc(p_act, 1)
                elif n < A0:
                    m = n - V0
                    if m >= 4:
                        act.wait_ge(p_vstore[m % 4], 16 * (m // 4))
                    act.copy(vst[:, m % 4, :], ps[:, n % PBANKS, :]).then_inc(p_act, 1)
                else:
                    h = (n - A0) // 2
                    rows_, a = (QC1, ast1) if (n - A0) % 2 else (P, ast0)
                    act.copy(a[:, :, h, :], ps[0:rows_, n % PBANKS, :].rearrange("p (b k) -> p b k", b=B)
                             ).then_inc(p_act, 1)
            act.wait_ge(in_ctx, 96)
            act.copy(ident_b[:, :], ident_f[:, :]).then_inc(p_const, 1)
            i = 0
            def evacuate_xt(n, b, out, ahead=0):
                act.wait_ge(sems["xt_ps"], at("xt_ps", i, 12 * ahead + n + 1))
                act.copy(out, ps[:, b, :].rearrange("p (c q) -> p c q", c=KC)).then_inc(sems["xt"], 1)

            def high_parts(j, ahead=0):
                if j < 2:
                    act.wait_ge(sems["rope_cv"], at("rope_cv", i, 4 * ahead + 2 * j + 2))
                else:
                    act.wait_ge(sems["rope_c"], at("rope_c", i, 2))
                if j:
                    act.wait_ge(sems["stack"], at("stack", i, 16 * NCOPY * (3 * ahead + j)))
                for odd in range(2):
                    act.copy(parts[:, odd, :], rot[:, 2 * odd, :]).then_inc(sems["rope_h"], 1)

            for t in range(NT):
                evacuate_xt(t, t % 2, xT[:, :, t * P:(t + 1) * P])
            act.wait_ge(ffn_done, 1)
            act.wait_ge(in_had, 16)
            act.copy(had_sb[:, :, :], had_in[:, :, :]).then_inc(had_ready, 1)
            high_parts(0)
            high_parts(1)

            with act.Fori(0, B) as i:
                def values(t):
                    act.wait_ge(sems["v_ps"], at("v_ps", i, t + 1))
                    act.copy(vw[:, t, 0:G * P].rearrange("p (g c) -> p g c", c=P)[:, :, 32:64],
                             ps[:, 6 + t % 2, 0:G * HD].rearrange("p (g c) -> p g c", c=HD)).then_inc(sems["vw"], 1)

                def maxima(hg):
                    act.wait_ge(sems["nmt_ps"], at("nmt_ps", i, hg + 1))
                    if hg:
                        act.wait_ge(sems["rows_in"], at("rows_in", i, 32))
                    act.copy(rows[:, :], ps[0:H, 0, :]).then_inc(sems["nmt"], 1)

                def exponentials(j):
                    act.wait_ge(sems["st_ps"], at("st_ps", i, j + 1))
                    if j >= 4:
                        act.wait_ge(sems["pv"], at("pv", i, (j - 4) // 2 + 1))
                    b0 = 2 + 2 * (j % 2)
                    act.activation(pt[:, j % 4, :], ps[:, b0:b0 + 2, :].rearrange("p b q -> p (b q)"), ACT.Exp,
                                   scale=SELF_SCALE).then_inc(sems["probs"], 1)

                high_parts(2)
                values(0)
                values(1)
                maxima(0)
                values(2)
                values(3)
                for j in range(2 * H):
                    if j == 14:
                        maxima(1)
                    exponentials(j)
                for half in range(2):
                    for t in (2 * half, 2 * half + 1):
                        evacuate_xt(4 + t, 4 + t % 2, xT[:, :, t * P:(t + 1) * P])
                    for m, q in enumerate((qc0, qc1)):
                        act.wait_ge(sems["dq_ps"], at("dq_ps", i, 2 * half + m + 1))
                        act.copy(q[:, 256 * half:256 * half + 256], ps[0:q.shape[0], 6 + m, 0:256]).then_inc(sems["qc"], 1)

                def cross_exp(t):
                    act.wait_ge(sems["centred"], at("centred", i, t + 1))
                    e = ex[:, t % 2, :, :].rearrange("p h k -> p (h k)")
                    act.activation(e, e, ACT.Exp, scale=X_SCALE).then_inc(sems["xexp"], 1)

                def cross_evacuate(t):
                    for hb in range(2):
                        act.wait_ge(sems["pt_ps"], at("pt_ps", i, 2 * t + hb + 1))
                        if t:
                            act.wait_ge(sems["xo_ps"], at("xo_ps", i, t))
                        act.copy(ptx[:, 4 * hb:4 * hb + 4, :].rearrange("p c q -> p (c q)"), ps[:, hb, :]
                                 ).then_inc(sems["ptx"], 1)

                def ffn_xt(t):
                    if t:
                        act.wait_ge(sems["had_ps"], at("had_ps", i, t))
                    evacuate_xt(8 + t, XT_BANK[t], xT3[:, :, :])

                def ffn_round(t):
                    act.wait_ge(sems["fsc"], at("fsc", i, t + 1))
                    if t:
                        act.wait_ge(sems["fint"], at("fint", i, t))
                    act.activation(fv[:, :], ps[:, ROT_BANK[t], :], ACT.Copy, bias=MAGIC, scale=fs[:, t, 2:3]
                                   ).then_inc(sems["fround"], 1)

                def ffn_intT(t):
                    act.wait_ge(sems["fintT_ps"], at("fintT_ps", i, t + 1))
                    if t:
                        act.wait_ge(sems["up_ps"], at("up_ps", i, FG * t))
                    act.copy(fqT[:, :, :].rearrange("p c q -> p (c q)"), ps[:, INT_BANK[t], :].bitcast(BF16)[:, 0:512]
                             ).then_inc(sems["fintT"], 1)

                def ffn_tanh(t, groups):
                    for g in groups:
                        n = FG * t + g
                        act.wait_ge(sems["gate_ps"], at("gate_ps", i, n + 1))
                        if n > 1:
                            act.wait_ge(sems["gated"], at("gated", i, n - 1))
                        act.activation(th[:, n % 2, :], ps[:, GU_BANK[t][g], :], ACT.Tanh, scale=fs[:, t, 3:4]
                                       ).then_inc(sems["th"], 1)

                def ffn_hidT(t):
                    if t:
                        act.wait_ge(sems["had2_ps"], at("had2_ps", i, FG * t))
                    for g in range(FG):
                        act.wait_ge(sems["hidT_ps"], at("hidT_ps", i, FG * t + g + 1))
                        act.copy(hidT[:, 4 * g:4 * g + 4, :].rearrange("p c q -> p (c q)"), ps[:, HT_BANK[t][g], :]
                                 ).then_inc(sems["hidT"], 1)

                def ffn_round2(t):
                    act.wait_ge(sems["f2sc"], at("f2sc", i, t + 1))
                    for half in range(2):
                        b0 = 4 + 2 * half
                        v = ps[:, b0:b0 + 2, :].rearrange("p b q -> p (b q)")
                        act.activation(v, v, ACT.Copy, bias=MAGIC, scale=f2s[:, t, 2:3]).then_inc(sems["f2round"], 1)

                def ffn_int2T(t):
                    for half in range(2):
                        act.wait_ge(sems["f2intT_ps"], at("f2intT_ps", i, 2 * t + half + 1))
                        if t:
                            act.wait_ge(sems["down_ps"], at("down_ps", i, t))
                        act.copy(f2qT[:, 8 * half:8 * half + 8, :].rearrange("p c q -> p (c q)"),
                                 ps[:, DOWN_BANK[t] + half, :].bitcast(BF16)).then_inc(sems["f2intT"], 1)

                cross_exp(0)
                cross_exp(1)
                cross_evacuate(0)
                cross_exp(2)
                cross_evacuate(1)
                cross_exp(3)
                cross_evacuate(2)
                ffn_xt(0)
                cross_evacuate(3)
                ffn_round(0)
                ffn_xt(1)
                ffn_intT(0)
                ffn_round(1)
                ffn_tanh(0, range(FG))
                ffn_intT(1)
                ffn_xt(2)
                ffn_tanh(1, range(FG))
                ffn_hidT(0)
                ffn_round(2)
                for t in range(NT):
                    if t == 0:
                        ffn_intT(2)
                    if t + 3 < NT:
                        ffn_xt(t + 3)
                    if t == 2:
                        evacuate_xt(0, 0, xT[:, :, 0:P], 1)
                        evacuate_xt(1, 1, xT[:, :, P:2 * P], 1)
                    if t + 1 < NT:
                        ffn_hidT(t + 1)
                    if t == 2:
                        ffn_round2(t)
                        evacuate_xt(2, 2, xT[:, :, 2 * P:3 * P], 1)
                        evacuate_xt(3, 3, xT[:, :, 3 * P:4 * P], 1)
                    else:
                        ffn_round2(t)
                    if t + 2 < NT:
                        ffn_tanh(t + 2, range(0, 2))
                    if t + 3 < NT:
                        ffn_round(t + 3)
                    if t + 2 < NT:
                        ffn_tanh(t + 2, range(2, FG))
                    if t == 3:
                        high_parts(0, 1)
                    ffn_int2T(t)
                    if t + 3 < NT:
                        ffn_intT(t + 3)
                high_parts(1, 1)

        @block.vector
        def _(dve):
            dve.wait_ge(in_ctx, 96)
            for n in (1, 2):
                dve.wait_ge(p_ps, n + 1)
                b3 = ps[:, n, :].rearrange("p (b k) -> p b k", b=B)
                for v in range(2):
                    tab = krope_sb[:, 2 * v + n - 1:2 * v + n, :].broadcast_to([P, B, LK])
                    last = dve.tensor_tensor(ktmp[:, 2 * v + n - 1, :].rearrange("p (b k) -> p b k", b=B), b3, tab,
                                             ALU.mult)
                last.then_inc(p_dve, 1)
            dve.wait_ge(p_dve, 2)
            dve.wait_ge(p_kzero, 1)
            for v in range(2):
                for u in range(2):
                    q = slice(64 * u, 64 * u + 64)
                    dve.tensor_tensor(kd_all[q, :, v, q], ktmp[q, 2 * v, :].rearrange("p (b k) -> p b k", b=B),
                                      ktmp[q, 2 * v + 1, :].rearrange("p (b k) -> p b k", b=B), ALU.add
                                      ).then_inc(kd_made, 1)
            for n, w in enumerate((gate_w, up_w, down_w)):
                dve.wait_ge(in_ffn[n], 64)
                dve.tensor_reduce(wsum[:, n:n + 1], wst[n][:, :], AX.X, ALU.add, apply_absolute_value=True
                                  ).then_inc(ffn_step, 1)
                dve.wait_ge(p_ffn_ps, n + 1)
                dve.tensor_scalar(wsc[:, n:n + 1], ps[:, PBANKS, n:n + 1], 1.0 / (F * D), EPS, ALU.mult, ALU.max
                                  ).then_inc(ffn_step, 1)
                dve.wait_ge(ffn_step, 6 * n + 2)
                dve.tensor_scalar(wthr[:, n:n + 1], wsc[:, n:n + 1], 0.5, None, ALU.mult).then_inc(ffn_step, 1)
                dve.tensor_scalar(wthr[:, 3 + n:4 + n], wsc[:, n:n + 1], -0.5, None, ALU.mult).then_inc(ffn_step, 1)
                dve.wait_ge(ffn_step, 6 * n + 4)
                dve.tensor_scalar(wlow[:, :], wst[n][:, :], wthr[:, 3 + n:4 + n], None, ALU.is_lt, saturate=False
                                  ).then_inc(ffn_step, 1)
                dve.wait_ge(ffn_step, 6 * n + 5)
                dve.scalar_tensor_tensor(w[:, :, :].rearrange("p c n -> p (c n)"), wst[n][:, :], wthr[:, n:n + 1],
                                         wlow[:, :], ALU.is_gt, ALU.subtract, saturate=False).then_inc(ffn_step, 1)
            dve.wait_ge(ffn_step, 18)
            dve.sem_inc(ffn_done, 1)

            i = 0
            steps = [0]

            def step(ins):
                steps[0] += 1
                ins.then_inc(sems["dve_step"], 1)

            def settle():
                dve.wait_ge(sems["dve_step"], at("dve_step", i, steps[0]))

            def ln_stats(n, src):
                step(dve.bn_stats(stats[:, n, :], src))
                settle()
                apart(dve)
                dve.bn_aggr(mv[:, n, :], stats[:, n, :]).then_inc(sems["mv"], 1)

            def ln_normalise(n, src, ahead=0):
                dve.wait_ge(sems["rstd"], at("rstd", i, 12 * ahead + n + 1))
                dve.wait_ge(sems["xt_ps"], at("xt_ps", i, 12 * ahead + n - 1))
                dve.tensor_scalar(xn[:, n % 2, :], src, mv[:, n, 0:1], rstd[:, n:n + 1], ALU.subtract, ALU.mult
                                  ).then_inc(sems["xn"], 1)

            def rotate(j, ahead=0):
                if j:
                    dve.wait_ge(sems["rope_l"], at("rope_l", i, 6 * ahead + 2 * j))
                for v in (0, 2, 1, 3):
                    dve.wait_ge(sems["proj"], at("proj", i, 6 * ahead + 2 * j + v % 2 + 1))
                    dve.tensor_tensor(rot[:, v, :], ps[:, 2 + 2 * j + v % 2, :], rope_sb[:, (v + v // 2) % 2, :],
                                      ALU.mult).then_inc(sems["rope_m"], 1)

            def low_parts(j, ahead=0):
                for odd in range(2):
                    dve.wait_ge(sems["rope_h"], at("rope_h", i, 6 * ahead + 2 * j + odd + 1))
                    dve.tensor_tensor(parts[:, 2 + odd, :], rot[:, 2 * odd, :], parts[:, odd, :].bitcast(F32),
                                      ALU.subtract).then_inc(sems["rope_l"], 1)

            def combine(j, ahead=0):
                dve.wait_ge(sems["rope_m"], at("rope_m", i, 12 * ahead + 4 * j + 4))
                dve.tensor_tensor(rot[:, 0, :], rot[:, 0, :], rot[:, 1, :], ALU.subtract).then_inc(sems["rope_cv"], 1)
                dve.tensor_tensor(rot[:, 2, :], rot[:, 2, :], rot[:, 3, :], ALU.add).then_inc(sems["rope_cv"], 1)

            def first_stats(ahead=0):
                dve.wait_ge(sems["x_in"], at("x_in", i, 16 * ahead + 16))
                for t in range(NT):
                    ln_stats(t, xin[:, t, :])

            first_stats()
            dve.wait_ge(p_ps, NJOBS)
            for t in range(NT):
                ln_normalise(t, xin[:, t, :])
            dve.wait_ge(in_rope, 16)
            for j in range(2):
                rotate(j)
                combine(j)
                low_parts(j)
            steps_before = steps[0]

            with dve.Fori(0, B) as i:
                steps[0] = steps_before
                def maximum(n):
                    h, t, b0 = MAX_JOBS[n]
                    dve.wait_ge(sems["smax_ps"], at("smax_ps", i, n + 1))
                    dve.tensor_reduce(negmax[:, t, h:h + 2], ps[:, b0:b0 + 2, :], AX.X, ALU.max, negate=True
                                      ).then_inc(sems["smax"], 1)

                def split_maxima(hg):
                    dve.wait_ge(sems["smax"], at("smax", i, 16 * (hg + 1)))
                    m = negmax[:, :, 8 * hg:8 * hg + 8]
                    step(dve.tensor_copy(negsplit[:, hg, :, 0:8], m))
                    settle()
                    dve.tensor_tensor(negsplit[:, hg, :, 8:16], m, negsplit[:, hg, :, 0:8].bitcast(F32), ALU.subtract
                                      ).then_inc(sems["nms"], 1)

                def denominators_of_heads(p, half):
                    if half == 0:
                        dve.wait_ge(sems["pv"], at("pv", i, 2 * p + 2))
                        if p:
                            dve.wait_ge(sems["at"], at("at", i, p))
                    q = slice(256 * half, 256 * half + 256)
                    step(dve.reciprocal(rcp[:, q], ps[64:128, 6 + p % 2, q]))

                def normalise_heads(p):
                    b = 6 + p % 2
                    settle()
                    r0 = 64 * (p % 2)
                    dve.tensor_tensor(aT[r0:r0 + 64, p // 2, :], ps[0:64, b, :], rcp[:, :], ALU.mult
                                      ).then_inc(sems["at"], 1)

                for n in range(16):
                    if n == 0:
                        rotate(2)
                    elif n == 8:
                        low_parts(2)
                    maximum(n)
                split_maxima(0)
                for n in range(16, 20):
                    maximum(n)
                for j in range(2 * H):
                    for n in MAX_AT.get(j, ()):
                        maximum(n)
                    if j == 11:
                        split_maxima(1)
                    if j % 4 == 0 and j:
                        denominators_of_heads(j // 4 - 1, 1)
                        normalise_heads(j // 4 - 1)
                    elif j % 4 == 3:
                        denominators_of_heads(j // 4, 0)
                denominators_of_heads(HP - 1, 1)
                normalise_heads(HP - 1)
                for t in range(NT):
                    dve.wait_ge(sems["wo_ps"], at("wo_ps", i, t + 1))
                    if t < 2:
                        dve.wait_ge(sems[f"store{t}"], at(f"store{t}", i, 0))
                    dve.tensor_tensor(xcur[:, t, :], ps[:, t, :], xin[:, t, :], ALU.add).then_inc(sems["x1"], 1)
                    dve.wait_ge(sems["x1"], at("x1", i, t + 1))
                    ln_stats(4 + t, xcur[:, t, :])
                    if t:
                        ln_normalise(4 + t - 1, xcur[:, t - 1, :])
                ln_normalise(7, xcur[:, 3, :])

                def rotate_queries(half):
                    if half:
                        dve.wait_ge(sems["sc_ps"], at("sc_ps", i, 2))
                    for p in range(HP):
                        m = HP * half + p
                        dve.wait_ge(sems["xr_ps"], at("xr_ps", i, m + 1))
                        q = slice(256 * half, 256 * half + 256)
                        dve.tensor_tensor(xc[:, p, :], ps[:, m % 4, 0:256], rope_sb[:, 2, q], ALU.mult)
                        dve.tensor_tensor(xs[:, p, :], ps[:, m % 4, 0:256], rope_sb[:, 3, q], ALU.mult
                                          ).then_inc(sems["xcs"], 1)

                def mask_and_centre(t):
                    dve.wait_ge(sems["sc_ps"], at("sc_ps", i, t + 1))
                    if t == 0:
                        dve.wait_ge(sems["maskt"], at("maskt", i, 1))
                    if t >= 2:
                        dve.wait_ge(sems["pt_ps"], at("pt_ps", i, 2 * (t - 1)))
                    b0 = 4 + 2 * (t % 2)
                    e = ex[:, t % 2, :, :]
                    dve.tensor_tensor(e, ps[:, b0:b0 + 2, :].rearrange("p b (h k) -> p (b h) k", k=LK),
                                      maskt[:, t:t + 1, :].broadcast_to([P, H, LK]), ALU.add).then_inc(sems["masked"], 1)
                    dve.wait_ge(sems["masked"], at("masked", i, t + 1))
                    step(dve.tensor_reduce(xmax[:, t, :], e, AX.X, ALU.max))
                    settle()
                    dve.tensor_tensor(e, e, xmax[:, t, :].unsqueeze(2).broadcast_to([P, H, LK]), ALU.subtract
                                      ).then_inc(sems["centred"], 1)

                def denominators(t):
                    dve.wait_ge(sems["xexp"], at("xexp", i, t + 1))
                    step(dve.tensor_reduce(xsum[:, t, :], ex[:, t % 2, :, :], AX.X, ALU.add))
                    settle()
                    dve.reciprocal(xrec[:, t, :], xsum[:, t, :]).then_inc(sems["xden"], 1)

                def residual2(t):
                    dve.wait_ge(sems["xo_ps"], at("xo_ps", i, t + 1))
                    dve.tensor_tensor(xcur[:, t, :], ps[:, 2 + t % 2, :], xcur[:, t, :], ALU.add).then_inc(sems["x2"], 1)

                def ffn_stats(t):
                    dve.wait_ge(sems["x2"], at("x2", i, t + 1))
                    ln_stats(8 + t, xcur[:, t, :])

                def ffn_ln(t):
                    ln_normalise(8 + t, xcur[:, t, :])

                def scales(s, t, src, c, weights):
                    if src is not None:
                        step(dve.tensor_reduce(s[:, t, 0:1], src, AX.X, ALU.max, apply_absolute_value=True))
                        settle()
                    step(dve.tensor_scalar(s[:, t, 1:2], s[:, t, 0:1], c, EPS, ALU.mult, ALU.max))
                    settle()
                    step(dve.reciprocal(s[:, t, 4:5], s[:, t, 1:2]))
                    for k, w in enumerate(weights):
                        step(dve.tensor_scalar(s[:, t, 5 + k:6 + k], s[:, t, 1:2], wsc[:, w:w + 1],
                                               (0.5 if w == 0 else 1.0) / 127.0, ALU.mult, ALU.mult))
                    settle()
                    if len(weights) == 2:
                        step(dve.tensor_copy(s[:, t, 3:4], s[:, t, 5:6]))
                        step(dve.tensor_tensor(s[:, t, 7:8], s[:, t, 5:6], s[:, t, 6:7], ALU.mult))
                    return dve.tensor_scalar(s[:, t, 2:3], s[:, t, 4:5], 127.0 * c, None, ALU.mult)

                def ffn_scales(t):
                    dve.wait_ge(sems["had_ps"], at("had_ps", i, t + 1))
                    scales(fs, t, ps[:, ROT_BANK[t], :], C512, (0, 1)).then_inc(sems["fsc"], 1)

                def ffn_int(t):
                    dve.wait_ge(sems["fround"], at("fround", i, t + 1))
                    if t:
                        dve.wait_ge(sems["fintT_ps"], at("fintT_ps", i, t))
                    dve.tensor_scalar(fq[:, :], fv[:, :], MAGIC, None, ALU.subtract).then_inc(sems["fint"], 1)

                def ffn_xt_low(t):
                    dve.wait_ge(sems["xt"], at("xt", i, 8 + t + 1))
                    dve.tensor_tensor(xT3_lo[:, :, :].rearrange("p c q -> p (c q)"), ps[:, XT_BANK[t], :],
                                      xT3[:, :, :].bitcast(F32).rearrange("p c q -> p (c q)"), ALU.subtract
                                      ).then_inc(sems["xt_lo"], 1)

                def ffn_hidT_low(t):
                    for g in range(FG):
                        dve.wait_ge(sems["hidT"], at("hidT", i, FG * t + g + 1))
                        hi = hidT[:, 4 * g:4 * g + 4, :].bitcast(F32).rearrange("p c q -> p (c q)")
                        dve.tensor_tensor(hidT_lo[:, 4 * g:4 * g + 4, :].rearrange("p c q -> p (c q)"),
                                          ps[:, HT_BANK[t][g], :], hi, ALU.subtract).then_inc(sems["hidT_lo"], 1)

                def ffn_hidden(t):
                    if t > 1:
                        dve.wait_ge(sems["hidT_ps"], at("hidT_ps", i, FG * (t - 1)))
                    elif t == 1:
                        dve.wait_ge(sems["sc_ps"], at("sc_ps", i, NT))

                    def second(g):
                        dve.wait_ge(sems["gated"], at("gated", i, FG * t + g + 1))
                        dve.wait_ge(sems["up_ps"], at("up_ps", i, FG * t + g + 1))
                        dve.scalar_tensor_tensor(hid[t % 2][:, g, :], gw[:, g % 2, :], fs[:, t, 7:8],
                                                 ps[:, GU_BANK[t][g] + 1, :], ALU.mult, ALU.mult).then_inc(sems["hid"], 1)

                    for g in range(FG):
                        n = FG * t + g
                        dve.wait_ge(sems["th"], at("th", i, n + 1))
                        dve.wait_ge(sems["hid"], at("hid", i, n - 1))
                        dve.scalar_tensor_tensor(gw[:, g % 2, :], th[:, n % 2, :], 1.0, ps[:, GU_BANK[t][g], :],
                                                 ALU.add, ALU.mult).then_inc(sems["gated"], 1)
                        if g:
                            second(g - 1)
                    second(FG - 1)

                def ffn_sum1(t):
                    dve.wait_ge(sems["hid"], at("hid", i, FG * t + FG))
                    if t:
                        dve.wait_ge(sems["diff2"], at("diff2", i, t))
                    a = hid[t % 2][:, :, :].rearrange("p (r u) n -> p r u n", u=2)
                    dve.tensor_tensor(sd[:, 0, :, :], a[:, :, 0, :], a[:, :, 1, :], ALU.add).then_inc(sems["sum1"], 1)

                def ffn_sum2(t):
                    dve.wait_ge(sems["sum1"], at("sum1", i, t + 1))
                    dve.wait_ge(sems["diff1"], at("diff1", i, t + 1))
                    dve.tensor_tensor(hid[t % 2][:, 0:2, :], sd[:, :, 0, :], sd[:, :, 1, :], ALU.add).then_inc(sems["sum2"], 1)

                def ffn_scales2(t):
                    for g in range(FG):
                        dve.wait_ge(sems["had2_ps"], at("had2_ps", i, FG * t + g + 1))
                        step(dve.tensor_reduce(gmax[:, t, g:g + 1], ps[:, 4 + g, :], AX.X, ALU.max,
                                               apply_absolute_value=True))
                    settle()
                    step(dve.tensor_reduce(f2s[:, t, 0:1], gmax[:, t, :], AX.X, ALU.max))
                    settle()
                    scales(f2s, t, None, C2048, (2,)).then_inc(sems["f2sc"], 1)

                def ffn_int2(t):
                    for half in range(2):
                        dve.wait_ge(sems["f2round"], at("f2round", i, 2 * t + half + 1))
                        if t and half == 0:
                            dve.wait_ge(sems["f2intT_ps"], at("f2intT_ps", i, 2 * t))
                        cols = slice(1024 * half, 1024 * half + 1024)
                        b0 = 4 + 2 * half
                        dve.tensor_scalar(f2q[:, cols], ps[:, b0:b0 + 2, :].rearrange("p b q -> p (b q)"), MAGIC, None,
                                          ALU.subtract).then_inc(sems["f2int"], 1)

                def ffn_out(t):
                    dve.wait_ge(sems["down_ps"], at("down_ps", i, t + 1))
                    dve.scalar_tensor_tensor(xcur[:, t, :], ps[:, DOWN_BANK[t], :], f2s[:, t, 5:6], xcur[:, t, :],
                                             ALU.mult, ALU.add).then_inc(sems["y"], 1)

                rotate_queries(0)
                mask_and_centre(0)
                rotate_queries(1)
                denominators(0)
                mask_and_centre(1)
                mask_and_centre(2)
                denominators(1)
                residual2(0)
                ffn_stats(0)
                denominators(2)
                ffn_ln(0)
                mask_and_centre(3)
                residual2(1)
                ffn_stats(1)
                denominators(3)
                ffn_xt_low(0)
                ffn_ln(1)
                residual2(2)
                ffn_scales(0)
                ffn_int(0)
                ffn_xt_low(1)
                residual2(3)
                ffn_stats(2)
                ffn_stats(3)
                ffn_scales(1)
                ffn_int(1)
                ffn_ln(2)
                ffn_hidden(0)
                ffn_xt_low(2)
                ffn_sum1(0)
                ffn_hidden(1)
                ffn_sum2(0)
                ffn_hidT_low(0)
                ffn_scales(2)
                ffn_int(2)
                ffn_sum1(1)
                for t in range(NT):
                    if t + 1 < NT:
                        ffn_sum2(t + 1)
                    if t + 3 < NT:
                        ffn_ln(t + 3)
                    ffn_scales2(t)
                    if t + 3 < NT:
                        ffn_xt_low(t + 3)
                    if t == 2:
                        ln_normalise(2, xin[:, 2, :], 1)
                        ln_normalise(3, xin[:, 3, :], 1)
                    if t + 1 < NT:
                        ffn_hidT_low(t + 1)
                    ffn_int2(t)
                    if t == 3:
                        for j in range(2):
                            rotate(j, 1)
                            combine(j, 1)
                            low_parts(j, 1)
                    if t + 3 < NT:
                        ffn_scales(t + 3)
                        ffn_int(t + 3)
                    if t + 2 < NT:
                        ffn_hidden(t + 2)
                        ffn_sum1(t + 2)
                    ffn_out(t)
                    if t == 0:
                        first_stats(1)
                    elif t == 1:
                        ln_normalise(0, xin[:, 0, :], 1)
                        ln_normalise(1, xin[:, 1, :], 1)
                assert steps[0] - steps_before == PER["dve_step"], steps

        @block.gpsimd
        def _(pool):
            pool.memset(mhalf[:, :], -0.5).then_inc(sems["pool_step"], 1)
            pool.memset(ones[:, :], 1.0).then_inc(p_const, 1)
            pool.memset(kd_all[:, :, :, :], 0.0).then_inc(p_kzero, 1)
            i = 0
            steps = [1]

            def step(ins):
                steps[0] += 1
                ins.then_inc(sems["pool_step"], 1)

            def settle():
                pool.wait_ge(sems["pool_step"], at("pool_step", i, steps[0]))
                apart(pool)

            def rsqrt(n, ahead=0):
                pool.wait_ge(sems["mv"], at("mv", i, 12 * ahead + n + 1))
                apart(pool)
                step(pool.tensor_scalar(vare[:, n:n + 1], mv[:, n, 1:2], EPS, None, ALU.add))
                settle()
                pool.tensor_tensor(rstd[:, n:n + 1], vare[:, n:n + 1], mhalf[:, :], ALU.pow).then_inc(sems["rstd"], 1)

            for t in range(NT):
                rsqrt(t)
            pool.wait_ge(arena_free, 1)
            pool.memset(vw[:, :, :], 0.0).then_inc(vw_zero, 1)
            pool.wait_ge(vw_zero, 1)
            pool.memset(vw[:, :, 0:G * P].rearrange("p t (g c) -> p t g c", c=P)[:, :, :, 96:128], 1.0).then_inc(vw_const, 1)
            steps_before = steps[0]

            with pool.Fori(0, B) as i:
                steps[0] = steps_before
                pool.wait_ge(sems["rope_m"], at("rope_m", i, 12))
                apart(pool)
                pool.tensor_tensor(rot[:, 0, :], rot[:, 0, :], rot[:, 1, :], ALU.subtract).then_inc(sems["rope_c"], 1)
                pool.tensor_tensor(rot[:, 2, :], rot[:, 2, :], rot[:, 3, :], ALU.add).then_inc(sems["rope_c"], 1)

                pool.wait_ge(sems["hidT_ps"], at("hidT_ps", i, 0))
                pool.wait_ge(sems["rope_c"], at("rope_c", i, 2))
                apart(pool)
                pool.memset(ks[96:98, :, :].bitcast(F32), 1.0).then_inc(sems["ks_ones"], 1)
                pool.wait_ge(sems["ks_ones"], at("ks_ones", i, 1))
                apart(pool)
                pool.wait_ge(sems["seg_in"], at("seg_in", i, 16))
                pool.wait_ge(sems["masked"], at("masked", i, 0))
                apart(pool)
                step(pool.tensor_copy(seg_f[:, :], seg_i[:, :]))
                settle()
                step(pool.tensor_scalar(seg_8[:, :], seg_f[:, :], -8.0, None, ALU.add))
                settle()
                for t in range(NT):
                    pool.tensor_scalar(maskt[:, t, :], iota_sb[:, :], seg_f[:, t:t + 1], NEG, ALU.is_gt, ALU.mult)
                    step(pool.tensor_scalar(mask_lo[:, :], iota_sb[:, :], seg_8[:, t:t + 1], NEG, ALU.is_lt, ALU.mult))
                    settle()
                    last = pool.tensor_tensor(maskt[:, t, :], maskt[:, t, :], mask_lo[:, :], ALU.add)
                    if t < NT - 1:
                        step(last)
                        settle()
                last.then_inc(sems["maskt"], 1)
                for t in range(NT):
                    rsqrt(4 + t)

                def normalise(t):
                    pool.wait_ge(sems["xden"], at("xden", i, t + 1))
                    apart(pool)
                    e = ex[:, t % 2, :, :]
                    pool.tensor_tensor(e, e, xrec[:, t, :].unsqueeze(2).broadcast_to([P, H, LK]), ALU.mult
                                       ).then_inc(sems["xprob"], 1)

                for t in range(3):
                    normalise(t)
                rsqrt(8)
                normalise(3)
                for t in range(1, NT):
                    rsqrt(8 + t)

                def differences(t):
                    pool.wait_ge(sems["hid"], at("hid", i, FG * t + FG))
                    if t:
                        pool.wait_ge(sems["sum2"], at("sum2", i, t))
                    pool.wait_ge(sems["diff2"], at("diff2", i, t))
                    apart(pool)
                    a = hid[t % 2][:, :, :].rearrange("p (r u) n -> p r u n", u=2)
                    pool.tensor_tensor(sd[:, 1, :, :], a[:, :, 0, :], a[:, :, 1, :], ALU.subtract).then_inc(sems["diff1"], 1)
                    pool.wait_ge(sems["sum1"], at("sum1", i, t + 1))
                    pool.wait_ge(sems["diff1"], at("diff1", i, t + 1))
                    apart(pool)
                    pool.tensor_tensor(hid[t % 2][:, 2:4, :], sd[:, :, 0, :], sd[:, :, 1, :], ALU.subtract).then_inc(sems["diff2"], 1)

                for t in range(NT):
                    differences(t)
                    if t == 2:
                        for n in range(NT):
                            rsqrt(n, 1)
                assert steps[0] - steps_before == PER["pool_step"], steps


MAX_AT = {j: (20 + j,) for j in range(12)}
MAX_JOBS = [(8 * (n // 16) + 2 * (n % 4), (n % 16) // 4, 2 * (n % 3) if n < 16 else 2 + 2 * (n % 2) if n < 20 else 0) for n in range(32)]
XT_BANK = [4, 6, 2, 0]
ROT_BANK = [5, 7, 1, 1]
INT_BANK = [4, 0, 0, 0]
GU_BANK = [[0, 2, 4, 6], [4, 0, 6, 2], [2, 4, 6, 0], [2, 0, 4, 6]]
HT_BANK = [[4, 5, 6, 7], [2, 3, 2, 3], [2, 3, 0, 1], [2, 3, 0, 1]]
DOWN_BANK = [2, 0, 0, 0]
V0 = 3 + 2 * H
A0 = V0 + 4 * H
NJOBS = A0 + 2 * H


PBANKS = 7
PJOBS = [("dve", n) if n in (1, 2) else ("act", n + 1 if n < 1 else n - 1) for n in range(NJOBS)]
NACT = PJOBS[NJOBS - 1][1]
NN_ACT = PJOBS[V0 - 1][1]
PV_ACT = [PJOBS[V0 + m][1] for m in range(4 * H)]
A_ACT = [PJOBS[A0 + 8 * g + 7][1] for g in range(4)]


def _tables(np):
    f = np.float32
    had = np.array([[1.0]], f)
    while had.shape[0] < D:
        had = np.block([[had, had], [had, -had]]).astype(f)
    inv = (f(1.0) / np.power(f(10000.0), np.arange(0, HD, 2, dtype=f) / f(HD))).astype(f)
    ang = (np.arange(S, dtype=f)[:, None] * inv[None, :]).T.astype(f)
    selfrope = np.stack([np.cos(ang), np.sin(ang)]).repeat(8, axis=1)
    inv2 = (f(1.0) / np.power(f(10000.0), np.arange(R // 2, dtype=f) / f(R // 2))).astype(f)
    ang2 = (np.arange(S, dtype=f)[:, None] * inv2[None, :]).T.astype(f)
    xrope = np.tile(np.stack([np.cos(ang2), np.sin(ang2)]), (1, 4, 1))
    rope = np.concatenate([selfrope, xrope]).transpose(1, 0, 2).astype(f)
    c, s = np.cos(ang2[:, :LK]), np.sin(ang2[:, :LK])
    krope = np.stack([np.concatenate([c, c]), np.concatenate([-s, s]), np.concatenate([s, s]),
                      np.concatenate([c, -c])])
    krope = np.tile(krope, (1, 2, 1)).transpose(1, 0, 2).astype(f)
    iota = np.tile(np.arange(LK, dtype=f), (P, 1))
    return dict(had=had, rope=rope, krope=krope, iota=iota, ident=np.eye(P, dtype=f))


def kernel(x, ctx_2048, itok_BxS_0_1023, L0_attn_wq, L0_attn_wk, L0_attn_wv, L0_attn_wo, L0_xattn_W_kvc,
           L0_xattn_W_dq, L0_xattn_W_uq, L0_xattn_W_qr, L0_xattn_W_uk, L0_xattn_W_kr, L0_xattn_W_uv,
           L0_xattn_W_o, L0_ffn_w_gate, L0_ffn_w_up, L0_ffn_w_down):
    import numpy as np
    import concourse.bacc as bacc
    from concourse.bass_utils import run_bass_kernel_spmd as run

    a = np.asarray
    wkr = a(L0_xattn_W_kr)
    swapped = np.concatenate([wkr[:, R // 2:], wkr[:, :R // 2]], axis=1)
    data = dict(
        x=a(x),
        seg=a(itok_BxS_0_1023).reshape(B, NT, P).transpose(0, 2, 1),
        ctxT=a(ctx_2048).reshape(B * LK, D).T,
        wq=a(L0_attn_wq).reshape(D, 2, 8, HD // 2, 2).transpose(0, 1, 4, 3, 2).reshape(D, D),
        wk=a(L0_attn_wk).reshape(D, G, HD // 2, 2).transpose(0, 3, 2, 1).reshape(D, G * HD),
        wv=a(L0_attn_wv), wo=a(L0_attn_wo), wkvc=a(L0_xattn_W_kvc), wdq=a(L0_xattn_W_dq),
        wuqT=a(L0_xattn_W_uq).T, wqr=a(L0_xattn_W_qr), wukT=a(L0_xattn_W_uk).T,
        wkr2=np.concatenate([wkr, wkr], axis=1), wkrs2=np.concatenate([swapped, swapped], axis=1),
        wuvT=a(L0_xattn_W_uv).T, wox=a(L0_xattn_W_o),
        gateT=a(L0_ffn_w_gate).T, upT=a(L0_ffn_w_up).T, downT=a(L0_ffn_w_down).T,
        **_tables(np),
    )
    nc = bacc.Bacc("TRN2", target_bir_lowering=False, num_devices=1)
    arrays, args = {}, {}
    for name, v in data.items():
        v = np.ascontiguousarray(v)
        arrays[f"in_{name}"] = v
        args[name] = nc.dram_tensor(f"in_{name}", v.shape, mybir.dt.from_np(v.dtype), kind="ExternalInput").ap()
    out = nc.dram_tensor("out_0", (B, S, D), F32, kind="ExternalOutput").ap()
    block_kernel(nc, out=out, **args)
    r = run(nc, [arrays], core_ids=[0])
    return r.results[0]["out_0"]
```
